# Optimizing a Trainium2 kernel written in Bass

```python
import numpy as np
import jax
import jax.numpy as jnp

def _softmax(x, axis=-1):
    return jax.nn.softmax(x, axis=axis)

def _gelu(x):
    return jax.nn.gelu(x, approximate=True)

def _silu(x):
    return jax.nn.silu(x)

def _sigmoid(x):
    return jax.nn.sigmoid(x)

def _layernorm(x, axis=-1, eps=1e-05):
    m = jnp.mean(x, axis=axis, keepdims=True)
    v = jnp.var(x, axis=axis, keepdims=True)
    return (x - m) / jnp.sqrt(v + eps)

def _scatter_add(tgt, idx, src, axis=0):
    return tgt.at[idx].add(src)

def _segment_sum(src, seg, n):
    return jax.ops.segment_sum(src, seg, n)
kernel_name = 'mk_lm_tower_d2_tok_ids256_r4_1f007c'

def setup_inputs(seed: int=0):
    np.random.seed(seed)
    _w = jnp.asarray

    def _rec_inputs():
        import jax
        import jax.numpy as jnp
        _rk = jax.random.key(seed)
        x = jax.random.randint(jax.random.fold_in(_rk, 1), (32, 128), 0, 9219, jnp.int32)
        return x
    x = _rec_inputs()

    def _L0_tok_setup():
        import jax, jax.numpy as jnp
        import numpy as np
        N_NODES = 96
        N_SPECIAL = 3
        D_MODEL = 64
        B, L = (8, 512)
        key = jax.random.key(seed)
        k1, k2, k3 = jax.random.split(key, 3)
        vocab = N_SPECIAL + N_NODES * N_NODES
        tokens = jax.random.randint(k1, (B, L), 0, vocab, dtype=jnp.int64 if jax.config.jax_enable_x64 else jnp.int32)
        edge_emb = jax.random.normal(k2, (B, N_NODES, N_NODES, D_MODEL), dtype=jnp.float32)
        special_emb = jax.random.normal(k3, (N_SPECIAL, D_MODEL), dtype=jnp.float32)
        t = np.arange(vocab) - N_SPECIAL
        t = np.clip(t, 0, None)
        lut = np.stack([t // N_NODES, t % N_NODES], axis=-1).astype(np.int32)
        token_to_edge = jnp.asarray(lut)
        return {'tokens': tokens, 'edge_emb': edge_emb, 'special_emb': special_emb, 'token_to_edge': token_to_edge}
    _L0_tok_all = _L0_tok_setup()
    _L0_tok_in = {k: v for k, v in _L0_tok_all.items() if k in ('edge_emb', 'special_emb', 'token_to_edge')}
    del _L0_tok_all

    def _L0_attn_setup():
        import jax, jax.numpy as jnp
        import numpy as np
        key = jax.random.key(seed)
        k1, k2, k3 = jax.random.split(key, 3)
        d = 64
        x = jax.random.normal(k1, (8, 512, d), dtype=jnp.float32)
        Wq = jax.random.normal(k2, (d, d), dtype=jnp.float32) * d ** (-0.5)
        Wk = jax.random.normal(k3, (d, d), dtype=jnp.float32) * d ** (-0.5)
        return {'x': x, 'Wq': Wq, 'Wk': Wk}
    _L0_attn_all = _L0_attn_setup()
    _L0_attn_in = {k: v for k, v in _L0_attn_all.items() if k in ('Wq', 'Wk')}
    del _L0_attn_all

    def _L0_ffn_setup():
        import jax, jax.numpy as jnp
        import numpy as np
        B, S, H, F, E, K = (8, 1024, 64, 128, 16, 2)
        EPS = 1e-05
        key = jax.random.key(seed)
        ks = jax.random.split(key, 9)
        sc = 0.02
        return {'x': jax.random.normal(ks[0], (B, S, H), dtype=jnp.float32), 'gate_w': jax.random.normal(ks[1], (H, E), dtype=jnp.float32) * sc, 'gate_b': jnp.zeros((E,), dtype=jnp.float32), 'w1': jax.random.normal(ks[2], (E, H, F), dtype=jnp.float32) * sc, 'b1': jnp.zeros((E, F), dtype=jnp.float32), 'w2': jax.random.normal(ks[3], (E, F, H), dtype=jnp.float32) * sc, 'b2': jnp.zeros((E, H), dtype=jnp.float32), 'gamma': jnp.ones((H,), dtype=jnp.float32), 'beta': jnp.zeros((H,), dtype=jnp.float32)}
    _L0_ffn_all = _L0_ffn_setup()
    _L0_ffn_in = {k: v for k, v in _L0_ffn_all.items() if k in ('gate_w', 'gate_b', 'w1', 'b1', 'w2', 'b2', 'gamma', 'beta')}
    del _L0_ffn_all

    def _L1_attn_setup():
        import jax, jax.numpy as jnp
        import numpy as np
        B, T, C = (16, 512, 64)
        TT = T
        LAYER_ID, N_LAYER = (3, 6)
        key = jax.random.key(seed)
        ks = jax.random.split(key, 6)
        ratio_0_to_1 = LAYER_ID / (N_LAYER - 1)
        ratio_1_to_almost0 = 1.0 - LAYER_ID / N_LAYER
        h = np.arange(TT, dtype=np.float32)
        decay_speed = -5.0 + 8.0 * (h / (TT - 1)) ** (0.7 + 1.3 * ratio_0_to_1)
        curve = -(TT - 1 - h)
        time_w = jnp.asarray(np.exp(np.clip(curve * decay_speed, -30.0, 0.0)), dtype=jnp.float32)
        i = np.arange(C, dtype=np.float32) / C
        time_mix_k = jnp.asarray((i ** ratio_1_to_almost0).reshape(1, 1, C), dtype=jnp.float32)
        time_mix_v = jnp.asarray((i ** ratio_1_to_almost0 + 0.3 * ratio_0_to_1).reshape(1, 1, C), dtype=jnp.float32)
        time_mix_r = jnp.asarray((i ** (0.5 * ratio_1_to_almost0)).reshape(1, 1, C), dtype=jnp.float32)
        x = jax.random.normal(ks[0], (B, T, C), dtype=jnp.float32)
        scale = 0.02
        Wk = scale * jax.random.normal(ks[1], (C, C), dtype=jnp.float32)
        Wv = scale * jax.random.normal(ks[2], (C, C), dtype=jnp.float32)
        Wr = scale * jax.random.normal(ks[3], (C, C), dtype=jnp.float32)
        Wo = scale * jax.random.normal(ks[4], (C, C), dtype=jnp.float32)
        return {'x': x, 'time_w': time_w, 'time_mix_k': time_mix_k, 'time_mix_v': time_mix_v, 'time_mix_r': time_mix_r, 'Wk': Wk, 'Wv': Wv, 'Wr': Wr, 'Wo': Wo}
    _L1_attn_all = _L1_attn_setup()
    _L1_attn_in = {k: v for k, v in _L1_attn_all.items() if k in ('time_w', 'time_mix_k', 'time_mix_v', 'time_mix_r', 'Wk', 'Wv', 'Wr', 'Wo')}
    del _L1_attn_all

    def _L1_ffn_setup():
        import jax, jax.numpy as jnp
        import numpy as np
        B, T, C = (64, 96, 64)
        NH, NKV = (4, 2)
        HD = C // NH
        NREP = NH // NKV
        NE, TOPK = (8, 2)
        HID = int(8 / 3 * C)
        EPS_RMS = 1e-06

        def _rope_tables(t_len):
            inv_freq = 1.0 / 10000.0 ** (np.arange(0, HD, 2, dtype=np.float32) / HD)
            t = np.arange(t_len, dtype=np.float32)
            freqs = np.outer(t, inv_freq)
            emb = np.concatenate([freqs, freqs], axis=-1)
            return (jnp.asarray(np.cos(emb)), jnp.asarray(np.sin(emb)))

        def _rotate_half(x):
            h = x.shape[-1] // 2
            return jnp.concatenate([-x[..., h:], x[..., :h]], axis=-1)

        def _rmsnorm(v, w):
            return v * jax.lax.rsqrt(jnp.mean(v * v, axis=-1, keepdims=True) + EPS_RMS) * w
        key = jax.random.key(seed)
        ks = jax.random.split(key, 10)
        s = lambda k, shape: jax.random.normal(k, shape, jnp.float32) * 0.02
        return {'x': jax.random.normal(ks[0], (B, T, C), jnp.float32), 'ln1_w': jnp.ones((C,), jnp.float32), 'ln2_w': jnp.ones((C,), jnp.float32), 'wq': s(ks[1], (NH * HD, C)), 'wk': s(ks[2], (NKV * HD, C)), 'wv': s(ks[3], (NKV * HD, C)), 'wo': s(ks[4], (C, C)), 'router_w': s(ks[5], (NE, C)), 'w1': s(ks[6], (NE, HID, C)), 'w2': s(ks[7], (NE, C, HID)), 'w3': s(ks[8], (NE, HID, C))}
    _L1_ffn_all = _L1_ffn_setup()
    _L1_ffn_in = {k: v for k, v in _L1_ffn_all.items() if k in ('ln1_w', 'ln2_w', 'wq', 'wk', 'wv', 'wo', 'router_w', 'w1', 'w2', 'w3')}
    del _L1_ffn_all
    return {'x': x, 'L0_tok_edge_emb': _L0_tok_in['edge_emb'], 'L0_tok_special_emb': _L0_tok_in['special_emb'], 'L0_tok_token_to_edge': _L0_tok_in['token_to_edge'], 'L0_attn_Wq': _L0_attn_in['Wq'], 'L0_attn_Wk': _L0_attn_in['Wk'], 'L0_ffn_gate_w': _L0_ffn_in['gate_w'], 'L0_ffn_gate_b': _L0_ffn_in['gate_b'], 'L0_ffn_w1': _L0_ffn_in['w1'], 'L0_ffn_b1': _L0_ffn_in['b1'], 'L0_ffn_w2': _L0_ffn_in['w2'], 'L0_ffn_b2': _L0_ffn_in['b2'], 'L0_ffn_gamma': _L0_ffn_in['gamma'], 'L0_ffn_beta': _L0_ffn_in['beta'], 'L1_attn_time_w': _L1_attn_in['time_w'], 'L1_attn_time_mix_k': _L1_attn_in['time_mix_k'], 'L1_attn_time_mix_v': _L1_attn_in['time_mix_v'], 'L1_attn_time_mix_r': _L1_attn_in['time_mix_r'], 'L1_attn_Wk': _L1_attn_in['Wk'], 'L1_attn_Wv': _L1_attn_in['Wv'], 'L1_attn_Wr': _L1_attn_in['Wr'], 'L1_attn_Wo': _L1_attn_in['Wo'], 'L1_ffn_ln1_w': _L1_ffn_in['ln1_w'], 'L1_ffn_ln2_w': _L1_ffn_in['ln2_w'], 'L1_ffn_wq': _L1_ffn_in['wq'], 'L1_ffn_wk': _L1_ffn_in['wk'], 'L1_ffn_wv': _L1_ffn_in['wv'], 'L1_ffn_wo': _L1_ffn_in['wo'], 'L1_ffn_router_w': _L1_ffn_in['router_w'], 'L1_ffn_w1': _L1_ffn_in['w1'], 'L1_ffn_w2': _L1_ffn_in['w2'], 'L1_ffn_w3': _L1_ffn_in['w3']}

def reference(x, L0_tok_edge_emb, L0_tok_special_emb, L0_tok_token_to_edge, L0_attn_Wq, L0_attn_Wk, L0_ffn_gate_w, L0_ffn_gate_b, L0_ffn_w1, L0_ffn_b1, L0_ffn_w2, L0_ffn_b2, L0_ffn_gamma, L0_ffn_beta, L1_attn_time_w, L1_attn_time_mix_k, L1_attn_time_mix_v, L1_attn_time_mix_r, L1_attn_Wk, L1_attn_Wv, L1_attn_Wr, L1_attn_Wo, L1_ffn_ln1_w, L1_ffn_ln2_w, L1_ffn_wq, L1_ffn_wk, L1_ffn_wv, L1_ffn_wo, L1_ffn_router_w, L1_ffn_w1, L1_ffn_w2, L1_ffn_w3):
    import jax
    import jax.numpy as jnp

    def _L0_tok_ref(tokens, edge_emb, special_emb, token_to_edge):
        import jax, jax.numpy as jnp
        import numpy as np
        N_NODES = 96
        N_SPECIAL = 3
        D_MODEL = 64
        B, L = (8, 512)
        Bb, Ll = tokens.shape
        sp_idx = jnp.where(tokens < N_SPECIAL, tokens, -1)
        is_special = sp_idx >= 0
        sp_vec = special_emb[jnp.clip(sp_idx, 0, N_SPECIAL - 1)]
        ij = token_to_edge[tokens]
        b_idx = jnp.arange(Bb)[:, None]
        gcn_vec = edge_emb[b_idx, ij[..., 0], ij[..., 1]]
        return jnp.where(is_special[..., None], sp_vec, gcn_vec)

    def _L0_attn_ref(x, Wq, Wk):
        import jax, jax.numpy as jnp
        import numpy as np
        d = x.shape[-1]
        scale = d ** (-0.5)
        q = jnp.einsum('bnd,ed->bne', x, Wq)
        k = jnp.einsum('bnd,ed->bne', x, Wk)
        sim = jnp.einsum('bid,bjd->bij', q, k) * scale
        attn = jax.nn.softmax(sim, axis=-1)
        out = jnp.einsum('bij,bjd->bid', attn, x)
        return out

    def _L0_ffn_ref(x, gate_w, gate_b, w1, b1, w2, b2, gamma, beta):
        import jax, jax.numpy as jnp
        import numpy as np
        B, S, H, F, E, K = (8, 1024, 64, 128, 16, 2)
        EPS = 1e-05
        gate_logits = x @ gate_w + gate_b
        topk_vals, topk_idx = jax.lax.top_k(gate_logits, K)
        topk_w = jax.nn.softmax(topk_vals, axis=-1)
        h = jax.nn.relu(jnp.einsum('bsh,ehf->bsef', x, w1) + b1)
        expert_out = jnp.einsum('bsef,efh->bseh', h, w2) + b2
        sel = jnp.take_along_axis(expert_out, topk_idx[:, :, :, None], axis=2)
        moe = jnp.sum(topk_w[..., None] * sel, axis=2)
        y = x + moe
        mu = jnp.mean(y, axis=-1, keepdims=True)
        var = jnp.var(y, axis=-1, keepdims=True)
        return (y - mu) / jnp.sqrt(var + EPS) * gamma + beta

    def _L1_attn_ref(x, time_w, time_mix_k, time_mix_v, time_mix_r, Wk, Wv, Wr, Wo):
        import jax, jax.numpy as jnp
        import numpy as np
        B, T, C = (16, 512, 64)
        TT = T
        LAYER_ID, N_LAYER = (3, 6)
        Bx, Tx, Cx = x.shape
        maxlen = time_w.shape[0]
        xx = jnp.pad(x, ((0, 0), (1, 0), (0, 0)))[:, :-1]
        xk = x * time_mix_k + xx * (1.0 - time_mix_k)
        xv = x * time_mix_v + xx * (1.0 - time_mix_v)
        xr = x * time_mix_r + xx * (1.0 - time_mix_r)
        k = jnp.exp(jnp.clip(xk @ Wk, -60.0, 30.0))
        v = xv @ Wv
        r = xr @ Wr
        sum_k = jnp.cumsum(k, axis=1)
        kv = k * v
        t_idx = jnp.arange(Tx)
        d = t_idx[:, None] - t_idx[None, :]
        W = jnp.where(d >= 0, time_w[jnp.clip(maxlen - 1 - d, 0, maxlen - 1)], 0.0)
        wkv = jnp.einsum('tu,buc->btc', W, kv)
        rwkv = jax.nn.sigmoid(r) * wkv / sum_k
        return rwkv @ Wo

    def _L1_ffn_ref(x, ln1_w, ln2_w, wq, wk, wv, wo, router_w, w1, w2, w3):
        import jax, jax.numpy as jnp
        import numpy as np
        B, T, C = (64, 96, 64)
        NH, NKV = (4, 2)
        HD = C // NH
        NREP = NH // NKV
        NE, TOPK = (8, 2)
        HID = int(8 / 3 * C)
        EPS_RMS = 1e-06

        def _rope_tables(t_len):
            inv_freq = 1.0 / 10000.0 ** (np.arange(0, HD, 2, dtype=np.float32) / HD)
            t = np.arange(t_len, dtype=np.float32)
            freqs = np.outer(t, inv_freq)
            emb = np.concatenate([freqs, freqs], axis=-1)
            return (jnp.asarray(np.cos(emb)), jnp.asarray(np.sin(emb)))

        def _rotate_half(x):
            h = x.shape[-1] // 2
            return jnp.concatenate([-x[..., h:], x[..., :h]], axis=-1)

        def _rmsnorm(v, w):
            return v * jax.lax.rsqrt(jnp.mean(v * v, axis=-1, keepdims=True) + EPS_RMS) * w
        Bx, Tx, Cx = x.shape
        h = _rmsnorm(x, ln1_w)
        q = (h @ wq.T).reshape(Bx, Tx, NH, HD).transpose(0, 2, 1, 3)
        k = (h @ wk.T).reshape(Bx, Tx, NKV, HD).transpose(0, 2, 1, 3)
        v = (h @ wv.T).reshape(Bx, Tx, NKV, HD).transpose(0, 2, 1, 3)
        cos, sin = _rope_tables(Tx)
        cos, sin = (cos[None, None], sin[None, None])
        q = q * cos + _rotate_half(q) * sin
        k = k * cos + _rotate_half(k) * sin
        k = jnp.repeat(k, NREP, axis=1)
        v = jnp.repeat(v, NREP, axis=1)
        scores = jnp.einsum('bhtd,bhsd->bhts', q, k) / jnp.sqrt(jnp.float32(HD))
        causal = jnp.tril(jnp.ones((Tx, Tx), dtype=bool))
        scores = jnp.where(causal[None, None], scores, jnp.float32(-1e+30))
        att = jax.nn.softmax(scores, axis=-1)
        y = jnp.einsum('bhts,bhsd->bhtd', att, v).transpose(0, 2, 1, 3).reshape(Bx, Tx, Cx)
        x = x + y @ wo.T
        flat = _rmsnorm(x, ln2_w).reshape(-1, Cx)
        probs = jax.nn.softmax(flat @ router_w.T, axis=-1)
        tp, ti = jax.lax.top_k(probs, TOPK)
        tp = tp / (jnp.sum(tp, axis=-1, keepdims=True) + 1e-09)
        weights = jnp.sum(tp[..., None] * jax.nn.one_hot(ti, NE, dtype=flat.dtype), axis=1)
        out = jnp.zeros_like(flat)
        for e in range(NE):
            hh = jax.nn.silu(flat @ w1[e].T) * (flat @ w3[e].T)
            out = out + weights[:, e:e + 1] * (hh @ w2[e].T)
        return x + out.reshape(Bx, Tx, Cx)
    h = _L0_tok_ref(x, L0_tok_edge_emb, L0_tok_special_emb, L0_tok_token_to_edge)
    h = h + _L0_attn_ref(_layernorm(h, axis=-1), L0_attn_Wq, L0_attn_Wk)
    h = h + _L0_ffn_ref(_layernorm(h, axis=-1), L0_ffn_gate_w, L0_ffn_gate_b, L0_ffn_w1, L0_ffn_b1, L0_ffn_w2, L0_ffn_b2, L0_ffn_gamma, L0_ffn_beta)
    h = h + _L1_attn_ref(_layernorm(h, axis=-1), L1_attn_time_w, L1_attn_time_mix_k, L1_attn_time_mix_v, L1_attn_time_mix_r, L1_attn_Wk, L1_attn_Wv, L1_attn_Wr, L1_attn_Wo)
    h = h + _L1_ffn_ref(_layernorm(h, axis=-1), L1_ffn_ln1_w, L1_ffn_ln2_w, L1_ffn_wq, L1_ffn_wk, L1_ffn_wv, L1_ffn_wo, L1_ffn_router_w, L1_ffn_w1, L1_ffn_w2, L1_ffn_w3)
    return h

_drawn_inputs = setup_inputs


def setup_inputs(seed=0):
    import zlib

    import numpy as np

    out = dict(_drawn_inputs(seed))
    spreads = {'L0_ffn_gate_b': (0.0, 0.1),
     'L0_ffn_b1': (0.0, 0.8),
     'L0_ffn_b2': (0.0, 0.1),
     'L0_ffn_gamma': (1.0, 0.2),
     'L0_ffn_beta': (0.0, 0.1),
     'L1_ffn_ln1_w': (1.0, 0.6),
     'L1_ffn_ln2_w': (1.0, 0.6)}
    factors = {'L0_ffn_w1': 7.255,
     'L0_ffn_w2': 5.415,
     'L1_attn_time_w': 8.0,
     'L1_attn_time_mix_k': 8.0,
     'L1_attn_time_mix_v': 8.0,
     'L1_attn_time_mix_r': 8.0,
     'L1_attn_Wk': 8.0,
     'L1_attn_Wv': 8.0,
     'L1_attn_Wr': 8.0,
     'L1_attn_Wo': 8.0,
     'L1_ffn_wq': 8.0,
     'L1_ffn_wk': 8.0,
     'L1_ffn_wv': 8.0,
     'L1_ffn_wo': 8.0,
     'L1_ffn_router_w': 8.0,
     'L1_ffn_w1': 8.0,
     'L1_ffn_w2': 8.0,
     'L1_ffn_w3': 8.0}
    for name, (base, spread) in spreads.items():
        noise = np.random.default_rng([zlib.crc32(name.encode()), seed]).standard_normal(out[name].shape)
        drawn = base * np.exp(spread * noise) if base else spread * noise
        out[name] = jnp.asarray(drawn.astype(out[name].dtype))
    for name, factor in factors.items():
        out[name] = (out[name] * factor).astype(out[name].dtype)
    return out
```

```python
from contextlib import ExitStack

import concourse.bass as bass
import numpy as np
from concourse import mybir

B, L, C = 32, 128, 64
NODES, TAB_B, SPECIAL = 96, 8, 3
ROWS = TAB_B * NODES * NODES
E0, F0 = 16, 128
E1, F1 = 8, 170
FM, FT = 128, 64
NH, NKV, HD = 4, 2, 16
KVR = 3 * C
WS = 64.0
NEG = -1e30
P = 128
HALF = B // 2 * L
IT, UN, UB = 4, 2, 4
PARTS = 3

F32, BF16, FP16, I32 = mybir.dt.float32, mybir.dt.bfloat16, mybir.dt.float16, mybir.dt.int32
ALU, ACT, AX = mybir.AluOpType, mybir.ActivationFunctionType, mybir.AxisListType

COLS = [("ident", P), ("tri", P), ("mask_ts", P), ("mask_st", P), ("cos", 96), ("sin", 96), ("base", B),
        ("pri0", E0), ("pri1", E1), ("eps_ln", 1), ("eps_rms", 1),
        ("wq0", C), ("wk0", C), ("gate_w", E0), ("gate_b", E0), ("b1", E0), ("b2", E0), ("gamma", C), ("beta", C),
        ("mix", 3), ("wkvr", KVR), ("wo0", P), ("toep", P), ("ln1", 1), ("ln2", 1), ("wqkv", P), ("wo1", P),
        ("router", E1)]
COLS16 = [("ident16", P), ("sel0", E0 * P), ("sel1", E1 * P), ("selm", UB * NH * P)]


def offsets(cols):
    at, out = 0, {}
    for name, n in cols:
        out[name] = slice(at, at + n)
        at += n
    return out, at


AT32, N32 = offsets(COLS)
AT16, N16 = offsets(COLS16)


class Steps:

    def __init__(self, sem, names, loop=False):
        self.sem, self.names, self.loop, self.next = sem, names, loop, 0
        self.place = {n: k + 1 for k, n in enumerate(names)}
        assert len(self.place) == len(names)

    def done(self, name):
        assert self.names[self.next % len(self.names)] == name, (self.names[self.next % len(self.names)], name)
        self.next += 1
        return self.sem, 1

    def at(self, name, turn=0, back=0):
        assert self.loop or not back
        if not self.loop:
            return self.sem, self.place[name]
        return self.sem, (turn + 1 - back) * len(self.names) + self.place[name]

    def prime(self, eng):
        eng.sem_inc(self.sem, len(self.names))


def both(*stages):
    return [f"{s}{u}" for s in stages for u in range(UN)]


def lm_tower(nc, tokens, t2e, rows, c32, c16, w1_0, w2_0, w1_1, w3_1, w2m_1, w2t_1, out):
    with ExitStack() as ctx:
        def sb(name, shape, dt=F32):
            return ctx.enter_context(nc.sbuf_tensor(name, shape, dt))

        def sem(name):
            return ctx.enter_context(nc.semaphore(name))

        def grp(ap, n=C):
            return ap.rearrange("p (b f) -> p b f", f=n)

        def bc(ap, n):
            return ap.unsqueeze(len(ap.shape)).to_broadcast([*ap.shape, n])

        def mid(ap, n):
            return ap.unsqueeze(1).to_broadcast([ap.shape[0], n, ap.shape[1]])

        banks = ctx.enter_context(nc.psum_tensor("banks", [P, 8, 512], F32))

        def bank(k, dt=F32):
            return banks[:, k, :] if dt == F32 else banks[:, k, :].bitcast(dt)

        cs = sb("cs", [P, N32])
        ch = sb("ch", [P, N16], FP16)
        k32 = {n: cs[:, s] for n, s in AT32.items()}
        k16 = {n: ch[:, s] for n, s in AT16.items()}
        h = sb("h", [P, B * C])
        x = sb("x", [P, B * C])
        xt = [sb(f"xt{j}", [P, HALF], FP16) for j in range(2)]
        wt = sb("wt", [2 * E0 * PARTS, HALF], BF16)
        acc = sb("acc", [P, HALF])

        w1s, w1h, w1l = sb("w1s", [P, E0 * F0]), sb("w1h", [P, E0 * F0], FP16), sb("w1l", [P, E0 * F0], FP16)
        w2s = sb("w2s", [P, E0 * C])
        NA = E1 * (FM + FT)
        a1s, a1h, a1l = sb("a1s", [P, NA]), sb("a1h", [P, NA], FP16), sb("a1l", [P, NA], FP16)
        a3s, a3h, a3l = sb("a3s", [P, NA]), sb("a3h", [P, NA], FP16), sb("a3l", [P, NA], FP16)
        b1s, b2s = sb("b1s", [P, E0]), sb("b2s", [P, E0])
        w2m, w2t = sb("w2m", [P, E1 * C]), sb("w2t", [P, E1 * C])
        m2 = sb("m2", [P, P])
        gh, gl = sb("gh", [P, E0], FP16), sb("gl", [P, E0], FP16)
        mix1 = sb("mix1", [P, 3])
        kvs, kvh, kvl = sb("kvs", [P, 2, KVR]), sb("kvh", [P, 2, KVR], FP16), sb("kvl", [P, 2, KVR], FP16)
        wtoep = sb("wtoep", [P, P])
        qs, qh_, ql_ = sb("qs", [P, P]), sb("qh", [P, P], FP16), sb("ql", [P, P], FP16)
        rs_, rh, rl = sb("rs", [P, E1]), sb("rh", [P, E1], FP16), sb("rl", [P, E1], FP16)
        identb = sb("identb", [P, P], BF16)
        mask_ts, mask_st = sb("mask_ts", [P, NH, P], BF16), sb("mask_st", [P, NH, P], BF16)

        ld = {n: sem(f"ld_{n}") for n in ("tok", "c32", "c16", "w1", "w2", "a1", "a3", "w2m", "w2t")}
        edges_in = sem("edges_in")
        rows_in = [sem(f"rows_in{g}") for g in range(B // UB)]
        group_in = sem("group_in")
        waited = {n: sem(f"waited_{n}") for n in ("pool", "dve")}
        out_done = [sem(f"out_done{u}") for u in range(UN)]

        tok = sb("tok", [B, L], I32)
        tokf = sb("tokf", [B, L])
        tokt = sb("tokt", [P, B])
        idx1 = sb("idx1", [P, B], I32)
        edge = sb("edge", [P, B, 2], I32)
        edgef = sb("edgef", [P, B, 2])
        rowf, isp, sprow = sb("rowf", [P, B]), sb("isp", [P, B]), sb("sprow", [P, B])
        idx2 = sb("idx2", [P, B], I32)

        ds = Steps(sem("dve_setup"), ["tokf", "tokt", "idx1", "m2z", "m2a", "m2b", "w1l", "gl", "mix1", "kvs",
                                      "kvl", "toep", "qs", "ql", "rs", "rl", "identb", "mask_a", "mask_b",
                                      "edgef", "isp", "row0", "row1", "sprow", "spd", "idx2", "a1s", "a1l", "a3s", "a3l", "b1s", "b2s"])
        as_ = Steps(sem("act_setup"), ["w1h", "gh", "kvh", "qh", "rh", "a1h", "a3h"])
        ts_ = Steps(sem("pe_setup"), ["tokt", "m2"])

        def setup_dve(dve):
            dve.wait_ge(ld["tok"], 16)
            dve.tensor_copy(tokf[:], tok[:]).then_inc(*ds.done("tokf"))
            dve.wait_ge(*ts_.at("tokt"))
            dve.tensor_copy(tokt[:], bank(0)[:, 0:B]).then_inc(*ds.done("tokt"))
            dve.tensor_scalar(idx1[:], bank(0)[:, 0:B], float(SPECIAL + NODES * NODES - 1), 0.0, ALU.min,
                              ALU.max).then_inc(*ds.done("idx1"))
            dve.memset(m2[:], 0.0).then_inc(*ds.done("m2z"))
            dve.wait_ge(*ts_.at("m2"))
            dve.wait_ge(*ds.at("m2z"))
            for j, n in enumerate(("m2a", "m2b")):
                q = slice(C * j, C * j + C)
                dve.tensor_scalar(m2[q, q], bank(1)[q, 0:C], C ** -0.5, None, ALU.mult).then_inc(*ds.done(n))

            def low(name, lo, src, hi, scale=1.0):
                dve.scalar_tensor_tensor(lo, src, scale, hi, ALU.mult, ALU.subtract).then_inc(*ds.done(name))

            dve.wait_ge(ld["w1"], 16)
            dve.wait_ge(*as_.at("w1h"))
            low("w1l", w1l[:], w1s[:], w1h[:], WS)
            dve.wait_ge(*as_.at("gh"))
            low("gl", gl[:], k32["gate_w"], gh[:], WS)
            dve.tensor_scalar(mix1[:], k32["mix"], -1.0, 1.0, ALU.mult, ALU.add).then_inc(*ds.done("mix1"))
            dve.wait_ge(*ds.at("mix1"))
            for m in range(3):
                q = slice(C * m, C * m + C)
                dve.tensor_scalar(kvs[:, 0, q], k32["wkvr"][:, q], k32["mix"][:, m:m + 1], WS, ALU.mult, ALU.mult)
                last = dve.tensor_scalar(kvs[:, 1, q], k32["wkvr"][:, q], mix1[:, m:m + 1], WS, ALU.mult, ALU.mult)
            last.then_inc(*ds.done("kvs"))
            dve.wait_ge(*as_.at("kvh"))
            low("kvl", kvl[:], kvs[:], kvh[:])
            dve.tensor_tensor(wtoep[:], k32["toep"], k32["tri"], ALU.mult).then_inc(*ds.done("toep"))
            dve.tensor_scalar(qs[:], k32["wqkv"], k32["ln1"], WS, ALU.mult, ALU.mult).then_inc(*ds.done("qs"))
            dve.wait_ge(*as_.at("qh"))
            low("ql", ql_[:], qs[:], qh_[:])
            dve.tensor_scalar(rs_[:], k32["router"], k32["ln2"], WS, ALU.mult, ALU.mult).then_inc(*ds.done("rs"))
            dve.wait_ge(*as_.at("rh"))
            low("rl", rl[:], rs_[:], rh[:])
            dve.tensor_copy(identb[:], k32["ident"]).then_inc(*ds.done("identb"))
            dve.tensor_copy(mask_ts[:], mid(k32["mask_ts"], NH)).then_inc(*ds.done("mask_a"))
            dve.tensor_copy(mask_st[:], mid(k32["mask_st"], NH)).then_inc(*ds.done("mask_b"))
            dve.wait_ge(edges_in, 16 * B)
            dve.tensor_scalar(edgef[:], edge[:], float(NODES - 1), 0.0, ALU.min, ALU.max).then_inc(*ds.done("edgef"))
            dve.tensor_scalar(isp[:], tokt[:], float(SPECIAL), None, ALU.is_lt).then_inc(*ds.done("isp"))
            dve.wait_ge(*ds.at("edgef"))
            dve.scalar_tensor_tensor(rowf[:], edgef[:, :, 0], float(NODES), edgef[:, :, 1], ALU.mult,
                                     ALU.add).then_inc(*ds.done("row0"))
            dve.wait_ge(*ds.at("row0"))
            dve.tensor_tensor(rowf[:], rowf[:], k32["base"], ALU.add).then_inc(*ds.done("row1"))
            dve.wait_ge(*ds.at("row1"))
            dve.scalar_tensor_tensor(sprow[:], tokt[:], float(ROWS), rowf[:], ALU.add,
                                     ALU.subtract).then_inc(*ds.done("sprow"))
            dve.wait_ge(*ds.at("sprow"))
            dve.tensor_tensor(sprow[:], sprow[:], isp[:], ALU.mult).then_inc(*ds.done("spd"))
            dve.wait_ge(*ds.at("spd"))
            dve.tensor_tensor(idx2[:], rowf[:], sprow[:], ALU.add).then_inc(*ds.done("idx2"))
            for n, s, hi, lo in (("a1", a1s, a1h, a1l), ("a3", a3s, a3h, a3l)):
                dve.wait_ge(ld[n], 16)
                dve.tensor_scalar(s[:], s[:], k32["ln2"], WS, ALU.mult, ALU.mult).then_inc(*ds.done(n + "s"))
                dve.wait_ge(*as_.at(n + "h"))
                low(n + "l", lo[:], s[:], hi[:])
            dve.tensor_scalar(b1s[:], k32["b1"], WS, None, ALU.mult).then_inc(*ds.done("b1s"))
            dve.tensor_scalar(b2s[:], k32["b2"], WS, None, ALU.mult).then_inc(*ds.done("b2s"))

        def setup_act(act):
            act.wait_ge(ld["w1"], 16)
            act.activation(w1h[:], w1s[:], ACT.Copy, scale=WS).then_inc(*as_.done("w1h"))
            act.wait_ge(ld["c32"], 16)
            act.activation(gh[:], k32["gate_w"], ACT.Copy, scale=WS).then_inc(*as_.done("gh"))
            for n, src, hi, dep in (("kvh", kvs, kvh, "kvs"), ("qh", qs, qh_, "qs"), ("rh", rs_, rh, "rs"),
                                    ("a1h", a1s, a1h, "a1s"), ("a3h", a3s, a3h, "a3s")):
                act.wait_ge(*ds.at(dep))
                act.activation(hi[:], src[:], ACT.Copy).then_inc(*as_.done(n))

        def setup_pe(pe):
            pe.wait_ge(ld["c32"], 16)
            pe.wait_ge(*ds.at("tokf"))
            pe.transpose(bank(0)[:, 0:B], tokf[:], k32["ident"][0:B, 0:B]).then_inc(*ts_.done("tokt"))
            for j in range(2):
                last = pe.matmul(bank(1)[C * j:C * j + C, 0:C], k32["wq0"][0:C, :], k32["wk0"][0:C, :],
                                 start=True, stop=True)
            last.then_inc(*ts_.done("m2"))

        eps_ln, eps_rms = 1e-5, 1e-6
        st = [sb(f"st{u}", [P, 12, UB]) for u in range(UN)]
        xc = [sb(f"xc{u}", [P, UB * C]) for u in range(UN)]
        sq = [sb(f"sq{u}", [P, UB * C]) for u in range(UN)]
        xr = [sb(f"xr{u}", [P, UB * C]) for u in range(UN)]
        tmp = [sb(f"tmp{u}", [P, UB * C]) for u in range(UN)]
        xs = [sb(f"xs{u}", [P, UB, 2, C], FP16) for u in range(UN)]
        fT = [sb(f"fT{u}", [P, 2 * P]) for u in range(UN)]
        qT = [sb(f"qT{u}", [P, 2 * P]) for u in range(UN)]
        at = [sb(f"at{u}", [P, UB, P]) for u in range(UN)]
        atT = [sb(f"atT{u}", [P, UB * P]) for u in range(UN)]
        xt16 = [sb(f"xt16{u}", [P, UB, P], FP16) for u in range(UN)]
        mx = [sb(f"mx{u}", [P, UB]) for u in range(UN)]
        smx = [sb(f"smx{u}", [P, UB]) for u in range(UN)]
        GB = UN * UB
        lg, eq, pr, wr = (sb(n, [P, GB, E0]) for n in ("lg", "eq", "pr", "wr"))
        f1, f2 = sb("f1", [P, GB, E0]), sb("f2", [P, GB, E0])
        sm = sb("sm", [P, 12, GB])
        wpf = sb("wp", [P, GB * E0 * PARTS], BF16)
        wp0 = wpf[:].rearrange("p (b e k) -> p b e k", b=GB, e=E0)
        wrem = sb("wrem", [P, GB, E0])

        NORM_D = ["sum", "mean", "xc", "ss", "var", "na", "nb", "r"]

        def norm_names(p):
            return both(*[p + s for s in NORM_D])

        def norm_dve(dve, D, A, i, p, src, ready):
            for u in range(UN):
                ready(u)
                dve.sem_inc(waited["dve"], 1)
                dve.tensor_reduce(st[u][:, 0, :], src(u), AX.X, ALU.add).then_inc(*D.done(f"{p}sum{u}"))
            for u in range(UN):
                dve.wait_ge(*D.at(f"{p}sum{u}", i))
                dve.tensor_scalar(st[u][:, 1, :], st[u][:, 0, :], 1.0 / C, None, ALU.mult).then_inc(*D.done(f"{p}mean{u}"))
            for u in range(UN):
                dve.wait_ge(*D.at(f"{p}mean{u}", i))
                dve.tensor_tensor(grp(xc[u][:]), src(u), bc(st[u][:, 1, :], C), ALU.subtract).then_inc(*D.done(f"{p}xc{u}"))
            norm_tail_dve(dve, D, A, i, p, eps_ln)

        def norm_tail_dve(dve, D, A, i, p, eps):
            for u in range(UN):
                dve.wait_ge(*A.at(f"{p}sq{u}", i))
                dve.tensor_reduce(st[u][:, 2, :], grp(sq[u][:]), AX.X, ALU.add).then_inc(*D.done(f"{p}ss{u}"))
            for u in range(UN):
                dve.wait_ge(*D.at(f"{p}ss{u}", i))
                dve.tensor_scalar(st[u][:, 3, :], st[u][:, 2, :], 1.0 / C, eps, ALU.mult, ALU.add).then_inc(*D.done(f"{p}var{u}"))
            newton(dve, D, A, i, p)

        def newton(dve, D, A, i, p):
            for u in range(UN):
                dve.wait_ge(*A.at(f"{p}exp{u}", i))
                dve.tensor_tensor(st[u][:, 5, :], st[u][:, 4, :], st[u][:, 4, :], ALU.mult).then_inc(*D.done(f"{p}na{u}"))
            for u in range(UN):
                dve.wait_ge(*D.at(f"{p}na{u}", i))
                dve.scalar_tensor_tensor(st[u][:, 6, :], st[u][:, 5, :], -0.5, st[u][:, 3, :], ALU.mult,
                                         ALU.mult).then_inc(*D.done(f"{p}nb{u}"))
            for u in range(UN):
                dve.wait_ge(*D.at(f"{p}nb{u}", i))
                dve.scalar_tensor_tensor(st[u][:, 7, :], st[u][:, 6, :], 1.5, st[u][:, 4, :], ALU.add,
                                         ALU.mult).then_inc(*D.done(f"{p}r{u}"))

        def norm_act(act, D, A, i, p, dep="xc"):
            for u in range(UN):
                act.wait_ge(*D.at(f"{p}{dep}{u}", i))
                act.activation(sq[u][:], xc[u][:], ACT.Square).then_inc(*A.done(f"{p}sq{u}"))
            for u in range(UN):
                act.wait_ge(*D.at(f"{p}var{u}", i))
                act.activation(st[u][:, 8, :], st[u][:, 3, :], ACT.Ln).then_inc(*A.done(f"{p}ln{u}"))
            for u in range(UN):
                act.wait_ge(*A.at(f"{p}ln{u}", i))
                act.activation(st[u][:, 4, :], st[u][:, 8, :], ACT.Exp, scale=-0.5).then_inc(*A.done(f"{p}exp{u}"))

        NORM_A = ["sq", "ln", "exp"]

        def dyn(buf, i, u, n=UB * C):
            return buf[:, bass.ds(i * (UN * n) + u * n, n)]

        TOP = ["m1", "eq1", "pr1", "pm1", "f1", "l2", "m2", "eq2", "pr2", "pm2", "f2"]

        def top2_dve(dve, D, i, src, w, pri, n_e):
            def one(k, val, m, pm, f):
                dve.tensor_reduce(m, val, AX.X, ALU.max).then_inc(*D.done(f"m{k}"))
                dve.wait_ge(*D.at(f"m{k}", i))
                dve.tensor_tensor(eq[:, :, 0:n_e], val, bc(m, n_e), ALU.is_equal).then_inc(*D.done(f"eq{k}"))
                dve.wait_ge(*D.at(f"eq{k}", i))
                dve.tensor_tensor(pr[:, :, 0:n_e], eq[:, :, 0:n_e], mid(pri, GB), ALU.mult).then_inc(*D.done(f"pr{k}"))
                dve.wait_ge(*D.at(f"pr{k}", i))
                dve.tensor_reduce(pm, pr[:, :, 0:n_e], AX.X, ALU.max).then_inc(*D.done(f"pm{k}"))
                dve.wait_ge(*D.at(f"pm{k}", i))
                dve.tensor_tensor(f, pr[:, :, 0:n_e], bc(pm, n_e), ALU.is_equal).then_inc(*D.done(f"f{k}"))
                dve.wait_ge(*D.at(f"f{k}", i))

            one(1, src, w[:, 0, :], w[:, 1, :], f1[:, :, 0:n_e])
            dve.scalar_tensor_tensor(wr[:, :, 0:n_e], f1[:, :, 0:n_e], -3e38, src, ALU.mult, ALU.add).then_inc(*D.done("l2"))
            dve.wait_ge(*D.at("l2", i))
            one(2, wr[:, :, 0:n_e], w[:, 3, :], w[:, 4, :], f2[:, :, 0:n_e])

        SPLIT = ["wph", "wprem", "wpm", "wpl"]

        def parts_dve(dve, D, i, n_e):
            ww, rem = wr[:, :, 0:n_e], wrem[:, :, 0:n_e]
            w = [wpf[:, 0:GB * n_e * PARTS].rearrange("p (b e k) -> p b e k", b=GB, e=n_e)[:, :, :, k] for k in range(PARTS)]
            dve.tensor_copy(w[0], ww).then_inc(*D.done("wph"))
            dve.wait_ge(*D.at("wph", i))
            dve.tensor_tensor(rem, ww, w[0], ALU.subtract).then_inc(*D.done("wprem"))
            dve.wait_ge(*D.at("wprem", i))
            dve.tensor_copy(w[1], rem).then_inc(*D.done("wpm"))
            dve.wait_ge(*D.at("wpm", i))
            dve.tensor_tensor(w[2], rem, w[1], ALU.subtract).then_inc(*D.done("wpl"))

        d1 = Steps(sem("dve1"), norm_names("a") + both("axn", "qT", "mxa", "mxb", "nmx", "atT", "rs", "yn", "h")
                   + norm_names("b") + both("bxn", "xl", "lg") + TOP
                   + ["dd", "den", "rec", "g2", "wa", "wb", "wc"] + SPLIT, loop=True)
        a1 = Steps(sem("act1"), both(*["a" + s for s in NORM_A]) + both("fT", "exp")
                   + both(*["b" + s for s in NORM_A]) + both("xh", "xt") + ["ed", "wt"], loop=True)
        t1 = Steps(sem("pe1"), both("fT", "qT", "sim", "atT", "av", "xt", "lg") + ["wt"], loop=True)
        p1 = Steps(sem("pool1"), both("xt"), loop=True)

        def xtgrp(j, i, u):
            return xt[j][:, bass.ds(i * (UN * 2 * P) + u * 2 * P, 2 * P)]

        def loop1_dve(dve):
            D = d1
            D.prime(dve)
            with dve.Fori(0, IT) as i:
                def rows(u):
                    return grp(dyn(h, i, u))

                def rows_ready(u):
                    dve.wait_ge(group_in, i * UN + u + 1)
                    dve.wait_ge(*D.at("wpl", i, 1))

                norm_dve(dve, D, a1, i, "a", rows, rows_ready)
                for u in range(UN):
                    dve.wait_ge(*D.at(f"ar{u}", i))
                    dve.wait_ge(*t1.at(f"av{u}", i, 1))
                    dve.tensor_tensor(grp(xr[u][:]), grp(xc[u][:]), bc(st[u][:, 7, :], C), ALU.mult).then_inc(*D.done(f"axn{u}"))
                for u in range(UN):
                    dve.wait_ge(*t1.at(f"qT{u}", i))
                    dve.tensor_copy(qT[u][:], bank(u)[:, 256:512]).then_inc(*D.done(f"qT{u}"))
                for j, n in enumerate(("mxa", "mxb")):
                    for u in range(UN):
                        dve.wait_ge(*t1.at(f"sim{u}", i))
                        dve.tensor_reduce(mx[u][:].rearrange("p (q j) -> p j q", j=2)[:, j, :],
                                          bank(2 + 2 * u + j)[:, 0:256].rearrange("p (q s) -> p q s", q=2), AX.X,
                                          ALU.max).then_inc(*D.done(f"{n}{u}"))
                for u in range(UN):
                    dve.wait_ge(*D.at(f"mxb{u}", i))
                    dve.tensor_scalar(mx[u][:], mx[u][:], -1.0, None, ALU.mult).then_inc(*D.done(f"nmx{u}"))
                for u in range(UN):
                    dve.wait_ge(*t1.at(f"atT{u}", i))
                    dve.tensor_copy(atT[u][:], bank(6 + u)).then_inc(*D.done(f"atT{u}"))
                for u in range(UN):
                    dve.wait_ge(*a1.at(f"exp{u}", i))
                    dve.reciprocal(smx[u][:], smx[u][:]).then_inc(*D.done(f"rs{u}"))
                for u in range(UN):
                    dve.wait_ge(*t1.at(f"av{u}", i))
                    dve.wait_ge(*D.at(f"rs{u}", i))
                    dve.tensor_tensor(grp(tmp[u][:]), grp(bank(u)[:, 0:256]), bc(smx[u][:], C), ALU.mult).then_inc(*D.done(f"yn{u}"))
                for u in range(UN):
                    dve.wait_ge(*D.at(f"yn{u}", i))
                    dve.tensor_tensor(dyn(h, i, u), dyn(h, i, u), tmp[u][:], ALU.add).then_inc(*D.done(f"h{u}"))

                norm_dve(dve, D, a1, i, "b", rows, lambda u: dve.wait_ge(*D.at(f"h{u}", i)))
                for u in range(UN):
                    dve.wait_ge(*D.at(f"br{u}", i))
                    dve.tensor_tensor(grp(dyn(x, i, u)), grp(xc[u][:]), bc(st[u][:, 7, :], C), ALU.mult).then_inc(*D.done(f"bxn{u}"))
                for u in range(UN):
                    dve.wait_ge(*a1.at(f"xh{u}", i))
                    dve.tensor_tensor(xs[u][:, :, 1, :], grp(dyn(x, i, u)), xs[u][:, :, 0, :], ALU.subtract).then_inc(*D.done(f"xl{u}"))
                for u in range(UN):
                    dve.wait_ge(*t1.at(f"lg{u}", i))
                    dve.scalar_tensor_tensor(lg[:, u * UB:(u + 1) * UB, :], grp(bank(4 + u)[:, 0:UB * E0], E0), 1.0 / WS,
                                             mid(k32["gate_b"], UB), ALU.mult, ALU.add).then_inc(*D.done(f"lg{u}"))
                dve.wait_ge(*D.at("lg1", i))
                top2_dve(dve, D, i, lg[:], sm, k32["pri0"], E0)
                dve.tensor_tensor(sm[:, 5, :], sm[:, 3, :], sm[:, 0, :], ALU.subtract).then_inc(*D.done("dd"))
                dve.wait_ge(*a1.at("ed", i))
                dve.tensor_scalar(sm[:, 7, :], sm[:, 6, :], 1.0, None, ALU.add).then_inc(*D.done("den"))
                dve.wait_ge(*D.at("den", i))
                dve.reciprocal(sm[:, 8, :], sm[:, 7, :]).then_inc(*D.done("rec"))
                dve.wait_ge(*D.at("rec", i))
                dve.tensor_tensor(sm[:, 9, :], sm[:, 8, :], sm[:, 6, :], ALU.mult).then_inc(*D.done("g2"))
                dve.wait_ge(*D.at("g2", i))
                dve.tensor_tensor(f1[:], f1[:], bc(sm[:, 8, :], E0), ALU.mult).then_inc(*D.done("wa"))
                dve.tensor_tensor(f2[:], f2[:], bc(sm[:, 9, :], E0), ALU.mult).then_inc(*D.done("wb"))
                dve.wait_ge(*D.at("wb", i))
                dve.tensor_tensor(wr[:], f1[:], f2[:], ALU.add).then_inc(*D.done("wc"))
                dve.wait_ge(*D.at("wc", i))
                dve.wait_ge(*t1.at("wt", i, 1))
                parts_dve(dve, D, i, E0)

        def loop1_act(act):
            A = a1
            A.prime(act)
            with act.Fori(0, IT) as i:
                norm_act(act, d1, A, i, "a")
                for u in range(UN):
                    act.wait_ge(*t1.at(f"fT{u}", i))
                    act.activation(fT[u][:], bank(u)[:, 0:256], ACT.Copy).then_inc(*A.done(f"fT{u}"))
                for u in range(UN):
                    act.wait_ge(*d1.at(f"nmx{u}", i))
                    for k in range(UB):
                        last = act.activation(at[u][:, k, :], bank(2 + 2 * u + k % 2)[:, k // 2 * P:k // 2 * P + P],
                                              ACT.Exp, bias=mx[u][:, k:k + 1], accum_out=smx[u][:, k:k + 1])
                    last.then_inc(*A.done(f"exp{u}"))
                norm_act(act, d1, A, i, "b")
                for u in range(UN):
                    act.wait_ge(*d1.at(f"bxn{u}", i))
                    act.activation(xs[u][:, :, 0, :], grp(dyn(x, i, u)), ACT.Copy).then_inc(*A.done(f"xh{u}"))
                for u in range(UN):
                    act.wait_ge(*t1.at(f"xt{u}", i))
                    act.wait_ge(*p1.at(f"xt{u}", i, 1))
                    act.activation(xt16[u][:].rearrange("p b t -> p (b t)"), bank(2 + u, FP16)[:, 0:512],
                                   ACT.Copy).then_inc(*A.done(f"xt{u}"))
                act.wait_ge(*d1.at("dd", i))
                act.activation(sm[:, 6, :], sm[:, 5, :], ACT.Exp).then_inc(*A.done("ed"))
                act.wait_ge(*t1.at("wt", i))
                act.activation(wt[:, bass.ds(i * 512, 512)], bank(6, BF16)[0:2 * E0 * PARTS, 0:512],
                               ACT.Copy).then_inc(*A.done("wt"))

        def loop1_pool(pool):
            p1.prime(pool)
            pool.wait_ge(*p3.at("z5"))
            with pool.Fori(0, IT) as i:
                for u in range(UN):
                    pool.wait_ge(*a1.at(f"xt{u}", i))
                    for j in range(2):
                        last = pool.tensor_copy(xtgrp(j, i, u).rearrange("p (q t) -> p q t", q=2),
                                                xt16[u][:].rearrange("p (q j) t -> p j q t", j=2)[:, j])
                    last.then_inc(*p1.done(f"xt{u}"))

        def loop1_pe(pe):
            T = t1
            T.prime(pe)
            with pe.Fori(0, IT) as i:
                for u in range(UN):
                    pe.wait_ge(*d1.at(f"axn{u}", i))
                    for q in range(2):
                        last = pe.transpose(bank(u)[:, q * P:q * P + P], xr[u][:, q * P:q * P + P], k32["ident"])
                    last.then_inc(*T.done(f"fT{u}"))
                for u in range(UN):
                    pe.wait_ge(*a1.at(f"fT{u}", i))
                    pe.matmul(bank(u)[:, 256:512], m2[:], fT[u][:], start=True, stop=True).then_inc(*T.done(f"qT{u}"))
                for u in range(UN):
                    pe.wait_ge(*d1.at(f"qT{u}", i))
                    for q in range(2):
                        for j in range(2):
                            r, c = slice(C * j, C * j + C), slice(q * P, q * P + P)
                            last = pe.matmul(bank(2 + 2 * u + j)[:, c], qT[u][r, c], fT[u][r, c], start=True, stop=True)
                    last.then_inc(*T.done(f"sim{u}"))
                for u in range(UN):
                    pe.wait_ge(*a1.at(f"exp{u}", i))
                    for k in range(UB):
                        last = pe.transpose(bank(6 + u)[:, k * P:k * P + P], at[u][:, k, :], k32["ident"])
                    last.then_inc(*T.done(f"atT{u}"))
                for u in range(UN):
                    pe.wait_ge(*d1.at(f"atT{u}", i))
                    for k in range(UB):
                        last = pe.matmul(bank(u)[:, k * C:k * C + C], atT[u][:, k * P:k * P + P], xr[u][:, k * C:k * C + C],
                                         start=True, stop=True)
                    last.then_inc(*T.done(f"av{u}"))
                for u in range(UN):
                    pe.wait_ge(*d1.at(f"xl{u}", i))
                    for k in range(UB):
                        last = pe.transpose(bank(2 + u, FP16)[:, k * P:k * P + P], xs[u][:, k].rearrange("p a c -> p (a c)"),
                                            k16["ident16"])
                    last.then_inc(*T.done(f"xt{u}"))
                for u in range(UN):
                    pe.wait_ge(*a1.at(f"xt{u}", i))
                    for k in range(UB):
                        for w in (gh, gl):
                            last = pe.matmul(bank(4 + u)[:, k * E0:k * E0 + E0], xt16[u][:, k, :], w[:], start=w is gh,
                                             stop=w is gl)
                    last.then_inc(*T.done(f"lg{u}"))
                pe.wait_ge(*d1.at("wpl", i))
                for q in range(GB // 2):
                    last = pe.transpose(bank(6, BF16)[0:2 * E0 * PARTS, q * P:q * P + P],
                                        wp0[:, 2 * q:2 * q + 2].rearrange("p b e k -> p (b e k)"), identb[:])
                last.then_inc(*T.done("wt"))

        N = 512
        hidden = sb("hidden", [P, 4 * N])
        hid = [[hidden[:, (2 * k + j) * N:(2 * k + j + 1) * N] for j in range(2)] for k in range(2)]
        wbs = [sb(f"wbs{k}", [P, N]) for k in range(2)]
        yw = [sb(f"yw{k}", [P, N]) for k in range(2)]
        lag2 = [(e, e - 1) for e in range(E0 + 1)]
        t2 = Steps(sem("pe2"), sum([([f"wb{e}", f"z0{e}", f"z1{e}"] if e < E0 else []) + ([f"y{f}"] if f >= 0 else [])
                                    for e, f in lag2], []), loop=True)
        a2 = Steps(sem("act2"), sum([[f"wb{e}", f"hid{e}"] for e in range(E0)], []), loop=True)
        d2 = Steps(sem("dve2"), sum([([f"hid{e}"] if e < E0 else []) + ([f"yw{f}"] if f >= 0 else [])
                                     for e, f in lag2], []), loop=True)
        p2 = Steps(sem("pool2"), [f"acc{e}" for e in range(E0)], loop=True)

        def before(S, name, e, back, i, n):
            return S.at(f"{name}{e - back}", i) if e >= back else S.at(f"{name}{e - back + n}", i, 1)

        def loop2_pe(pe):
            T = t2
            T.prime(pe)
            pe.wait_ge(*p1.at("xt1", IT - 1))
            pe.wait_ge(*a1.at("wt", IT - 1))
            pe.wait_ge(ld["w2"], 16)
            with pe.Fori(0, IT) as i:
                for e, f in lag2:
                    if e < E0:
                        pe.wait_ge(*before(a2, "wb", e, 2, i, E0))
                        pe.matmul(bank(e % 2), k16["sel0"][0:2 * E0 * PARTS, e * P:(e + 1) * P], wt[:, bass.ts(i, N)],
                                  start=True, stop=True).then_inc(*T.done(f"wb{e}"))
                        for j in range(2):
                            pe.wait_ge(*before(d2 if j else a2, "hid", e, 2, i, E0))
                            for w in (w1h, w1l):
                                last = pe.matmul(bank(2 + 2 * (e % 2) + j), w[:, e * F0:(e + 1) * F0], xt[j][:, bass.ts(i, N)],
                                                 start=w is w1h, stop=w is w1l)
                            last.then_inc(*T.done(f"z{j}{e}"))
                    if f >= 0:
                        pe.wait_ge(*a2.at(f"hid{f}", i))
                        pe.wait_ge(*d2.at(f"hid{f}", i))
                        for j in range(2):
                            last = pe.matmul(bank(6 + f % 2)[C * j:C * j + C, :], w2s[:, f * C:(f + 1) * C], hid[f % 2][j][:],
                                             start=True, stop=True)
                        last.then_inc(*T.done(f"y{f}"))

        def loop2_act(act):
            A = a2
            A.prime(act)
            with act.Fori(0, IT) as i:
                for e in range(E0):
                    act.wait_ge(*t2.at(f"wb{e}", i))
                    act.wait_ge(*before(d2, "yw", e, 2, i, E0))
                    act.activation(wbs[e % 2][:], bank(e % 2), ACT.Copy).then_inc(*A.done(f"wb{e}"))
                    act.wait_ge(*t2.at(f"z0{e}", i))
                    act.activation(hid[e % 2][0][:], bank(2 + 2 * (e % 2)), ACT.Relu,
                                   bias=b1s[:, e:e + 1]).then_inc(*A.done(f"hid{e}"))

        def loop2_dve(dve):
            D = d2
            D.prime(dve)
            with dve.Fori(0, IT) as i:
                for e, f in lag2:
                    if e < E0:
                        dve.wait_ge(*t2.at(f"z1{e}", i))
                        dve.tensor_scalar(hid[e % 2][1][:], bank(3 + 2 * (e % 2)), b1s[:, e:e + 1], 0.0, ALU.add,
                                          ALU.max).then_inc(*D.done(f"hid{e}"))
                    if f >= 0:
                        dve.wait_ge(*t2.at(f"y{f}", i))
                        dve.wait_ge(*a2.at(f"wb{f}", i))
                        dve.wait_ge(*before(p2, "acc", f, 2, i, E0))
                        dve.scalar_tensor_tensor(yw[f % 2][:], bank(6 + f % 2), b2s[:, f:f + 1], wbs[f % 2][:], ALU.add,
                                                 ALU.mult).then_inc(*D.done(f"yw{f}"))

        accs = sb("accs", [P, N])

        def moe_pool(pool, S, D, ne):
            S.prime(pool)
            with pool.Fori(0, IT) as i:
                for e in range(ne):
                    pool.wait_ge(*D.at(f"yw{e}", i))
                    pool.wait_ge(*before(S, "acc", e, 1, i, ne))
                    if e == 0:
                        pool.sem_inc(waited["pool"], 1)
                        pool.tensor_copy(accs[:], yw[0][:]).then_inc(*S.done("acc0"))
                    elif e < ne - 1:
                        pool.tensor_tensor(accs[:], accs[:], yw[e % 2][:], ALU.add).then_inc(*S.done(f"acc{e}"))
                    else:
                        pool.sem_inc(waited["pool"], 1)
                        pool.tensor_tensor(acc[:, bass.ts(i, N)], accs[:], yw[e % 2][:], ALU.add).then_inc(*S.done(f"acc{e}"))

        ar = qT
        xp = [sb(f"xp{u}", [P, UB, L + 1], FP16) for u in range(UN)]
        kc, ek, er, kv, rw = ([sb(f"{n}{u}", [P, UB * C]) for u in range(UN)] for n in ("kc", "ek", "er", "kv", "rw"))
        rT = [sb(f"rT{u}", [P, 2 * P]) for u in range(UN)]
        ra, rb = ([sb(f"{n}{u}", [P, UB, 96]) for u in range(UN)] for n in ("ra", "rb"))
        qr = [sb(f"qr{u}", [P, UB * NH, HD]) for u in range(UN)]
        kr = [sb(f"kr{u}", [P, UB * NKV, HD]) for u in range(UN)]
        qst = [sb(f"qst{u}", [P, UB * NH, 2, 2, HD], FP16) for u in range(UN)]
        kst = [sb(f"kst{u}", [P, UB * NKV, 2, 2, 2, HD], FP16) for u in range(UN)]
        va = [sb(f"va{u}", [P, UB, NKV, 32]) for u in range(UN)]
        qb = [sb(f"qb{u}", [P, UB * NKV, 2, P], FP16) for u in range(UN)]
        kd = [sb(f"kd{u}", [P, UB * NKV * P], FP16) for u in range(UN)]
        mh = [sb(f"mh{u}", [P, UB * NH]) for u in range(UN)]
        mrem = [sb(f"mrem{u}", [P, UB * NH]) for u in range(UN)]
        mp = [sb(f"mp{u}", [P, 2, UB * NH, PARTS], BF16) for u in range(UN)]
        mT = [sb(f"mT{u}", [UB * NH * PARTS, P], BF16) for u in range(UN)]
        ex = [grp(w1s[:], NH * P), grp(hidden[:], NH * P)]
        ot = atT
        yt = kv
        rc = [sb(f"rc{u}", [P, UB * NH]) for u in range(UN)]

        TAIL_D = ["ss", "var", "na", "nb", "r"]
        d3 = Steps(sem("dve3"),
                   both("y") + norm_names("c") + both("cx", "cg", "h") + norm_names("d") + both("dxn", "dl", "kc", "kv", "den", "rden",
                                                                                          "rw", "ho")
                   + norm_names("e") + both("ex", "e1", "e2", "fvar", "fna", "fnb", "fr", "e3", "hn", "fl")
                   + both("ra", "rb", "qr", "kr", "ql", "kl", "qb", "kd", "mx0", "mx1", "mx2", "mx3", "mh", "mrem", "mm", "ml",
                          "rc", "yt", "xm") + both(*["g" + s for s in TAIL_D]) + both("gf", "gl", "lg")
                   + ["sx", "ls", "se", "rse", "pb"] + TOP + ["d0", "d1", "d2", "ff", "fp", "wc"] + SPLIT, loop=True)
        a3 = Steps(sem("act3"),
                   both(*["c" + s for s in NORM_A]) + both(*["d" + s for s in NORM_A]) + both("dh", "xp", "er", "ek", "rT")
                   + both(*["e" + s for s in NORM_A]) + both("fln", "fexp", "fh", "xt", "va", "qh", "kh", "qb", "mT",
                                                             "ex0", "ex1", "ex2", "ex3", "ot", "yT")
                   + both(*["g" + s for s in NORM_A]) + both("gh", "xt3") + ["es", "wt"], loop=True)
        t3 = Steps(sem("pe3"), both("aT", "dx", "kvr", "sum", "rT", "wo", "fx", "qkv", "qT", "s0", "s1", "s2", "s3", "mT",
                                    "t0", "t1", "t2", "t3", "oT", "o", "yT", "wo1", "gx", "lg") + ["wt"], loop=True)
        p3 = Steps(sem("pool3"), ["z0", "z1", "z2", "z3", "z4", "z5"], loop=False)
        q3 = Steps(sem("pool3b"), both("ar", "hb", "xt"), loop=True)

        def newton_to(dve, D, A, i, p, row):
            for u in range(UN):
                dve.wait_ge(*A.at(f"{p}exp{u}", i))
                dve.tensor_tensor(st[u][:, 5, :], st[u][:, 4, :], st[u][:, 4, :], ALU.mult).then_inc(*D.done(f"{p}na{u}"))
            for u in range(UN):
                dve.wait_ge(*D.at(f"{p}na{u}", i))
                dve.scalar_tensor_tensor(st[u][:, 6, :], st[u][:, 5, :], -0.5, st[u][:, 3, :], ALU.mult,
                                         ALU.mult).then_inc(*D.done(f"{p}nb{u}"))
            for u in range(UN):
                dve.wait_ge(*D.at(f"{p}nb{u}", i))
                dve.scalar_tensor_tensor(st[u][:, row, :], st[u][:, 6, :], 1.5, st[u][:, 4, :], ALU.add,
                                         ALU.mult).then_inc(*D.done(f"{p}r{u}"))

        def loop3_dve(dve):
            D = d3
            D.prime(dve)
            with dve.Fori(0, IT) as i:
                def state(u):
                    return grp(dyn(h, i, u))

                for u in range(UN):
                    dve.wait_ge(*t3.at(f"aT{u}", i))
                    dve.wait_ge(*D.at("wpl", i, 1))
                    dve.scalar_tensor_tensor(tmp[u][:], bank(4 * u)[:, 0:256], 1.0 / WS, dyn(x, i, u), ALU.mult,
                                             ALU.add).then_inc(*D.done(f"y{u}"))
                norm_dve(dve, D, a3, i, "c", lambda u: grp(tmp[u][:]), lambda u: dve.wait_ge(*D.at(f"y{u}", i)))
                for u in range(UN):
                    dve.wait_ge(*D.at(f"cr{u}", i))
                    dve.tensor_tensor(grp(xc[u][:]), grp(xc[u][:]), bc(st[u][:, 7, :], C), ALU.mult).then_inc(*D.done(f"cx{u}"))
                for u in range(UN):
                    dve.wait_ge(*D.at(f"cx{u}", i))
                    dve.tensor_tensor(grp(xc[u][:]), grp(xc[u][:]), mid(k32["gamma"], UB), ALU.mult).then_inc(*D.done(f"cg{u}"))
                for u in range(UN):
                    dve.wait_ge(*D.at(f"cg{u}", i))
                    dve.wait_ge(*q3.at(f"hb{u}", i))
                    dve.tensor_tensor(dyn(h, i, u), dyn(h, i, u), xc[u][:], ALU.add).then_inc(*D.done(f"h{u}"))
                norm_dve(dve, D, a3, i, "d", state, lambda u: dve.wait_ge(*D.at(f"h{u}", i)))
                for u in range(UN):
                    dve.wait_ge(*D.at(f"dr{u}", i))
                    dve.tensor_tensor(grp(xr[u][:]), grp(xc[u][:]), bc(st[u][:, 7, :], C), ALU.mult).then_inc(*D.done(f"dxn{u}"))
                for u in range(UN):
                    dve.wait_ge(*a3.at(f"dh{u}", i))
                    dve.tensor_tensor(xs[u][:, :, 1, :], grp(xr[u][:]), xs[u][:, :, 0, :], ALU.subtract).then_inc(*D.done(f"dl{u}"))

                def kvr(u, q, m):
                    return bank(4 * u + q)[:, 0:2 * KVR].rearrange("p (b n) -> p b n", b=2)[:, :, m * C:(m + 1) * C]

                for u in range(UN):
                    dve.wait_ge(*t3.at(f"kvr{u}", i))
                    for q in range(2):
                        last = dve.tensor_scalar(grp(kc[u][:, q * P:(q + 1) * P]), kvr(u, q, 0), 30.0 * WS, -60.0 * WS, ALU.min,
                                                 ALU.max)
                    last.then_inc(*D.done(f"kc{u}"))
                for u in range(UN):
                    dve.wait_ge(*a3.at(f"ek{u}", i))
                    for q in range(2):
                        last = dve.tensor_tensor(grp(kv[u][:, q * P:(q + 1) * P]), kvr(u, q, 1), grp(ek[u][:, q * P:(q + 1) * P]),
                                                 ALU.mult)
                    last.then_inc(*D.done(f"kv{u}"))
                for u in range(UN):
                    dve.wait_ge(*t3.at(f"sum{u}", i))
                    dve.scalar_tensor_tensor(er[u][:], er[u][:], 1.0, bank(4 * u + 2)[:, 0:256], ALU.add,
                                             ALU.mult).then_inc(*D.done(f"den{u}"))
                for u in range(UN):
                    dve.wait_ge(*D.at(f"den{u}", i))
                    dve.reciprocal(er[u][:], er[u][:]).then_inc(*D.done(f"rden{u}"))
                for u in range(UN):
                    dve.wait_ge(*D.at(f"rden{u}", i))
                    dve.tensor_tensor(rw[u][:], bank(4 * u + 2)[:, 256:512], er[u][:], ALU.mult).then_inc(*D.done(f"rw{u}"))
                for u in range(UN):
                    dve.wait_ge(*t3.at(f"wo{u}", i))
                    dve.scalar_tensor_tensor(dyn(h, i, u), bank(4 * u + 3)[:, 256:512], 1.0 / WS, dyn(h, i, u), ALU.mult,
                                             ALU.add).then_inc(*D.done(f"ho{u}"))
                norm_dve(dve, D, a3, i, "e", state, lambda u: dve.wait_ge(*D.at(f"ho{u}", i)))
                for u in range(UN):
                    dve.wait_ge(*D.at(f"er{u}", i))
                    dve.tensor_tensor(grp(dyn(x, i, u)), grp(xc[u][:]), bc(st[u][:, 7, :], C), ALU.mult).then_inc(*D.done(f"ex{u}"))
                for u in range(UN):
                    dve.scalar_tensor_tensor(st[u][:, 9, :], st[u][:, 2, :], 1.0 / C, st[u][:, 7, :], ALU.mult,
                                             ALU.mult).then_inc(*D.done(f"e1{u}"))
                for u in range(UN):
                    dve.wait_ge(*D.at(f"e1{u}", i))
                    dve.tensor_tensor(st[u][:, 9, :], st[u][:, 9, :], st[u][:, 7, :], ALU.mult).then_inc(*D.done(f"e2{u}"))
                for u in range(UN):
                    dve.wait_ge(*D.at(f"e2{u}", i))
                    dve.tensor_scalar(st[u][:, 3, :], st[u][:, 9, :], eps_rms, None, ALU.add).then_inc(*D.done(f"fvar{u}"))
                newton_to(dve, D, a3, i, "f", 10)
                for u in range(UN):
                    dve.wait_ge(*D.at(f"fr{u}", i))
                    dve.tensor_tensor(st[u][:, 11, :], st[u][:, 10, :], st[u][:, 7, :], ALU.mult).then_inc(*D.done(f"e3{u}"))
                for u in range(UN):
                    dve.wait_ge(*D.at(f"e3{u}", i))
                    dve.tensor_tensor(grp(tmp[u][:]), grp(xc[u][:]), bc(st[u][:, 11, :], C), ALU.mult).then_inc(*D.done(f"hn{u}"))
                for u in range(UN):
                    dve.wait_ge(*a3.at(f"fh{u}", i))
                    dve.tensor_tensor(xs[u][:, :, 1, :], grp(tmp[u][:]), xs[u][:, :, 0, :], ALU.subtract).then_inc(*D.done(f"fl{u}"))

                def qkv(u):
                    return bank(4 * u + 1).rearrange("p (b n) -> p b n", b=UB)

                def halves(ap):
                    return ap.rearrange("p b (g s d) -> p b g s d", g=NH + NKV, s=2)

                def table(name, s):
                    return k32[name].rearrange("p (g s d) -> p g s d", g=NH + NKV, s=2)[:, :, s, :].unsqueeze(1) \
                        .to_broadcast([P, UB, NH + NKV, HD // 2])

                for u in range(UN):
                    dve.wait_ge(*a3.at(f"va{u}", i))
                    dve.tensor_tensor(ra[u][:], qkv(u)[:, :, 0:96], mid(k32["cos"], UB), ALU.mult).then_inc(*D.done(f"ra{u}"))
                for u in range(UN):
                    for s in range(2):
                        last = dve.tensor_tensor(halves(rb[u][:])[:, :, :, s, :], halves(qkv(u)[:, :, 0:96])[:, :, :, 1 - s, :],
                                                 table("sin", s), ALU.mult)
                    last.then_inc(*D.done(f"rb{u}"))
                for u in range(UN):
                    dve.wait_ge(*D.at(f"rb{u}", i))
                    dve.tensor_tensor(qr[u][:].rearrange("p (b g) d -> p b (g d)", b=UB), ra[u][:, :, 0:C], rb[u][:, :, 0:C],
                                      ALU.add).then_inc(*D.done(f"qr{u}"))
                for u in range(UN):
                    dve.tensor_tensor(kr[u][:].rearrange("p (b g) d -> p b (g d)", b=UB), ra[u][:, :, C:96], rb[u][:, :, C:96],
                                      ALU.add).then_inc(*D.done(f"kr{u}"))
                for u in range(UN):
                    dve.wait_ge(*a3.at(f"qh{u}", i))
                    q2 = qr[u][:].unsqueeze(2).to_broadcast([P, UB * NH, 2, HD])
                    dve.tensor_tensor(qst[u][:, :, :, 1, :], q2, qst[u][:, :, :, 0, :], ALU.subtract).then_inc(*D.done(f"ql{u}"))
                for u in range(UN):
                    dve.wait_ge(*a3.at(f"kh{u}", i))
                    k2 = kr[u][:].unsqueeze(2).to_broadcast([P, UB * NKV, 2, HD])
                    for s in range(2):
                        last = dve.tensor_tensor(kst[u][:, :, s, 1, :, :], k2, kst[u][:, :, s, 0, :, :], ALU.subtract)
                    last.then_inc(*D.done(f"kl{u}"))
                for u in range(UN):
                    dve.wait_ge(*t3.at(f"qT{u}", i))
                    dve.tensor_copy(qb[u][C:P, :, 1, :], bank(4 * u, FP16)[C:P, :].rearrange("p (g t) -> p g t", t=P)
                                    ).then_inc(*D.done(f"qb{u}"))
                for u in range(UN):
                    dve.tensor_copy(kd[u][:], bank(4 * u + 2, FP16)).then_inc(*D.done(f"kd{u}"))
                for k in range(UB):
                    for u in range(UN):
                        dve.wait_ge(*t3.at(f"s{k}{u}", i))
                        dve.tensor_reduce(mh[u][:, k * NH:(k + 1) * NH], grp(bank(4 * u + k), P), AX.X,
                                          ALU.max).then_inc(*D.done(f"mx{k}{u}"))
                for u in range(UN):
                    dve.wait_ge(*D.at(f"mx3{u}", i))
                    dve.tensor_scalar(mp[u][:, 0, :, 0], mh[u][:], -1.0, None, ALU.mult).then_inc(*D.done(f"mh{u}"))
                for u in range(UN):
                    dve.wait_ge(*D.at(f"mh{u}", i))
                    dve.scalar_tensor_tensor(mrem[u][:], mh[u][:], -1.0, mp[u][:, 0, :, 0], ALU.mult,
                                             ALU.subtract).then_inc(*D.done(f"mrem{u}"))
                for u in range(UN):
                    dve.wait_ge(*D.at(f"mrem{u}", i))
                    dve.tensor_copy(mp[u][:, 0, :, 1], mrem[u][:]).then_inc(*D.done(f"mm{u}"))
                for u in range(UN):
                    dve.wait_ge(*D.at(f"mm{u}", i))
                    dve.tensor_tensor(mp[u][:, 0, :, 2], mrem[u][:], mp[u][:, 0, :, 1], ALU.subtract).then_inc(*D.done(f"ml{u}"))

                def heads(u):
                    return bank(4 * u + 1).rearrange("p (g n) -> p g n", n=32)

                for u in range(UN):
                    dve.wait_ge(*t3.at(f"o{u}", i))
                    dve.reciprocal(rc[u][:], heads(u)[:, :, HD]).then_inc(*D.done(f"rc{u}"))
                for u in range(UN):
                    dve.wait_ge(*D.at(f"rc{u}", i))
                    dve.tensor_tensor(grp(yt[u][:], HD), heads(u)[:, :, 0:HD], bc(rc[u][:], HD), ALU.mult).then_inc(*D.done(f"yt{u}"))
                for u in range(UN):
                    dve.wait_ge(*t3.at(f"wo1{u}", i))
                    dve.tensor_tensor(dyn(x, i, u), bank(4 * u + 2)[:, 256:512], dyn(x, i, u), ALU.add).then_inc(*D.done(f"xm{u}"))
                norm_tail_dve(dve, D, a3, i, "g", eps_rms)
                for u in range(UN):
                    dve.wait_ge(*D.at(f"gr{u}", i))
                    dve.tensor_tensor(grp(tmp[u][:]), grp(dyn(x, i, u)), bc(st[u][:, 7, :], C), ALU.mult).then_inc(*D.done(f"gf{u}"))
                for u in range(UN):
                    dve.wait_ge(*a3.at(f"gh{u}", i))
                    dve.tensor_tensor(xs[u][:, :, 1, :], grp(tmp[u][:]), xs[u][:, :, 0, :], ALU.subtract).then_inc(*D.done(f"gl{u}"))
                l8, w8 = lg[:, :, 0:E1], wr[:, :, 0:E1]
                for u in range(UN):
                    dve.wait_ge(*t3.at(f"lg{u}", i))
                    dve.tensor_scalar(l8[:, u * UB:(u + 1) * UB, :], grp(bank(4 * u)[:, 0:UB * E1], E1), 1.0 / WS, None,
                                      ALU.mult).then_inc(*D.done(f"lg{u}"))
                dve.wait_ge(*D.at("lg1", i))
                dve.tensor_reduce(sm[:, 5, :], l8, AX.X, ALU.max).then_inc(*D.done("sx"))
                dve.wait_ge(*D.at("sx", i))
                dve.tensor_tensor(l8, l8, bc(sm[:, 5, :], E1), ALU.subtract).then_inc(*D.done("ls"))
                dve.wait_ge(*a3.at("es", i))
                dve.tensor_reduce(sm[:, 6, :], w8, AX.X, ALU.add).then_inc(*D.done("se"))
                dve.wait_ge(*D.at("se", i))
                dve.reciprocal(sm[:, 7, :], sm[:, 6, :]).then_inc(*D.done("rse"))
                dve.wait_ge(*D.at("rse", i))
                dve.tensor_tensor(l8, w8, bc(sm[:, 7, :], E1), ALU.mult).then_inc(*D.done("pb"))
                dve.wait_ge(*D.at("pb", i))
                top2_dve(dve, D, i, l8, sm, k32["pri1"], E1)
                dve.tensor_tensor(sm[:, 8, :], sm[:, 0, :], sm[:, 3, :], ALU.add).then_inc(*D.done("d0"))
                dve.wait_ge(*D.at("d0", i))
                dve.tensor_scalar(sm[:, 9, :], sm[:, 8, :], 1e-9, None, ALU.add).then_inc(*D.done("d1"))
                dve.wait_ge(*D.at("d1", i))
                dve.reciprocal(sm[:, 10, :], sm[:, 9, :]).then_inc(*D.done("d2"))
                ff = f1[:, :, 0:E1]
                dve.tensor_tensor(ff, ff, f2[:, :, 0:E1], ALU.add).then_inc(*D.done("ff"))
                dve.wait_ge(*D.at("ff", i))
                dve.tensor_tensor(ff, ff, l8, ALU.mult).then_inc(*D.done("fp"))
                dve.wait_ge(*D.at("fp", i))
                dve.tensor_tensor(w8, ff, bc(sm[:, 10, :], E1), ALU.mult).then_inc(*D.done("wc"))
                dve.wait_ge(*D.at("wc", i))
                dve.wait_ge(*t3.at("wt", i, 1))
                parts_dve(dve, D, i, E1)

        def loop3_act(act):
            A = a3
            A.prime(act)
            with act.Fori(0, IT) as i:
                norm_act(act, d3, A, i, "c")
                norm_act(act, d3, A, i, "d")
                for u in range(UN):
                    act.wait_ge(*d3.at(f"dxn{u}", i))
                    act.activation(xs[u][:, :, 0, :], grp(xr[u][:]), ACT.Copy).then_inc(*A.done(f"dh{u}"))
                for u in range(UN):
                    act.wait_ge(*t3.at(f"dx{u}", i))
                    act.activation(xp[u][:, :, 1:L + 1], grp(bank(4 * u + 1, FP16)[:, 0:512], P), ACT.Copy).then_inc(*A.done(f"xp{u}"))
                for u in range(UN):
                    act.wait_ge(*d3.at(f"kc{u}", i))
                    for q in range(2):
                        r = bank(4 * u + q)[:, 0:2 * KVR].rearrange("p (b n) -> p b n", b=2)[:, :, 2 * C:3 * C]
                        last = act.activation(grp(er[u][:, q * P:(q + 1) * P]), r, ACT.Exp, scale=-1.0 / WS)
                    last.then_inc(*A.done(f"er{u}"))
                for u in range(UN):
                    act.activation(ek[u][:], kc[u][:], ACT.Exp, scale=1.0 / WS).then_inc(*A.done(f"ek{u}"))
                for u in range(UN):
                    act.wait_ge(*t3.at(f"rT{u}", i))
                    act.activation(rT[u][:], bank(4 * u + 3)[:, 0:256], ACT.Copy).then_inc(*A.done(f"rT{u}"))
                norm_act(act, d3, A, i, "e")
                for u in range(UN):
                    act.wait_ge(*d3.at(f"fvar{u}", i))
                    act.activation(st[u][:, 8, :], st[u][:, 3, :], ACT.Ln).then_inc(*A.done(f"fln{u}"))
                for u in range(UN):
                    act.wait_ge(*A.at(f"fln{u}", i))
                    act.activation(st[u][:, 4, :], st[u][:, 8, :], ACT.Exp, scale=-0.5).then_inc(*A.done(f"fexp{u}"))
                for u in range(UN):
                    act.wait_ge(*d3.at(f"hn{u}", i))
                    act.activation(xs[u][:, :, 0, :], grp(tmp[u][:]), ACT.Copy).then_inc(*A.done(f"fh{u}"))
                for u in range(UN):
                    act.wait_ge(*t3.at(f"fx{u}", i))
                    act.activation(xt16[u][:].rearrange("p b t -> p (b t)"), bank(4 * u, FP16)[:, 0:512],
                                   ACT.Copy).then_inc(*A.done(f"xt{u}"))
                for u in range(UN):
                    act.wait_ge(*t3.at(f"qkv{u}", i))
                    v = bank(4 * u + 1).rearrange("p (b n) -> p b n", b=UB)[:, :, 96:P].rearrange("p b (g d) -> p b g d", g=NKV)
                    act.activation(va[u][:, :, :, 0:HD], v, ACT.Copy, scale=1.0 / WS).then_inc(*A.done(f"va{u}"))
                for u in range(UN):
                    act.wait_ge(*d3.at(f"qr{u}", i))
                    q2 = qr[u][:].unsqueeze(2).to_broadcast([P, UB * NH, 2, HD])
                    act.activation(qst[u][:, :, :, 0, :], q2, ACT.Copy).then_inc(*A.done(f"qh{u}"))
                for u in range(UN):
                    act.wait_ge(*d3.at(f"kr{u}", i))
                    k2 = kr[u][:].unsqueeze(2).to_broadcast([P, UB * NKV, 2, HD])
                    for s in range(2):
                        last = act.activation(kst[u][:, :, s, 0, :, :], k2, ACT.Copy)
                    last.then_inc(*A.done(f"kh{u}"))
                for u in range(UN):
                    act.wait_ge(*t3.at(f"qT{u}", i))
                    act.activation(qb[u][0:C, :, 0, :], bank(4 * u, FP16)[0:C, :].rearrange("p (g t) -> p g t", t=P),
                                   ACT.Copy).then_inc(*A.done(f"qb{u}"))
                for u in range(UN):
                    act.wait_ge(*t3.at(f"mT{u}", i))
                    act.activation(mT[u][:], bank(4 * u, BF16)[0:UB * NH * PARTS, 0:P], ACT.Copy).then_inc(*A.done(f"mT{u}"))
                for k in range(UB):
                    for u in range(UN):
                        act.wait_ge(*t3.at(f"t{k}{u}", i))
                        act.activation(ex[u][:, k, :], bank(4 * u + k), ACT.Exp).then_inc(*A.done(f"ex{k}{u}"))
                for u in range(UN):
                    act.wait_ge(*t3.at(f"oT{u}", i))
                    act.activation(ot[u][:], bank(4 * u), ACT.Copy).then_inc(*A.done(f"ot{u}"))
                for u in range(UN):
                    act.wait_ge(*t3.at(f"yT{u}", i))
                    act.activation(rT[u][:], bank(4 * u + 2)[:, 0:256], ACT.Copy).then_inc(*A.done(f"yT{u}"))
                for u in range(UN):
                    act.wait_ge(*d3.at(f"xm{u}", i))
                    act.activation(sq[u][:], dyn(x, i, u), ACT.Square).then_inc(*A.done(f"gsq{u}"))
                for u in range(UN):
                    act.wait_ge(*d3.at(f"gvar{u}", i))
                    act.activation(st[u][:, 8, :], st[u][:, 3, :], ACT.Ln).then_inc(*A.done(f"gln{u}"))
                for u in range(UN):
                    act.wait_ge(*A.at(f"gln{u}", i))
                    act.activation(st[u][:, 4, :], st[u][:, 8, :], ACT.Exp, scale=-0.5).then_inc(*A.done(f"gexp{u}"))
                for u in range(UN):
                    act.wait_ge(*d3.at(f"gf{u}", i))
                    act.activation(xs[u][:, :, 0, :], grp(tmp[u][:]), ACT.Copy).then_inc(*A.done(f"gh{u}"))
                for u in range(UN):
                    act.wait_ge(*t3.at(f"gx{u}", i))
                    act.activation(xt16[u][:].rearrange("p b t -> p (b t)"), bank(4 * u + 3, FP16)[:, 0:512],
                                   ACT.Copy).then_inc(*A.done(f"xt3{u}"))
                act.wait_ge(*d3.at("ls", i))
                act.activation(wr[:, :, 0:E1], lg[:, :, 0:E1], ACT.Exp).then_inc(*A.done("es"))
                act.wait_ge(*t3.at("wt", i))
                act.activation(wt[:, bass.ts(i, N)], bank(1, BF16)[0:2 * E0 * PARTS, 0:512], ACT.Copy).then_inc(*A.done("wt"))

        def pool3_zeros(pool):
            for u in range(UN):
                last = pool.memset(xp[u][:, :, 0:1], 0.0)
            last.then_inc(*p3.done("z0"))
            for u in range(UN):
                last = pool.memset(va[u][:], 0.0)
            last.then_inc(*p3.done("z1"))
            pool.wait_ge(*p3.at("z1"))
            for u in range(UN):
                last = pool.memset(va[u][:, :, :, HD:HD + 1], 1.0)
            last.then_inc(*p3.done("z2"))
            pool.wait_ge(*p3.at("z2"))
            for u in range(UN):
                last = pool.memset(qb[u][0:C, :, 1, :], 0.0)
            last.then_inc(*p3.done("z3"))
            pool.wait_ge(*p3.at("z3"))
            for u in range(UN):
                last = pool.memset(qb[u][C:P, :, 0, :], 0.0)
            last.then_inc(*p3.done("z4"))
            pool.wait_ge(*p3.at("z4"))
            for u in range(UN):
                last = pool.memset(mp[u][:], 0.0)
            last.then_inc(*p3.done("z5"))

        def loop3_pool(pool):
            S = q3
            S.prime(pool)
            with pool.Fori(0, IT) as i:
                for u in range(UN):
                    pool.wait_ge(*t3.at(f"aT{u}", i, 1))
                    if u == 0:
                        pool.wait_ge(*p2.at(f"acc{E0 - 1}", IT - 1))
                    pool.tensor_copy(ar[u][:], acc[:, bass.ds(i * UN * 2 * P + u * 2 * P, 2 * P)]).then_inc(*S.done(f"ar{u}"))
                for u in range(UN):
                    if u == 0:
                        pool.wait_ge(*d1.at("h1", IT - 1))
                    pool.tensor_tensor(grp(dyn(h, i, u)), grp(dyn(h, i, u)), mid(k32["beta"], UB), ALU.add).then_inc(*S.done(f"hb{u}"))
                for u in range(UN):
                    pool.wait_ge(*a3.at(f"xt3{u}", i))
                    for j in range(2):
                        last = pool.tensor_copy(xtgrp(j, i, u).rearrange("p (q t) -> p q t", q=2),
                                                xt16[u][:].rearrange("p (q j) t -> p j q t", j=2)[:, j])
                    last.then_inc(*S.done(f"xt{u}"))

        def loop3_pe(pe):
            T = t3
            T.prime(pe)

            def transposes(u, k, dt, src, ident, name, n=UB, w=P):
                for q in range(n):
                    last = pe.transpose(bank(4 * u + k, dt)[:, q * w:(q + 1) * w], src(q), ident)
                last.then_inc(*T.done(f"{name}{u}"))

            pe.wait_ge(*p3.at("z5"))
            pe.wait_ge(*ds.at("kvl"))
            pe.wait_ge(*ds.at("rl"))
            pe.wait_ge(*ds.at("mask_b"))
            with pe.Fori(0, IT) as i:
                def stack(u):
                    return lambda q: xs[u][:, q].rearrange("p a c -> p (a c)")

                for u in range(UN):
                    pe.wait_ge(*q3.at(f"ar{u}", i))
                    transposes(u, 0, F32, lambda q: ar[u][:, q * P:(q + 1) * P], k32["ident"], "aT", 2)
                for u in range(UN):
                    pe.wait_ge(*d3.at(f"dl{u}", i))
                    transposes(u, 1, FP16, stack(u), k16["ident16"], "dx")
                for u in range(UN):
                    pe.wait_ge(*a3.at(f"xp{u}", i))
                    for k in range(UB):
                        dst = bank(4 * u + k // 2)[:, k % 2 * KVR:(k % 2 + 1) * KVR]
                        for n, (w, before_) in enumerate(((kvh, 0), (kvl, 0), (kvh, 1), (kvl, 1))):
                            last = pe.matmul(dst, xp[u][:, k, 1 - before_:L + 1 - before_], w[:, before_, :], start=n == 0,
                                             stop=n == 3)
                    last.then_inc(*T.done(f"kvr{u}"))
                for u in range(UN):
                    pe.wait_ge(*d3.at(f"kv{u}", i))
                    pe.matmul(bank(4 * u + 2)[:, 0:256], k32["tri"], ek[u][:], start=True, stop=True)
                    pe.matmul(bank(4 * u + 2)[:, 256:512], wtoep[:], kv[u][:], start=True, stop=True).then_inc(*T.done(f"sum{u}"))
                for u in range(UN):
                    pe.wait_ge(*d3.at(f"rw{u}", i))
                    transposes(u, 3, F32, lambda q: rw[u][:, q * P:(q + 1) * P], k32["ident"], "rT", 2)
                for u in range(UN):
                    pe.wait_ge(*a3.at(f"rT{u}", i))
                    for q in range(2):
                        last = pe.matmul(bank(4 * u + 3)[:, 256 + q * P:256 + (q + 1) * P], rT[u][:, q * P:(q + 1) * P], k32["wo0"],
                                         start=True, stop=True)
                    last.then_inc(*T.done(f"wo{u}"))
                for u in range(UN):
                    pe.wait_ge(*d3.at(f"fl{u}", i))
                    transposes(u, 0, FP16, stack(u), k16["ident16"], "fx")
                for u in range(UN):
                    pe.wait_ge(*a3.at(f"xt{u}", i))
                    for k in range(UB):
                        for w in (qh_, ql_):
                            last = pe.matmul(bank(4 * u + 1)[:, k * P:(k + 1) * P], xt16[u][:, k, :], w[:], start=w is qh_,
                                             stop=w is ql_)
                    last.then_inc(*T.done(f"qkv{u}"))
                for u in range(UN):
                    pe.wait_ge(*d3.at(f"kl{u}", i))
                    for g in range(UB * NKV):
                        pe.transpose(bank(4 * u, FP16)[:, g * P:(g + 1) * P],
                                     qst[u][:, 2 * g:2 * g + 2].rearrange("p g s two d -> p (g s two d)"), k16["ident16"])
                    for g in range(UB * NKV):
                        last = pe.transpose(bank(4 * u + 2, FP16)[:, g * P:(g + 1) * P],
                                            kst[u][:, g].rearrange("p a s two d -> p (a s two d)"), k16["ident16"])
                    last.then_inc(*T.done(f"qT{u}"))
                for k in range(UB):
                    for u in range(UN):
                        if k == 0:
                            pe.wait_ge(*a3.at(f"qb{u}", i))
                            pe.wait_ge(*d3.at(f"kd{u}", i))
                        dst = bank(4 * u + k)
                        pe.matmul(dst, identb[:], mask_ts[:].rearrange("p h t -> p (h t)"), start=True, stop=False,
                                  skip_group_check=True)
                        for n in range(NH):
                            last = pe.matmul(dst[:, n * P:(n + 1) * P], qb[u][:, NKV * k + n // 2, n % 2, :],
                                             kd[u][:, (NKV * k + n // 2) * P:(NKV * k + n // 2 + 1) * P], start=False,
                                             stop=n == NH - 1, skip_group_check=True)
                        last.then_inc(*T.done(f"s{k}{u}"))
                for u in range(UN):
                    pe.wait_ge(*d3.at(f"ml{u}", i))
                    pe.transpose(bank(4 * u, BF16)[0:2 * UB * NH * PARTS, 0:P], mp[u][:].rearrange("p z a b -> p (z a b)"),
                                 identb[:]).then_inc(*T.done(f"mT{u}"))
                for k in range(UB):
                    for u in range(UN):
                        if k == 0:
                            pe.wait_ge(*a3.at(f"mT{u}", i))
                        dst = bank(4 * u + k)
                        pe.matmul(dst, identb[:], mask_st[:].rearrange("p h t -> p (h t)"), start=True, stop=False,
                                  skip_group_check=True)
                        for n in range(NH):
                            pe.matmul(dst[:, n * P:(n + 1) * P],
                                      k16["selm"][0:UB * NH * PARTS, (NH * k + n) * P:(NH * k + n + 1) * P], mT[u][:],
                                      start=False, stop=False, skip_group_check=True)
                        for g in range(NKV):
                            q = NKV * k + g
                            last = pe.matmul(dst[:, g * 256:(g + 1) * 256], kd[u][:, q * P:(q + 1) * P],
                                             qb[u][:, q].rearrange("p a t -> p (a t)"), start=False, stop=g == NKV - 1,
                                             skip_group_check=True)
                        last.then_inc(*T.done(f"t{k}{u}"))
                for u in range(UN):
                    for k in range(UB):
                        pe.wait_ge(*a3.at(f"ex{k}{u}", i))
                        for n in range(NH):
                            last = pe.matmul(bank(4 * u)[32 * n:32 * n + 32, k * P:(k + 1) * P], va[u][:, k, n // 2, :],
                                             ex[u][:, k, n * P:(n + 1) * P], start=True, stop=True)
                    last.then_inc(*T.done(f"oT{u}"))
                for u in range(UN):
                    pe.wait_ge(*a3.at(f"ot{u}", i))
                    transposes(u, 1, F32, lambda q: ot[u][:, q * P:(q + 1) * P], k32["ident"], "o")
                for u in range(UN):
                    pe.wait_ge(*d3.at(f"yt{u}", i))
                    transposes(u, 2, F32, lambda q: yt[u][:, q * P:(q + 1) * P], k32["ident"], "yT", 2)
                for u in range(UN):
                    pe.wait_ge(*a3.at(f"yT{u}", i))
                    for q in range(2):
                        last = pe.matmul(bank(4 * u + 2)[:, 256 + q * P:256 + (q + 1) * P], rT[u][:, q * P:(q + 1) * P], k32["wo1"],
                                         start=True, stop=True)
                    last.then_inc(*T.done(f"wo1{u}"))
                for u in range(UN):
                    pe.wait_ge(*d3.at(f"gl{u}", i))
                    transposes(u, 3, FP16, stack(u), k16["ident16"], "gx")
                for u in range(UN):
                    pe.wait_ge(*a3.at(f"xt3{u}", i))
                    for k in range(UB):
                        for w in (rh, rl):
                            last = pe.matmul(bank(4 * u)[:, k * E1:(k + 1) * E1], xt16[u][:, k, :], w[:], start=w is rh,
                                             stop=w is rl)
                    last.then_inc(*T.done(f"lg{u}"))
                pe.wait_ge(*d3.at("wpl", i))
                for q in range(GB // 2):
                    w = 2 * E1 * PARTS
                    last = pe.transpose(bank(1, BF16)[0:2 * w, q * P:(q + 1) * P], wpf[:, q * w:(q + 2) * w], identb[:])
                last.then_inc(*T.done("wt"))

        hm = hid
        ht = [[w1s[:, (2 * k + j) * N:(2 * k + j + 1) * N] for j in range(2)] for k in range(2)]
        sa = [a1s[:, k * N:(k + 1) * N] for k in range(2)]
        units = []
        for q in range(E1 // 2):
            for chunk, cols, buf in ((f"main{2 * q}", 2 * q * FM, hm[0]), (f"tail{q}", E1 * FM + q * P, ht[q % 2]),
                                     (f"main{2 * q + 1}", (2 * q + 1) * FM, hm[1])):
                units += [(chunk, cols, buf[j], j) for j in range(2)]
        plan = []
        for q in range(E1 // 2):
            n = 6 * q
            plan += [("wb", 2 * q), ("ab", n)] + ([("y", 2 * q - 1)] if q else []) + [("ab", n + 1), ("ab", n + 2), ("ab", n + 3),
                     ("wb", 2 * q + 1), ("ab", n + 4), ("y", 2 * q), ("ab", n + 5)]
        plan.append(("y", E1 - 1))
        t4 = Steps(sem("pe4"), [f"{a}{n}" for a, n in plan], loop=True)
        a4 = Steps(sem("act4"), [f"{'silu' if a == 'ab' else a}{n}" for a, n in plan if a != "y"], loop=True)
        d4 = Steps(sem("dve4"), [f"{'u' if a == 'ab' else 'yw'}{n}" for a, n in plan if a != "wb"], loop=True)
        p4 = Steps(sem("pool4"), [f"acc{e}" for e in range(E1)], loop=True)
        NU = len(units)

        def loop4_pe(pe):
            T = t4
            T.prime(pe)
            pe.wait_ge(*q3.at("xt1", IT - 1))
            pe.wait_ge(*a3.at("wt", IT - 1))
            pe.wait_ge(*ds.at("a3l"))
            pe.wait_ge(ld["w2m"], 16)
            pe.wait_ge(ld["w2t"], 16)
            with pe.Fori(0, IT) as i:
                for kind, n in plan:
                    if kind == "wb":
                        pe.wait_ge(*before(a4, "wb", n, 2, i, E1))
                        pe.matmul(bank(n % 2), k16["sel1"][0:2 * E0 * PARTS, n * P:(n + 1) * P], wt[:, bass.ts(i, N)], start=True, stop=True).then_inc(*T.done(f"wb{n}"))
                    elif kind == "ab":
                        _, cols, _, j = units[n]
                        pe.wait_ge(*before(d4, "u", n, 2, i, NU))
                        for m, (hi, lo) in enumerate(((a1h, a1l), (a3h, a3l))):
                            for w in (hi, lo):
                                last = pe.matmul(bank(2 + 2 * (n % 2) + m), w[:, cols:cols + P], xt[j][:, bass.ts(i, N)],
                                                 start=w is hi, stop=w is lo)
                        last.then_inc(*T.done(f"ab{n}"))
                    else:
                        pe.wait_ge(*d4.at(f"u{6 * (n // 2) + (5 if n % 2 else 3)}", i))
                        for w, buf in ((w2m, hm[n % 2]), (w2t, ht[n // 2 % 2])):
                            for j in range(2):
                                last = pe.matmul(bank(6 + n % 2)[C * j:C * j + C, :], w[:, n * C:(n + 1) * C], buf[j][:],
                                                 start=w is w2m, stop=w is w2t, skip_group_check=True)
                        last.then_inc(*T.done(f"y{n}"))

        def loop4_act(act):
            A = a4
            A.prime(act)
            with act.Fori(0, IT) as i:
                for kind, n in plan:
                    if kind == "wb":
                        act.wait_ge(*t4.at(f"wb{n}", i))
                        act.wait_ge(*before(d4, "yw", n, 2, i, E1))
                        act.activation(wbs[n % 2][:], bank(n % 2), ACT.Copy).then_inc(*A.done(f"wb{n}"))
                    elif kind == "ab":
                        act.wait_ge(*t4.at(f"ab{n}", i))
                        act.wait_ge(*before(d4, "u", n, 2, i, NU))
                        act.activation(sa[n % 2][:], bank(2 + 2 * (n % 2)), ACT.Silu, scale=1.0 / WS).then_inc(*A.done(f"silu{n}"))

        def loop4_dve(dve):
            D = d4
            D.prime(dve)
            with dve.Fori(0, IT) as i:
                for kind, n in plan:
                    if kind == "ab":
                        dve.wait_ge(*a4.at(f"silu{n}", i))
                        dve.tensor_tensor(units[n][2][:], sa[n % 2][:], bank(3 + 2 * (n % 2)), ALU.mult).then_inc(*D.done(f"u{n}"))
                    elif kind == "y":
                        dve.wait_ge(*t4.at(f"y{n}", i))
                        dve.wait_ge(*a4.at(f"wb{n}", i))
                        dve.wait_ge(*before(p4, "acc", n, 2, i, E1))
                        dve.tensor_tensor(yw[n % 2][:], bank(6 + n % 2), wbs[n % 2][:], ALU.mult).then_inc(*D.done(f"yw{n}"))

        ob = rw
        p5 = Steps(sem("pool5"), both("ar"), loop=True)
        t5 = Steps(sem("pe5"), both("aT"), loop=True)
        d5 = Steps(sem("dve5"), both("o", "out"), loop=True)

        def loop5_pool(pool):
            p5.prime(pool)
            pool.wait_ge(*p4.at(f"acc{E1 - 1}", IT - 1))
            with pool.Fori(0, IT) as i:
                for u in range(UN):
                    pool.wait_ge(*t5.at(f"aT{u}", i, 1))
                    pool.tensor_copy(ar[u][:], acc[:, bass.ds(i * UN * 2 * P + u * 2 * P, 2 * P)]).then_inc(*p5.done(f"ar{u}"))

        def loop5_pe(pe):
            t5.prime(pe)
            with pe.Fori(0, IT) as i:
                for u in range(UN):
                    pe.wait_ge(*p5.at(f"ar{u}", i))
                    pe.wait_ge(*d5.at(f"o{u}", i, 1))
                    for q in range(2):
                        last = pe.transpose(bank(u)[:, q * P:(q + 1) * P], ar[u][:, q * P:(q + 1) * P], k32["ident"])
                    last.then_inc(*t5.done(f"aT{u}"))

        def loop5_dve(dve):
            d5.prime(dve)
            with dve.Fori(0, IT) as i:
                for u in range(UN):
                    dve.wait_ge(*t5.at(f"aT{u}", i))
                    dve.wait_ge(out_done[u], i * 16)
                    dve.scalar_tensor_tensor(ob[u][:], bank(u)[:, 0:256], 1.0 / WS, dyn(x, i, u), ALU.mult,
                                             ALU.add).then_inc(*d5.done(f"o{u}"))
                for u in range(UN):
                    dve.wait_ge(*d5.at(f"o{u}", i))
                    dve.tensor_tensor(ob[u][:], ob[u][:], dyn(h, i, u), ALU.add).then_inc(*d5.done(f"out{u}"))

        out_v = out.rearrange("b t c -> t b c")

        def loop5_sync(sp):
            with sp.Fori(0, IT) as i:
                for u in range(UN):
                    sp.wait_ge(*d5.at(f"out{u}", i))
                    sp.dma_start(out_v[:, bass.ds(i * GB + u * UB, UB), :], grp(ob[u][:])).then_inc(out_done[u], 16)
            for u in range(UN):
                sp.wait_ge(out_done[u], 16 * IT)

        block = ctx.enter_context(nc.Block())

        @block.sync
        def _(sp):
            sp.dma_start(cs[:], c32).then_inc(ld["c32"], 16)
            for n, dst, src in (("w1", w1s, w1_0), ("c16", ch, c16), ("w2", w2s, w2_0), ("a1", a1s, w1_1),
                                ("a3", a3s, w3_1), ("w2m", w2m, w2m_1), ("w2t", w2t, w2t_1)):
                sp.dma_start(dst[:], src).then_inc(ld[n], 16)
            for g in range(B // UB):
                sp.wait_ge(rows_in[g], 16 * UB)
                sp.sem_inc(group_in, 1)
            loop5_sync(sp)

        @block.gpsimd
        def _(pool):
            pool.wait_ge(*ds.at("idx1"))
            for b in range(B):
                pool.indirect_dma_start(edge[:, b, :], None, t2e, bass.IndirectOffsetOnAxis(ap=idx1[:, b:b + 1], axis=0)
                                        ).then_inc(edges_in, 16)
            pool.wait_ge(*ds.at("idx2"))
            for b in range(B):
                pool.indirect_dma_start(h[:, b * C:(b + 1) * C], None, rows,
                                        bass.IndirectOffsetOnAxis(ap=idx2[:, b:b + 1], axis=0)
                                        ).then_inc(rows_in[b // UB], 16)
            pool3_zeros(pool)
            loop1_pool(pool)
            moe_pool(pool, p2, d2, E0)
            loop3_pool(pool)
            moe_pool(pool, p4, d4, E1)
            loop5_pool(pool)

        @block.scalar
        def _(act):
            act.dma_start(tok[:], tokens).then_inc(ld["tok"], 16)
            setup_act(act)
            loop1_act(act)
            loop2_act(act)
            loop3_act(act)
            loop4_act(act)

        @block.vector
        def _(dve):
            setup_dve(dve)
            loop1_dve(dve)
            loop2_dve(dve)
            loop3_dve(dve)
            loop4_dve(dve)
            loop5_dve(dve)

        @block.tensor
        def _(pe):
            setup_pe(pe)
            pe.wait_ge(ld["c16"], 16)
            loop1_pe(pe)
            loop2_pe(pe)
            loop3_pe(pe)
            loop4_pe(pe)
            loop5_pe(pe)


def packed(ins):
    f = np.float32
    t = np.arange(P)
    v = {"ident": np.eye(P, dtype=f), "tri": (t[:, None] <= t[None, :]).astype(f),
         "mask_ts": np.where(t[None, :] <= t[:, None], 0.0, NEG).astype(f),
         "mask_st": np.where(t[:, None] <= t[None, :], 0.0, NEG).astype(f)}
    inv = 1.0 / 10000.0 ** (np.arange(0, HD, 2, dtype=f) / HD)
    ang = np.outer(t.astype(f), inv).astype(f)
    cos, sin = np.cos(ang), np.sin(ang)
    scale = np.array([HD ** -0.5] * NH + [1.0] * NKV, f) / f(WS)
    v["cos"] = (scale[None, :, None] * np.concatenate([cos, cos], 1)[:, None, :]).reshape(P, 96)
    v["sin"] = (scale[None, :, None] * np.concatenate([-sin, sin], 1)[:, None, :]).reshape(P, 96)
    v["base"] = np.broadcast_to(np.minimum(np.arange(B), TAB_B - 1) * NODES * NODES, (P, B))
    v["pri0"] = np.broadcast_to(E0 - np.arange(E0), (P, E0))
    v["pri1"] = np.broadcast_to(E1 - np.arange(E1), (P, E1))
    v["eps_ln"], v["eps_rms"] = np.full((P, 1), 1e-5), np.full((P, 1), 1e-6)

    def twice(a):
        return np.concatenate([a, a], 0)

    def rows_(a):
        return np.broadcast_to(a[None, :], (P, a.shape[0]))

    def diag(a):
        d = np.zeros((P, P), f)
        d[:C, :C] = a
        d[C:, C:] = a
        return d

    g = ins
    v["wq0"], v["wk0"] = twice(g["L0_attn_Wq"]), twice(g["L0_attn_Wk"])
    v["gate_w"], v["gate_b"] = twice(g["L0_ffn_gate_w"]), rows_(g["L0_ffn_gate_b"])
    v["b1"], v["b2"] = g["L0_ffn_b1"].T, twice(g["L0_ffn_b2"].T)
    v["gamma"], v["beta"] = rows_(g["L0_ffn_gamma"]), rows_(g["L0_ffn_beta"])
    v["mix"] = twice(np.stack([g[f"L1_attn_time_mix_{m}"].reshape(C) for m in "kvr"], 1))
    v["wkvr"] = twice(np.concatenate([g[f"L1_attn_W{m}"] for m in "kvr"], 1))
    v["wo0"] = diag(g["L1_attn_Wo"])
    tw = g["L1_attn_time_w"]
    v["toep"] = tw[np.clip(tw.shape[0] - 1 - (t[None, :] - t[:, None]), 0, tw.shape[0] - 1)]
    v["ln1"], v["ln2"] = twice(g["L1_ffn_ln1_w"][:, None]), twice(g["L1_ffn_ln2_w"][:, None])
    v["wqkv"] = twice(np.concatenate([g["L1_ffn_wq"], g["L1_ffn_wk"], g["L1_ffn_wv"]], 0).T)
    v["wo1"] = diag(g["L1_ffn_wo"].T)
    v["router"] = twice(g["L1_ffn_router_w"].T)
    big = np.zeros((P, N32), f)
    for n, s in AT32.items():
        big[:, s] = v[n]
    return big


def selectors():
    out = np.zeros((P, N16), np.float16)
    out[:, AT16["ident16"]] = np.eye(P)
    for name, ne in (("sel0", E0), ("sel1", E1)):
        s = np.zeros((P, ne, P), np.float16)
        for j in range(2):
            for e in range(ne):
                r = (j * ne + e) * PARTS
                s[r:r + PARTS, e, j * C:(j + 1) * C] = 1
        out[:, AT16[name]] = s.reshape(P, -1)
    s = np.zeros((P, UB * NH, P), np.float16)
    for k in range(UB * NH):
        s[k * PARTS:(k + 1) * PARTS, k, :] = 1
    out[:, AT16["selm"]] = s.reshape(P, -1)
    return out


def laid_out(ins):
    def twice(a):
        return np.concatenate([a, a], 0)

    a = {"tokens": ins["x"], "t2e": ins["L0_tok_token_to_edge"],
         "rows": np.concatenate([ins["L0_tok_edge_emb"].reshape(ROWS, C), ins["L0_tok_special_emb"]], 0),
         "c32": packed(ins), "c16": selectors(),
         "w1_0": twice(ins["L0_ffn_w1"].transpose(1, 0, 2).reshape(C, E0 * F0)),
         "w2_0": ins["L0_ffn_w2"].transpose(1, 0, 2).reshape(F0, E0 * C)}
    for n, w in (("w1_1", ins["L1_ffn_w1"]), ("w3_1", ins["L1_ffn_w3"])):
        wt = w.transpose(2, 0, 1)
        tail = np.zeros((C, E1, FT), np.float32)
        tail[:, :, :F1 - FM] = wt[:, :, FM:]
        a[n] = twice(np.concatenate([wt[:, :, :FM].reshape(C, -1), tail.reshape(C, -1)], 1))
    wt = ins["L1_ffn_w2"].transpose(2, 0, 1)
    tail = np.zeros((2, FT, E1, C), np.float32)
    for e in range(E1):
        tail[e % 2, :F1 - FM, e] = wt[FM:, e]
    a["w2m_1"], a["w2t_1"] = wt[:FM].reshape(FM, -1), tail.reshape(P, -1)
    return {n: np.ascontiguousarray(v) for n, v in a.items()}


def kernel(**inputs):
    import concourse.bacc as _bacc
    from concourse.bass_utils import run_bass_kernel_spmd as _run

    nc = _bacc.Bacc("TRN2", target_bir_lowering=False, num_devices=1)
    arrays, args = {}, []
    for name, a in laid_out({n: np.asarray(v) for n, v in inputs.items()}).items():
        arrays[f"in_{name}"] = a
        args.append(nc.dram_tensor(f"in_{name}", a.shape, mybir.dt.from_np(a.dtype), kind="ExternalInput").ap())
    args.append(nc.dram_tensor("tower_out", (B, L, C), F32, kind="ExternalOutput").ap())
    lm_tower(nc, *args)
    r = _run(nc, [arrays], core_ids=[0])
    return r.results[0]["tower_out"]
```

```python
from contextlib import ExitStack

import concourse.bass as bass
import numpy as np
from concourse import mybir

B, L, C = 32, 128, 64
NODES, TAB_B, SPECIAL = 96, 8, 3
ROWS = TAB_B * NODES * NODES
E0, F0 = 16, 128
E1, F1 = 8, 170
FM, FT = 128, 64
NH, NKV, HD = 4, 2, 16
KVR = 3 * C
WS = 64.0
NEG = -1e30
P = 128
HALF = B // 2 * L
IT, UN, UB = 4, 2, 4
PARTS = 3

F32, BF16, FP16, I32 = mybir.dt.float32, mybir.dt.bfloat16, mybir.dt.float16, mybir.dt.int32
ALU, ACT, AX = mybir.AluOpType, mybir.ActivationFunctionType, mybir.AxisListType

COLS = [("ident", P), ("tri", P), ("mask_ts", P), ("mask_st", P), ("cos", 96), ("sin", 96), ("base", B),
        ("pri0", E0), ("pri1", E1), ("eps_ln", 1), ("eps_rms", 1),
        ("wq0", C), ("wk0", C), ("gate_w", E0), ("gate_b", E0), ("b1", E0), ("b2", E0), ("gamma", C), ("beta", C),
        ("mix", 3), ("wkvr", KVR), ("wo0", P), ("toep", P), ("ln1", 1), ("ln2", 1), ("wqkv", P), ("wo1", P),
        ("router", E1)]
COLS16 = [("ident16", P), ("sel0", E0 * P), ("sel1", E1 * P), ("selm", UB * NH * P)]


def offsets(cols):
    at, out = 0, {}
    for name, n in cols:
        out[name] = slice(at, at + n)
        at += n
    return out, at


AT32, N32 = offsets(COLS)
AT16, N16 = offsets(COLS16)


class Steps:

    def __init__(self, sem, names, loop=False):
        self.sem, self.names, self.loop, self.next = sem, names, loop, 0
        self.place = {n: k + 1 for k, n in enumerate(names)}
        assert len(self.place) == len(names)

    def done(self, name):
        assert self.names[self.next % len(self.names)] == name, (self.names[self.next % len(self.names)], name)
        self.next += 1
        return self.sem, 1

    def at(self, name, turn=0, back=0):
        assert self.loop or not back
        if not self.loop:
            return self.sem, self.place[name]
        return self.sem, (turn + 1 - back) * len(self.names) + self.place[name]

    def prime(self, eng):
        eng.sem_inc(self.sem, len(self.names))


def both(*stages):
    return [f"{s}{u}" for s in stages for u in range(UN)]


def lm_tower(nc, tokens, t2e, rows, c32, c16, w1_0, w2_0, w1_1, w3_1, w2m_1, w2t_1, out):
    with ExitStack() as ctx:
        def sb(name, shape, dt=F32):
            return ctx.enter_context(nc.sbuf_tensor(name, shape, dt))

        def sem(name):
            return ctx.enter_context(nc.semaphore(name))

        def grp(ap, n=C):
            return ap.rearrange("p (b f) -> p b f", f=n)

        def bc(ap, n):
            return ap.unsqueeze(len(ap.shape)).to_broadcast([*ap.shape, n])

        def mid(ap, n):
            return ap.unsqueeze(1).to_broadcast([ap.shape[0], n, ap.shape[1]])

        banks = ctx.enter_context(nc.psum_tensor("banks", [P, 8, 512], F32))

        def bank(k, dt=F32):
            return banks[:, k, :] if dt == F32 else banks[:, k, :].bitcast(dt)

        cs = sb("cs", [P, N32])
        ch = sb("ch", [P, N16], FP16)
        k32 = {n: cs[:, s] for n, s in AT32.items()}
        k16 = {n: ch[:, s] for n, s in AT16.items()}
        h = sb("h", [P, B * C])
        x = sb("x", [P, B * C])
        xt = [sb(f"xt{j}", [P, HALF], FP16) for j in range(2)]
        wt = sb("wt", [2 * E0 * PARTS, HALF], BF16)
        acc = sb("acc", [P, HALF])

        w1s, w1h, w1l = sb("w1s", [P, E0 * F0]), sb("w1h", [P, E0 * F0], FP16), sb("w1l", [P, E0 * F0], FP16)
        w2s = sb("w2s", [P, E0 * C])
        NA = E1 * (FM + FT)
        a1s, a1h, a1l = sb("a1s", [P, NA]), sb("a1h", [P, NA], FP16), sb("a1l", [P, NA], FP16)
        a3s, a3h, a3l = sb("a3s", [P, NA]), sb("a3h", [P, NA], FP16), sb("a3l", [P, NA], FP16)
        b1s, b2s = sb("b1s", [P, E0]), sb("b2s", [P, E0])
        w2m, w2t = sb("w2m", [P, E1 * C]), sb("w2t", [P, E1 * C])
        m2 = sb("m2", [P, P])
        gh, gl = sb("gh", [P, E0], FP16), sb("gl", [P, E0], FP16)
        mix1 = sb("mix1", [P, 3])
        kvs, kvh, kvl = sb("kvs", [P, 2, KVR]), sb("kvh", [P, 2, KVR], FP16), sb("kvl", [P, 2, KVR], FP16)
        wtoep = sb("wtoep", [P, P])
        qs, qh_, ql_ = sb("qs", [P, P]), sb("qh", [P, P], FP16), sb("ql", [P, P], FP16)
        rs_, rh, rl = sb("rs", [P, E1]), sb("rh", [P, E1], FP16), sb("rl", [P, E1], FP16)
        identb = sb("identb", [P, P], BF16)
        mask_ts, mask_st = sb("mask_ts", [P, NH, P], BF16), sb("mask_st", [P, NH, P], BF16)

        ld = {n: sem(f"ld_{n}") for n in ("tok", "c32", "c16", "w1", "w2", "a1", "a3", "w2m", "w2t")}
        edges_in = [sem(f"edges_in{t}") for t in range(IT)]
        rows_in = [sem(f"rows_in{g}") for g in range(B // UB)]
        group_in = sem("group_in")
        waited = {n: sem(f"waited_{n}") for n in ("pool", "dve")}
        out_done = sem("out_done")

        tok = sb("tok", [B, L], I32)
        tokf = sb("tokf", [B, L])
        tokt = sb("tokt", [P, B])
        idx1 = sb("idx1", [P, B], I32)
        edge = sb("edge", [P, B, 2], I32)
        edgef = sb("edgef", [P, B, 2])
        rowf, isp, sprow, spt = (sb(n, [P, B]) for n in ("rowf", "isp", "sprow", "spt"))
        idx2 = sb("idx2", [P, B], I32)

        ds = Steps(sem("dve_setup"), ["tokf", "tokt", "idx1", "spt", "m2z", "m2a", "m2b", "w1l", "gl", "mix1", "kvs",
                                      "kvl", "toep", "qs", "ql", "rs", "rl", "identb", "mask_a", "mask_b", "a1s", "a1l", "a3s", "a3l", "b1s", "b2s"])
        as_ = Steps(sem("act_setup"), ["w1h", "gh", "kvh", "qh", "rh", "a1h", "a3h"])
        ts_ = Steps(sem("pe_setup"), ["tokt", "m2"])

        px = Steps(sem("pool_index"), [f"{s}{t}" for t in range(IT) for s in
                                       ("edgef", "isp", "row0", "row1", "row2", "sprow", "spd", "row3", "idx2")])

        def edges_pool(pool, lo, hi):
            for b in range(lo, hi):
                pool.indirect_dma_start(edge[:, b, :], None, t2e, bass.IndirectOffsetOnAxis(ap=idx1[:, b:b + 1], axis=0)
                                        ).then_inc(edges_in[b // (UN * UB)], 16)

        def index_pool(pool, t):
            b = slice(t * UN * UB, (t + 1) * UN * UB)
            pool.wait_ge(edges_in[t], 16 * UN * UB)
            pool.tensor_scalar(edgef[:, b], edge[:, b], float(NODES - 1), 0.0, ALU.min, ALU.max).then_inc(*px.done(f"edgef{t}"))
            pool.tensor_scalar(isp[:, b], tokt[:, b], float(SPECIAL), None, ALU.is_lt).then_inc(*px.done(f"isp{t}"))
            pool.wait_ge(*px.at(f"edgef{t}"))
            pool.tensor_scalar(rowf[:, b], edgef[:, b, 0], float(NODES), None, ALU.mult).then_inc(*px.done(f"row0{t}"))
            pool.wait_ge(*px.at(f"row0{t}"))
            pool.tensor_tensor(rowf[:, b], rowf[:, b], edgef[:, b, 1], ALU.add).then_inc(*px.done(f"row1{t}"))
            pool.wait_ge(*px.at(f"row1{t}"))
            pool.tensor_tensor(rowf[:, b], rowf[:, b], k32["base"][:, b], ALU.add).then_inc(*px.done(f"row2{t}"))
            pool.wait_ge(*px.at(f"row2{t}"))
            pool.tensor_tensor(sprow[:, b], spt[:, b], rowf[:, b], ALU.subtract).then_inc(*px.done(f"sprow{t}"))
            pool.wait_ge(*px.at(f"sprow{t}"))
            pool.tensor_tensor(sprow[:, b], sprow[:, b], isp[:, b], ALU.mult).then_inc(*px.done(f"spd{t}"))
            pool.wait_ge(*px.at(f"spd{t}"))
            pool.tensor_tensor(rowf[:, b], rowf[:, b], sprow[:, b], ALU.add).then_inc(*px.done(f"row3{t}"))
            pool.wait_ge(*px.at(f"row3{t}"))
            pool.tensor_copy(idx2[:, b], rowf[:, b]).then_inc(*px.done(f"idx2{t}"))

        def rows_pool(pool, t):
            pool.wait_ge(*px.at(f"idx2{t}"))
            for b in range(t * UN * UB, (t + 1) * UN * UB):
                pool.indirect_dma_start(h[:, b * C:(b + 1) * C], None, rows,
                                        bass.IndirectOffsetOnAxis(ap=idx2[:, b:b + 1], axis=0)
                                        ).then_inc(rows_in[b // UB], 16)

        def setup_dve(dve):
            dve.wait_ge(ld["tok"], 16)
            dve.tensor_copy(tokf[:], tok[:]).then_inc(*ds.done("tokf"))
            dve.wait_ge(*ts_.at("tokt"))
            dve.tensor_copy(tokt[:], bank(0)[:, 0:B]).then_inc(*ds.done("tokt"))
            dve.tensor_scalar(idx1[:], bank(0)[:, 0:B], float(SPECIAL + NODES * NODES - 1), 0.0, ALU.min,
                              ALU.max).then_inc(*ds.done("idx1"))
            dve.tensor_scalar(spt[:], bank(0)[:, 0:B], float(ROWS), None, ALU.add).then_inc(*ds.done("spt"))
            dve.memset(m2[:], 0.0).then_inc(*ds.done("m2z"))
            dve.wait_ge(*ts_.at("m2"))
            dve.wait_ge(*ds.at("m2z"))
            for j, n in enumerate(("m2a", "m2b")):
                q = slice(C * j, C * j + C)
                dve.tensor_scalar(m2[q, q], bank(1)[q, 0:C], C ** -0.5, None, ALU.mult).then_inc(*ds.done(n))

            def low(name, lo, src, hi, scale=1.0):
                dve.scalar_tensor_tensor(lo, src, scale, hi, ALU.mult, ALU.subtract).then_inc(*ds.done(name))

            dve.wait_ge(ld["w1"], 16)
            dve.wait_ge(*as_.at("w1h"))
            low("w1l", w1l[:], w1s[:], w1h[:], WS)
            dve.wait_ge(*as_.at("gh"))
            low("gl", gl[:], k32["gate_w"], gh[:], WS)
            dve.tensor_scalar(mix1[:], k32["mix"], -1.0, 1.0, ALU.mult, ALU.add).then_inc(*ds.done("mix1"))
            dve.wait_ge(*ds.at("mix1"))
            for m in range(3):
                q = slice(C * m, C * m + C)
                dve.tensor_scalar(kvs[:, 0, q], k32["wkvr"][:, q], k32["mix"][:, m:m + 1], WS, ALU.mult, ALU.mult)
                last = dve.tensor_scalar(kvs[:, 1, q], k32["wkvr"][:, q], mix1[:, m:m + 1], WS, ALU.mult, ALU.mult)
            last.then_inc(*ds.done("kvs"))
            dve.wait_ge(*as_.at("kvh"))
            low("kvl", kvl[:], kvs[:], kvh[:])
            dve.tensor_tensor(wtoep[:], k32["toep"], k32["tri"], ALU.mult).then_inc(*ds.done("toep"))
            dve.tensor_scalar(qs[:], k32["wqkv"], k32["ln1"], WS, ALU.mult, ALU.mult).then_inc(*ds.done("qs"))
            dve.wait_ge(*as_.at("qh"))
            low("ql", ql_[:], qs[:], qh_[:])
            dve.tensor_scalar(rs_[:], k32["router"], k32["ln2"], WS, ALU.mult, ALU.mult).then_inc(*ds.done("rs"))
            dve.wait_ge(*as_.at("rh"))
            low("rl", rl[:], rs_[:], rh[:])
            dve.tensor_copy(identb[:], k32["ident"]).then_inc(*ds.done("identb"))
            dve.tensor_copy(mask_ts[:], mid(k32["mask_ts"], NH)).then_inc(*ds.done("mask_a"))
            dve.tensor_copy(mask_st[:], mid(k32["mask_st"], NH)).then_inc(*ds.done("mask_b"))
            for n, s, hi, lo in (("a1", a1s, a1h, a1l), ("a3", a3s, a3h, a3l)):
                dve.wait_ge(ld[n], 16)
                dve.tensor_scalar(s[:], s[:], k32["ln2"], WS, ALU.mult, ALU.mult).then_inc(*ds.done(n + "s"))
                dve.wait_ge(*as_.at(n + "h"))
                low(n + "l", lo[:], s[:], hi[:])
            dve.tensor_scalar(b1s[:], k32["b1"], WS, None, ALU.mult).then_inc(*ds.done("b1s"))
            dve.tensor_scalar(b2s[:], k32["b2"], WS, None, ALU.mult).then_inc(*ds.done("b2s"))

        def setup_act(act):
            act.wait_ge(ld["w1"], 16)
            act.activation(w1h[:], w1s[:], ACT.Copy, scale=WS).then_inc(*as_.done("w1h"))
            act.wait_ge(ld["c32"], 16)
            act.activation(gh[:], k32["gate_w"], ACT.Copy, scale=WS).then_inc(*as_.done("gh"))
            for n, src, hi, dep in (("kvh", kvs, kvh, "kvs"), ("qh", qs, qh_, "qs"), ("rh", rs_, rh, "rs"),
                                    ("a1h", a1s, a1h, "a1s"), ("a3h", a3s, a3h, "a3s")):
                act.wait_ge(*ds.at(dep))
                act.activation(hi[:], src[:], ACT.Copy).then_inc(*as_.done(n))

        def setup_pe(pe):
            pe.wait_ge(ld["c32"], 16)
            pe.wait_ge(*ds.at("tokf"))
            pe.transpose(bank(0)[:, 0:B], tokf[:], k32["ident"][0:B, 0:B]).then_inc(*ts_.done("tokt"))
            for j in range(2):
                last = pe.matmul(bank(1)[C * j:C * j + C, 0:C], k32["wq0"][0:C, :], k32["wk0"][0:C, :],
                                 start=True, stop=True)
            last.then_inc(*ts_.done("m2"))

        eps_ln, eps_rms = 1e-5, 1e-6
        xc = [sb(f"xc{u}", [P, UB * C]) for u in range(UN)]
        sq = [sb(f"sq{u}", [P, UB * C]) for u in range(UN)]
        xr = [sb(f"xr{u}", [P, UB * C]) for u in range(UN)]
        tmp = [sb(f"tmp{u}", [P, UB * C]) for u in range(UN)]
        xs = [sb(f"xs{u}", [P, UB, 2, C], FP16) for u in range(UN)]
        fT = [sb(f"fT{u}", [P, 2 * P]) for u in range(UN)]
        qT = [sb(f"qT{u}", [P, 2 * P]) for u in range(UN)]
        at = [sb(f"at{u}", [P, UB, P]) for u in range(UN)]
        atT = [sb(f"atT{u}", [P, UB * P]) for u in range(UN)]
        xt16 = [sb(f"xt16{u}", [P, UB, P], FP16) for u in range(UN)]
        mx = [sb(f"mx{u}", [P, UB]) for u in range(UN)]
        smx = [sb(f"smx{u}", [P, UB]) for u in range(UN)]
        GB = UN * UB
        lg, eq, pr, wr = (sb(n, [P, GB, E0]) for n in ("lg", "eq", "pr", "wr"))
        f1, f2 = sb("f1", [P, GB, E0]), sb("f2", [P, GB, E0])
        sm = sb("sm", [P, 12, GB])
        wpf = sb("wp", [P, GB * E0 * PARTS], BF16)
        wp0 = wpf[:].rearrange("p (b e k) -> p b e k", b=GB, e=E0)
        wrem = sb("wrem", [P, GB, E0])

        SUM, SS, VAR, Y, A_, B_, R = range(7)
        RSQRT = ["guess", "a", "s", "t", "z", "b", "c", "r"]

        class Norm:

            def __init__(self, name, xc, sq):
                self.st, self.xc, self.sq = sb(name, [P, 7, 2, UN * UB]), xc, sq

            def row(self, k):
                return self.st[:, k, 0, :]

            def part(self, k, u, second=0):
                return self.st[:, k, second, u * UB:(u + 1) * UB]

            def r(self, u, second=0):
                return self.part(R, u, second)

        norm_a = Norm("st_a", [b[:] for b in xc], [b[:] for b in sq])
        kc, ek, er, kv, rw = ([sb(f"{n}{u}", [P, UB * C]) for u in range(UN)] for n in ("kc", "ek", "er", "kv", "rw"))
        norm_r = Norm("st_r", [b[:] for b in kc], [b[:] for b in ek])

        def norm_names(p):
            return both(p + "sum", p + "xc", p + "ss") + [p + s for s in ["var"] + (["var2"] if p == "e" else []) + RSQRT]

        def rms_names(p):
            return both(p + "ss") + [p + s for s in ["var"] + RSQRT]

        def norm_centre(dve, D, i, p, w, src, ready):
            for u in range(UN):
                ready(u)
                dve.sem_inc(waited["dve"], 1)
                dve.tensor_reduce(w.part(SUM, u), src(u), AX.X, ALU.add).then_inc(*D.done(f"{p}sum{u}"))
            for u in range(UN):
                dve.wait_ge(*D.at(f"{p}sum{u}", i))
                dve.scalar_tensor_tensor(grp(w.xc[u]), bc(w.part(SUM, u), C), 1.0 / C, src(u), ALU.mult,
                                         ALU.subtract).then_inc(*D.done(f"{p}xc{u}"))

        def rms_dve(dve, D, A, i, p, w, eps, sign=1.0, rms_too=False):
            for u in range(UN):
                dve.wait_ge(*A.at(f"{p}sq{u}", i))
                dve.tensor_reduce(w.part(SS, u), grp(w.sq[u]), AX.X, ALU.add).then_inc(*D.done(f"{p}ss{u}"))
            dve.wait_ge(*D.at(f"{p}ss{UN - 1}", i))
            dve.tensor_scalar(w.row(VAR), w.row(SS), 1.0 / C, eps, ALU.mult, ALU.add).then_inc(*D.done(p + "var"))
            if rms_too:
                dve.tensor_scalar(w.st[:, VAR, 1, :], w.row(SS), (1.0 + eps_rms) / C, eps_rms * eps, ALU.mult,
                                  ALU.add).then_inc(*D.done(p + "var2"))
            dve.wait_ge(*D.at(p + ("var2" if rms_too else "var"), i))
            var, y, a, b, r = (w.st[:, k, :, :].rearrange("p w b -> p (w b)") if rms_too else w.row(k)
                               for k in (VAR, Y, A_, B_, R))
            k = 3.0 / 8.0
            dve.tensor_scalar(y.bitcast(I32), var.bitcast(I32), -0.5, float(0x5f3759df), ALU.mult,
                              ALU.add).then_inc(*D.done(p + "guess"))
            dve.wait_ge(*D.at(p + "guess", i))
            dve.tensor_tensor(a, y, y, ALU.mult).then_inc(*D.done(p + "a"))
            dve.wait_ge(*D.at(p + "a", i))
            dve.tensor_tensor(a, a, var, ALU.mult).then_inc(*D.done(p + "s"))
            dve.wait_ge(*D.at(p + "s", i))
            dve.scalar_tensor_tensor(b, a, -10.0 / 3.0, a, ALU.add, ALU.mult).then_inc(*D.done(p + "t"))
            dve.wait_ge(*D.at(p + "t", i))
            dve.scalar_tensor_tensor(y, b, 5.0, y, ALU.add, ALU.mult).then_inc(*D.done(p + "z"))
            dve.wait_ge(*D.at(p + "z", i))
            dve.tensor_tensor(a, y, y, ALU.mult).then_inc(*D.done(p + "b"))
            dve.wait_ge(*D.at(p + "b", i))
            dve.scalar_tensor_tensor(b, a, -0.5 * sign * k ** 3, var, ALU.mult, ALU.mult).then_inc(*D.done(p + "c"))
            dve.wait_ge(*D.at(p + "c", i))
            dve.scalar_tensor_tensor(r, b, 1.5 * sign * k, y, ALU.add, ALU.mult).then_inc(*D.done(p + "r"))

        def norm_act(act, D, A, i, p, w):
            for u in range(UN):
                act.wait_ge(*D.at(f"{p}xc{u}", i))
                act.activation(w.sq[u], w.xc[u], ACT.Square).then_inc(*A.done(f"{p}sq{u}"))

        def dyn(buf, i, u, n=UB * C):
            return buf[:, bass.ds(i * (UN * n) + u * n, n)]

        TOP = ["m1", "eq1", "pr1", "pm1", "f1", "l2", "m2", "eq2", "pr2", "pm2", "f2"]

        def top2_dve(dve, D, i, src, w, pri, n_e):
            def one(k, val, m, pm, f):
                dve.tensor_reduce(m, val, AX.X, ALU.max).then_inc(*D.done(f"m{k}"))
                dve.wait_ge(*D.at(f"m{k}", i))
                dve.tensor_tensor(eq[:, :, 0:n_e], val, bc(m, n_e), ALU.is_equal).then_inc(*D.done(f"eq{k}"))
                dve.wait_ge(*D.at(f"eq{k}", i))
                dve.tensor_tensor(pr[:, :, 0:n_e], eq[:, :, 0:n_e], mid(pri, GB), ALU.mult).then_inc(*D.done(f"pr{k}"))
                dve.wait_ge(*D.at(f"pr{k}", i))
                dve.tensor_reduce(pm, pr[:, :, 0:n_e], AX.X, ALU.max).then_inc(*D.done(f"pm{k}"))
                dve.wait_ge(*D.at(f"pm{k}", i))
                dve.tensor_tensor(f, pr[:, :, 0:n_e], bc(pm, n_e), ALU.is_equal).then_inc(*D.done(f"f{k}"))
                dve.wait_ge(*D.at(f"f{k}", i))

            one(1, src, w[:, 0, :], w[:, 1, :], f1[:, :, 0:n_e])
            dve.scalar_tensor_tensor(wr[:, :, 0:n_e], f1[:, :, 0:n_e], -3e38, src, ALU.mult, ALU.add).then_inc(*D.done("l2"))
            dve.wait_ge(*D.at("l2", i))
            one(2, wr[:, :, 0:n_e], w[:, 3, :], w[:, 4, :], f2[:, :, 0:n_e])

        SPLIT = ["wph", "wprem", "wpm", "wpl"]

        def parts_dve(dve, D, i, n_e):
            ww, rem = wr[:, :, 0:n_e], wrem[:, :, 0:n_e]
            w = [wpf[:, 0:GB * n_e * PARTS].rearrange("p (b e k) -> p b e k", b=GB, e=n_e)[:, :, :, k] for k in range(PARTS)]
            dve.tensor_copy(w[0], ww).then_inc(*D.done("wph"))
            dve.wait_ge(*D.at("wph", i))
            dve.tensor_tensor(rem, ww, w[0], ALU.subtract).then_inc(*D.done("wprem"))
            dve.wait_ge(*D.at("wprem", i))
            dve.tensor_copy(w[1], rem).then_inc(*D.done("wpm"))
            dve.wait_ge(*D.at("wpm", i))
            dve.tensor_tensor(w[2], rem, w[1], ALU.subtract).then_inc(*D.done("wpl"))

        d1a = Steps(sem("dve_attention0"), norm_names("a") + both("axn", "qT", "mxa", "mxb", "nmx", "atT", "rs", "yn", "h"),
                    loop=True)
        d1r = Steps(sem("dve_routing0"), norm_names("b") + both("bxn", "xl", "lg") + TOP
                    + ["dd", "den", "rec", "g2", "wa", "wb", "wc"] + SPLIT, loop=True)
        a1a = Steps(sem("act_attention0"), both("asq", "fT", "exp"), loop=True)
        a1r = Steps(sem("act_routing0"), both("bsq", "xh", "xt") + ["ed", "wt"], loop=True)
        t1a = Steps(sem("pe_attention0"), both("fT", "qT", "sim", "atT", "av"), loop=True)
        t1r = Steps(sem("pe_routing0"), both("xt", "lg") + ["wt"], loop=True)
        p1 = Steps(sem("pool1"), both("xt"), loop=True)

        def xtgrp(j, i, u):
            return xt[j][:, bass.ds(i * (UN * 2 * P) + u * 2 * P, 2 * P)]

        def alone(part):
            for _ in part:
                pass

        def interleaved(order, front, back):
            for k in order:
                next(front if k == "f" else back, None)

        def pipelined(eng, order, front, back):
            alone(front(eng, 0))
            with eng.Fori(0, IT - 1) as i:
                interleaved(order, front(eng, i + 1), back(eng, i))
            alone(back(eng, IT - 1))

        def attention0_dve(dve, i):
            D = d1a

            def rows(u):
                return grp(dyn(h, i, u))

            def rows_ready(u):
                dve.wait_ge(group_in, i * UN + u + 1)
                dve.wait_ge(*D.at("h1", i, 1))

            norm_centre(dve, D, i, "a", norm_a, rows, rows_ready)
            yield
            rms_dve(dve, D, a1a, i, "a", norm_a, eps_ln, -1.0)
            for u in range(UN):
                dve.wait_ge(*D.at("ar", i))
                dve.wait_ge(*t1a.at(f"av{u}", i, 1))
                dve.tensor_tensor(grp(xr[u][:]), grp(xc[u][:]), bc(norm_a.r(u), C), ALU.mult).then_inc(*D.done(f"axn{u}"))
            yield
            for u in range(UN):
                dve.wait_ge(*t1a.at(f"qT{u}", i))
                dve.tensor_copy(qT[u][:], bank(2 * u)[:, 256:512]).then_inc(*D.done(f"qT{u}"))
            yield
            for j, n in enumerate(("mxa", "mxb")):
                for u in range(UN):
                    dve.wait_ge(*t1a.at(f"sim{u}", i))
                    dve.tensor_reduce(mx[u][:].rearrange("p (q j) -> p j q", j=2)[:, j, :],
                                      bank(2 * u + j)[:, 0:256].rearrange("p (q s) -> p q s", q=2), AX.X,
                                      ALU.max).then_inc(*D.done(f"{n}{u}"))
            for u in range(UN):
                dve.wait_ge(*D.at(f"mxb{u}", i))
                dve.tensor_scalar(mx[u][:], mx[u][:], -1.0, None, ALU.mult).then_inc(*D.done(f"nmx{u}"))
            yield
            for u in range(UN):
                dve.wait_ge(*t1a.at(f"atT{u}", i))
                dve.tensor_copy(atT[u][:], bank(2 * u)).then_inc(*D.done(f"atT{u}"))
            yield
            for u in range(UN):
                dve.wait_ge(*a1a.at(f"exp{u}", i))
                dve.reciprocal(smx[u][:], smx[u][:]).then_inc(*D.done(f"rs{u}"))
            for u in range(UN):
                dve.wait_ge(*t1a.at(f"av{u}", i))
                dve.wait_ge(*D.at(f"rs{u}", i))
                dve.tensor_tensor(grp(tmp[u][:]), grp(bank(2 * u + 1)[:, 0:256]), bc(smx[u][:], C), ALU.mult).then_inc(*D.done(f"yn{u}"))
            for u in range(UN):
                dve.wait_ge(*D.at(f"yn{u}", i))
                dve.tensor_tensor(dyn(h, i, u), dyn(h, i, u), tmp[u][:], ALU.add).then_inc(*D.done(f"h{u}"))

        def routing0_dve(dve, i):
            D = d1r

            def rows(u):
                return grp(dyn(h, i, u))

            norm_centre(dve, D, i, "b", norm_r, rows, lambda u: dve.wait_ge(*d1a.at(f"h{u}", i)))
            yield
            rms_dve(dve, D, a1r, i, "b", norm_r, eps_ln, -1.0)
            for u in range(UN):
                dve.wait_ge(*D.at("br", i))
                dve.tensor_tensor(grp(dyn(x, i, u)), grp(norm_r.xc[u]), bc(norm_r.r(u), C), ALU.mult).then_inc(*D.done(f"bxn{u}"))
            yield
            for u in range(UN):
                dve.wait_ge(*a1r.at(f"xh{u}", i))
                dve.tensor_tensor(xs[u][:, :, 1, :], grp(dyn(x, i, u)), xs[u][:, :, 0, :], ALU.subtract).then_inc(*D.done(f"xl{u}"))
            yield
            for u in range(UN):
                dve.wait_ge(*t1r.at(f"lg{u}", i))
                dve.scalar_tensor_tensor(lg[:, u * UB:(u + 1) * UB, :], grp(bank(6 + u)[:, 0:UB * E0], E0), 1.0 / WS,
                                         mid(k32["gate_b"], UB), ALU.mult, ALU.add).then_inc(*D.done(f"lg{u}"))
            dve.wait_ge(*D.at("lg1", i))
            top2_dve(dve, D, i, lg[:], sm, k32["pri0"], E0)
            yield
            dve.tensor_tensor(sm[:, 5, :], sm[:, 3, :], sm[:, 0, :], ALU.subtract).then_inc(*D.done("dd"))
            yield
            dve.wait_ge(*a1r.at("ed", i))
            dve.tensor_scalar(sm[:, 7, :], sm[:, 6, :], 1.0, None, ALU.add).then_inc(*D.done("den"))
            dve.wait_ge(*D.at("den", i))
            dve.reciprocal(sm[:, 8, :], sm[:, 7, :]).then_inc(*D.done("rec"))
            dve.wait_ge(*D.at("rec", i))
            dve.tensor_tensor(sm[:, 9, :], sm[:, 8, :], sm[:, 6, :], ALU.mult).then_inc(*D.done("g2"))
            dve.wait_ge(*D.at("g2", i))
            dve.tensor_tensor(f1[:], f1[:], bc(sm[:, 8, :], E0), ALU.mult).then_inc(*D.done("wa"))
            dve.tensor_tensor(f2[:], f2[:], bc(sm[:, 9, :], E0), ALU.mult).then_inc(*D.done("wb"))
            dve.wait_ge(*D.at("wb", i))
            dve.tensor_tensor(wr[:], f1[:], f2[:], ALU.add).then_inc(*D.done("wc"))
            dve.wait_ge(*D.at("wc", i))
            yield
            dve.wait_ge(*t1r.at("wt", i, 1))
            parts_dve(dve, D, i, E0)

        def attention0_act(act, i):
            A = a1a

            norm_act(act, d1a, A, i, "a", norm_a)
            yield
            for u in range(UN):
                act.wait_ge(*t1a.at(f"fT{u}", i))
                act.activation(fT[u][:], bank(2 * u)[:, 0:256], ACT.Copy).then_inc(*A.done(f"fT{u}"))
            yield
            yield
            for u in range(UN):
                act.wait_ge(*d1a.at(f"nmx{u}", i))
                for k in range(UB):
                    last = act.activation(at[u][:, k, :], bank(2 * u + k % 2)[:, k // 2 * P:k // 2 * P + P],
                                          ACT.Exp, bias=mx[u][:, k:k + 1], accum_out=smx[u][:, k:k + 1])
                last.then_inc(*A.done(f"exp{u}"))
            yield
            yield

        def routing0_act(act, i):
            A = a1r

            norm_act(act, d1r, A, i, "b", norm_r)
            yield
            for u in range(UN):
                act.wait_ge(*d1r.at(f"bxn{u}", i))
                act.activation(xs[u][:, :, 0, :], grp(dyn(x, i, u)), ACT.Copy).then_inc(*A.done(f"xh{u}"))
            yield
            for u in range(UN):
                act.wait_ge(*t1r.at(f"xt{u}", i))
                act.wait_ge(*p1.at(f"xt{u}", i, 1))
                act.activation(xt16[u][:].rearrange("p b t -> p (b t)"), bank(4 + u, FP16)[:, 0:512],
                               ACT.Copy).then_inc(*A.done(f"xt{u}"))
            yield
            yield
            act.wait_ge(*d1r.at("dd", i))
            act.activation(sm[:, 6, :], sm[:, 5, :], ACT.Exp).then_inc(*A.done("ed"))
            yield
            yield
            act.wait_ge(*t1r.at("wt", i))
            act.activation(wt[:, bass.ds(i * 512, 512)], bank(4, BF16)[0:2 * E0 * PARTS, 0:512],
                           ACT.Copy).then_inc(*A.done("wt"))

        def tokens_pool(pool, i):
            for u in range(UN):
                pool.wait_ge(*a1r.at(f"xt{u}", i))
                for j in range(2):
                    last = pool.tensor_copy(xtgrp(j, i, u).rearrange("p (q t) -> p q t", q=2),
                                            xt16[u][:].rearrange("p (q j) t -> p j q t", j=2)[:, j])
                last.then_inc(*p1.done(f"xt{u}"))

        def loop1_pool(pool):
            with pool.Fori(0, IT - 1) as i:
                tokens_pool(pool, i + 1)

        def attention0_pe(pe, i):
            T = t1a

            yield
            for u in range(UN):
                pe.wait_ge(*d1a.at(f"axn{u}", i))
                for q in range(2):
                    last = pe.transpose(bank(2 * u)[:, q * P:q * P + P], xr[u][:, q * P:q * P + P], k32["ident"])
                last.then_inc(*T.done(f"fT{u}"))
            for u in range(UN):
                pe.wait_ge(*a1a.at(f"fT{u}", i))
                pe.matmul(bank(2 * u)[:, 256:512], m2[:], fT[u][:], start=True, stop=True).then_inc(*T.done(f"qT{u}"))
            yield
            for u in range(UN):
                pe.wait_ge(*d1a.at(f"qT{u}", i))
                for q in range(2):
                    for j in range(2):
                        r, c = slice(C * j, C * j + C), slice(q * P, q * P + P)
                        last = pe.matmul(bank(2 * u + j)[:, c], qT[u][r, c], fT[u][r, c], start=True, stop=True)
                last.then_inc(*T.done(f"sim{u}"))
            yield
            yield
            for u in range(UN):
                pe.wait_ge(*a1a.at(f"exp{u}", i))
                for k in range(UB):
                    last = pe.transpose(bank(2 * u)[:, k * P:k * P + P], at[u][:, k, :], k32["ident"])
                last.then_inc(*T.done(f"atT{u}"))
            for u in range(UN):
                pe.wait_ge(*d1a.at(f"atT{u}", i))
                for k in range(UB):
                    last = pe.matmul(bank(2 * u + 1)[:, k * C:k * C + C], atT[u][:, k * P:k * P + P], xr[u][:, k * C:k * C + C],
                                     start=True, stop=True)
                last.then_inc(*T.done(f"av{u}"))
            yield

        def routing0_pe(pe, i):
            T = t1r

            yield
            yield
            for u in range(UN):
                pe.wait_ge(*d1r.at(f"xl{u}", i))
                for k in range(UB):
                    last = pe.transpose(bank(4 + u, FP16)[:, k * P:k * P + P], xs[u][:, k].rearrange("p a c -> p (a c)"),
                                        k16["ident16"])
                last.then_inc(*T.done(f"xt{u}"))
            for u in range(UN):
                pe.wait_ge(*a1r.at(f"xt{u}", i))
                for k in range(UB):
                    for w in (gh, gl):
                        last = pe.matmul(bank(6 + u)[:, k * E0:k * E0 + E0], xt16[u][:, k, :], w[:], start=w is gh,
                                         stop=w is gl)
                last.then_inc(*T.done(f"lg{u}"))
            yield
            yield
            yield
            yield
            pe.wait_ge(*d1r.at("wpl", i))
            for q in range(GB // 2):
                last = pe.transpose(bank(4, BF16)[0:2 * E0 * PARTS, q * P:q * P + P],
                                    wp0[:, 2 * q:2 * q + 2].rearrange("p b e k -> p (b e k)"), identb[:])
            last.then_inc(*T.done("wt"))

        ORDER0 = "fbfbfbfbbfbbf"

        def loop1_dve(dve):
            d1a.prime(dve)
            d1r.prime(dve)
            pipelined(dve, ORDER0, attention0_dve, routing0_dve)

        def loop1_act(act):
            a1a.prime(act)
            a1r.prime(act)
            pipelined(act, ORDER0, attention0_act, routing0_act)

        def loop1_pe(pe):
            t1a.prime(pe)
            t1r.prime(pe)
            pipelined(pe, ORDER0, attention0_pe, routing0_pe)

        N = 512
        hidden = sb("hidden", [P, 4 * N])
        hid = [[hidden[:, (2 * k + j) * N:(2 * k + j + 1) * N] for j in range(2)] for k in range(2)]
        wbs = [sb(f"wbs{k}", [P, N]) for k in range(2)]
        yw = [sb(f"yw{k}", [P, N]) for k in range(2)]
        lag2 = [(e, e - 1) for e in range(E0 + 1)]
        t2 = Steps(sem("pe2"), sum([([f"wb{e}", f"z0{e}", f"z1{e}"] if e < E0 else []) + ([f"y{f}"] if f >= 0 else [])
                                    for e, f in lag2], []), loop=True)
        a2 = Steps(sem("act2"), sum([[f"wb{e}", f"hid{e}"] for e in range(E0)], []), loop=True)
        d2 = Steps(sem("dve2"), sum([([f"hid{e}"] if e < E0 else []) + ([f"yw{f}"] if f >= 0 else [])
                                     for e, f in lag2], []), loop=True)
        p2 = Steps(sem("pool2"), [f"acc{e}" for e in range(E0)], loop=True)

        def before(S, name, e, back, i, n):
            return S.at(f"{name}{e - back}", i) if e >= back else S.at(f"{name}{e - back + n}", i, 1)

        def loop2_pe(pe):
            T = t2
            T.prime(pe)
            pe.wait_ge(*p1.at("xt1", IT - 1))
            pe.wait_ge(*a1r.at("wt", IT - 1))
            pe.wait_ge(ld["w2"], 16)
            with pe.Fori(0, IT) as i:
                for e, f in lag2:
                    if e < E0:
                        pe.wait_ge(*before(a2, "wb", e, 2, i, E0))
                        pe.matmul(bank(e % 2), k16["sel0"][0:2 * E0 * PARTS, e * P:(e + 1) * P], wt[:, bass.ts(i, N)],
                                  start=True, stop=True).then_inc(*T.done(f"wb{e}"))
                        for j in range(2):
                            pe.wait_ge(*before(d2 if j else a2, "hid", e, 2, i, E0))
                            for w in (w1h, w1l):
                                last = pe.matmul(bank(2 + 2 * (e % 2) + j), w[:, e * F0:(e + 1) * F0], xt[j][:, bass.ts(i, N)],
                                                 start=w is w1h, stop=w is w1l)
                            last.then_inc(*T.done(f"z{j}{e}"))
                    if f >= 0:
                        pe.wait_ge(*a2.at(f"hid{f}", i))
                        pe.wait_ge(*d2.at(f"hid{f}", i))
                        for j in range(2):
                            last = pe.matmul(bank(6 + f % 2)[C * j:C * j + C, :], w2s[:, f * C:(f + 1) * C], hid[f % 2][j][:],
                                             start=True, stop=True)
                        last.then_inc(*T.done(f"y{f}"))

        def loop2_act(act):
            A = a2
            A.prime(act)
            with act.Fori(0, IT) as i:
                for e in range(E0):
                    act.wait_ge(*t2.at(f"wb{e}", i))
                    act.wait_ge(*before(d2, "yw", e, 2, i, E0))
                    act.activation(wbs[e % 2][:], bank(e % 2), ACT.Copy).then_inc(*A.done(f"wb{e}"))
                    act.wait_ge(*t2.at(f"z0{e}", i))
                    act.activation(hid[e % 2][0][:], bank(2 + 2 * (e % 2)), ACT.Relu,
                                   bias=b1s[:, e:e + 1]).then_inc(*A.done(f"hid{e}"))

        def loop2_dve(dve):
            D = d2
            D.prime(dve)
            with dve.Fori(0, IT) as i:
                for e, f in lag2:
                    if e < E0:
                        dve.wait_ge(*t2.at(f"z1{e}", i))
                        dve.tensor_scalar(hid[e % 2][1][:], bank(3 + 2 * (e % 2)), b1s[:, e:e + 1], 0.0, ALU.add,
                                          ALU.max).then_inc(*D.done(f"hid{e}"))
                    if f >= 0:
                        dve.wait_ge(*t2.at(f"y{f}", i))
                        dve.wait_ge(*a2.at(f"wb{f}", i))
                        dve.wait_ge(*before(p2, "acc", f, 2, i, E0))
                        dve.scalar_tensor_tensor(yw[f % 2][:], bank(6 + f % 2), b2s[:, f:f + 1], wbs[f % 2][:], ALU.add,
                                                 ALU.mult).then_inc(*D.done(f"yw{f}"))

        accs = sb("accs", [P, N])

        def moe_pool(pool, S, D, ne):
            S.prime(pool)
            with pool.Fori(0, IT) as i:
                for e in range(ne):
                    pool.wait_ge(*D.at(f"yw{e}", i))
                    pool.wait_ge(*before(S, "acc", e, 1, i, ne))
                    if e == 0:
                        pool.sem_inc(waited["pool"], 1)
                        pool.tensor_copy(accs[:], yw[0][:]).then_inc(*S.done("acc0"))
                    elif e < ne - 1:
                        pool.tensor_tensor(accs[:], accs[:], yw[e % 2][:], ALU.add).then_inc(*S.done(f"acc{e}"))
                    else:
                        pool.sem_inc(waited["pool"], 1)
                        pool.tensor_tensor(acc[:, bass.ts(i, N)], accs[:], yw[e % 2][:], ALU.add).then_inc(*S.done(f"acc{e}"))

        ar = qT
        xp = [sb(f"xp{u}", [P, UB, L + 1], FP16) for u in range(UN)]
        rT = [sb(f"rT{u}", [P, 2 * P]) for u in range(UN)]
        ra, rb = ([sb(f"{n}{u}", [P, UB, 96]) for u in range(UN)] for n in ("ra", "rb"))
        qr = [sb(f"qr{u}", [P, UB * NH, HD]) for u in range(UN)]
        kr = [sb(f"kr{u}", [P, UB * NKV, HD]) for u in range(UN)]
        qst = [sb(f"qst{u}", [P, UB * NH, 2, 2, HD], FP16) for u in range(UN)]
        kst = [sb(f"kst{u}", [P, UB * NKV, 2, 2, 2, HD], FP16) for u in range(UN)]
        va = [sb(f"va{u}", [P, UB, NKV, 32]) for u in range(UN)]
        qb = [sb(f"qb{u}", [P, UB * NKV, 2, P], FP16) for u in range(UN)]
        kd = [sb(f"kd{u}", [P, UB * NKV * P], FP16) for u in range(UN)]
        mh = [sb(f"mh{u}", [P, UB * NH]) for u in range(UN)]
        mrem = [sb(f"mrem{u}", [P, UB * NH]) for u in range(UN)]
        mp = [sb(f"mp{u}", [P, 2, UB * NH, PARTS], BF16) for u in range(UN)]
        mT = [sb(f"mT{u}", [UB * NH * PARTS, P], BF16) for u in range(UN)]
        ex = [grp(w1s[:], NH * P), grp(hidden[:], NH * P)]
        ot = atT
        quarters = [b[:].bitcast(F32)[:, k * UB * C:(k + 1) * UB * C] for b in (w1h, w1l) for k in range(4)]
        tmp2, xc2, sq2, rT2 = (quarters[2 * k:2 * k + 2] for k in range(4))
        norm_b = Norm("st_b", xc2, sq2)
        xs2 = [fT[u][:].bitcast(FP16).rearrange("p (b a c) -> p b a c", b=UB, a=2) for u in range(UN)]
        yt = [at[u][:].rearrange("p b t -> p (b t)")[:, 0:UB * C] for u in range(UN)]
        rc = [sb(f"rc{u}", [P, UB * NH]) for u in range(UN)]

        dm = Steps(sem("dve_mixing"), both("y") + norm_names("c") + both("cx", "h") + norm_names("d")
                   + both("dxn", "dl", "kc", "kv", "den", "rden", "rw", "ho"), loop=True)
        am = Steps(sem("act_mixing"), both("csq", "dsq", "dh", "xp", "er", "ek", "rT"), loop=True)
        tm = Steps(sem("pe_mixing"), both("aT", "dx", "kvr", "sum", "rT", "wo"), loop=True)
        qm = Steps(sem("pool_mixing"), both("ar", "hb", "cg"), loop=True)
        da = Steps(sem("dve_attention"), norm_names("e")
                   + both("hn", "fl", "ra", "rb", "qr", "kr", "ql", "kl", "qb", "kd", "mx0", "mx1", "mx2", "mx3", "mh",
                          "mrem", "mm", "ml", "rc", "yt", "xm") + rms_names("g") + both("gf", "gl", "lg")
                   + ["sx", "ls", "se", "rse", "pb"] + TOP + ["d0", "d1", "d2", "ff", "fp", "wc"] + SPLIT, loop=True)
        aa = Steps(sem("act_attention"), both("esq", "fh", "xt", "va", "qh", "kh", "qb", "mT", "ex0", "ex1", "ex2", "ex3", "ot",
                                              "yT", "gsq", "gh", "xt3") + ["es", "wt"], loop=True)
        ta = Steps(sem("pe_attention"), both("fx", "qkv", "qT", "s0", "s1", "s2", "s3", "mT", "t0", "t1", "t2", "t3", "oT", "o",
                                             "yT", "wo1", "gx", "lg") + ["wt"], loop=True)
        qa = Steps(sem("pool_attention"), both("ex", "xt"), loop=True)
        p3 = Steps(sem("pool3"), ["z0", "z1", "z2", "z3", "z4", "z5"], loop=False)

        def mixing_dve(dve, i):
            D = dm

            def state(u):
                return grp(dyn(h, i, u))

            def kvr(u, q, m):
                return bank(2 * u + q)[:, 0:2 * KVR].rearrange("p (b n) -> p b n", b=2)[:, :, m * C:(m + 1) * C]

            for u in range(UN):
                dve.wait_ge(*tm.at(f"aT{u}", i))
                dve.wait_ge(*D.at("ho1", i, 1))
                dve.scalar_tensor_tensor(tmp[u][:], bank(2 * u)[:, 0:256], 1.0 / WS, dyn(x, i, u), ALU.mult,
                                         ALU.add).then_inc(*D.done(f"y{u}"))
            norm_centre(dve, D, i, "c", norm_a, lambda u: grp(tmp[u][:]), lambda u: dve.wait_ge(*D.at(f"y{u}", i)))
            yield
            rms_dve(dve, D, am, i, "c", norm_a, eps_ln, -1.0)
            for u in range(UN):
                dve.wait_ge(*D.at("cr", i))
                dve.wait_ge(*qm.at(f"cg{u}", i))
                dve.tensor_tensor(grp(tmp[u][:]), grp(tmp[u][:]), bc(norm_a.r(u), C), ALU.mult).then_inc(*D.done(f"cx{u}"))
            for u in range(UN):
                dve.wait_ge(*D.at(f"cx{u}", i))
                dve.tensor_tensor(dyn(h, i, u), dyn(h, i, u), tmp[u][:], ALU.add).then_inc(*D.done(f"h{u}"))
            yield
            norm_centre(dve, D, i, "d", norm_a, state, lambda u: dve.wait_ge(*D.at(f"h{u}", i)))
            yield
            rms_dve(dve, D, am, i, "d", norm_a, eps_ln, -1.0)
            for u in range(UN):
                dve.wait_ge(*D.at("dr", i))
                dve.tensor_tensor(grp(xr[u][:]), grp(xc[u][:]), bc(norm_a.r(u), C), ALU.mult).then_inc(*D.done(f"dxn{u}"))
            yield
            for u in range(UN):
                dve.wait_ge(*am.at(f"dh{u}", i))
                dve.tensor_tensor(xs[u][:, :, 1, :], grp(xr[u][:]), xs[u][:, :, 0, :], ALU.subtract).then_inc(*D.done(f"dl{u}"))
            yield
            for u in range(UN):
                dve.wait_ge(*tm.at(f"kvr{u}", i))
                for q in range(2):
                    last = dve.tensor_scalar(grp(kc[u][:, q * P:(q + 1) * P]), kvr(u, q, 0), 30.0 * WS, -60.0 * WS, ALU.min,
                                             ALU.max)
                last.then_inc(*D.done(f"kc{u}"))
            yield
            for u in range(UN):
                dve.wait_ge(*am.at(f"ek{u}", i))
                for q in range(2):
                    last = dve.tensor_tensor(grp(kv[u][:, q * P:(q + 1) * P]), kvr(u, q, 1), grp(ek[u][:, q * P:(q + 1) * P]),
                                             ALU.mult)
                last.then_inc(*D.done(f"kv{u}"))
            yield
            for u in range(UN):
                dve.wait_ge(*tm.at(f"sum{u}", i))
                dve.scalar_tensor_tensor(er[u][:], er[u][:], 1.0, bank(2 * u)[:, 0:256], ALU.add,
                                         ALU.mult).then_inc(*D.done(f"den{u}"))
            for u in range(UN):
                dve.wait_ge(*D.at(f"den{u}", i))
                dve.reciprocal(er[u][:], er[u][:]).then_inc(*D.done(f"rden{u}"))
            yield
            for u in range(UN):
                dve.wait_ge(*D.at(f"rden{u}", i))
                dve.tensor_tensor(rw[u][:], bank(2 * u)[:, 256:512], er[u][:], ALU.mult).then_inc(*D.done(f"rw{u}"))
            yield
            for u in range(UN):
                dve.wait_ge(*tm.at(f"wo{u}", i))
                dve.scalar_tensor_tensor(dyn(h, i, u), bank(2 * u + 1)[:, 256:512], 1.0 / WS, dyn(h, i, u), ALU.mult,
                                         ALU.add).then_inc(*D.done(f"ho{u}"))

        def attention_dve(dve, i):
            D = da

            def state(u):
                return grp(dyn(h, i, u))

            def qkv(u):
                return bank(5 + 2 * u).rearrange("p (b n) -> p b n", b=UB)

            def halves(ap):
                return ap.rearrange("p b (g s d) -> p b g s d", g=NH + NKV, s=2)

            def table(name, s):
                return k32[name].rearrange("p (g s d) -> p g s d", g=NH + NKV, s=2)[:, :, s, :].unsqueeze(1) \
                    .to_broadcast([P, UB, NH + NKV, HD // 2])

            def heads(u):
                return bank(5 + 2 * u).rearrange("p (g n) -> p g n", n=32)

            l8, w8 = lg[:, :, 0:E1], wr[:, :, 0:E1]

            norm_centre(dve, D, i, "e", norm_b, state, lambda u: dve.wait_ge(*dm.at(f"ho{u}", i)))
            yield
            rms_dve(dve, D, aa, i, "e", norm_b, eps_ln, -1.0, rms_too=True)
            for u in range(UN):
                dve.wait_ge(*D.at("er", i))
                dve.tensor_tensor(grp(tmp2[u]), grp(norm_b.xc[u]), bc(norm_b.r(u, 1), C), ALU.mult).then_inc(*D.done(f"hn{u}"))
            yield
            for u in range(UN):
                dve.wait_ge(*aa.at(f"fh{u}", i))
                dve.tensor_tensor(xs2[u][:, :, 1, :], grp(tmp2[u]), xs2[u][:, :, 0, :], ALU.subtract).then_inc(*D.done(f"fl{u}"))
            yield
            for u in range(UN):
                dve.wait_ge(*aa.at(f"va{u}", i))
                dve.tensor_tensor(ra[u][:], qkv(u)[:, :, 0:96], mid(k32["cos"], UB), ALU.mult).then_inc(*D.done(f"ra{u}"))
            for u in range(UN):
                for s in range(2):
                    last = dve.tensor_tensor(halves(rb[u][:])[:, :, :, s, :], halves(qkv(u)[:, :, 0:96])[:, :, :, 1 - s, :],
                                             table("sin", s), ALU.mult)
                last.then_inc(*D.done(f"rb{u}"))
            yield
            for u in range(UN):
                dve.wait_ge(*D.at(f"rb{u}", i))
                dve.tensor_tensor(qr[u][:].rearrange("p (b g) d -> p b (g d)", b=UB), ra[u][:, :, 0:C], rb[u][:, :, 0:C],
                                  ALU.add).then_inc(*D.done(f"qr{u}"))
            for u in range(UN):
                dve.tensor_tensor(kr[u][:].rearrange("p (b g) d -> p b (g d)", b=UB), ra[u][:, :, C:96], rb[u][:, :, C:96],
                                  ALU.add).then_inc(*D.done(f"kr{u}"))
            yield
            for u in range(UN):
                dve.wait_ge(*aa.at(f"qh{u}", i))
                q2 = qr[u][:].unsqueeze(2).to_broadcast([P, UB * NH, 2, HD])
                dve.tensor_tensor(qst[u][:, :, :, 1, :], q2, qst[u][:, :, :, 0, :], ALU.subtract).then_inc(*D.done(f"ql{u}"))
            for u in range(UN):
                dve.wait_ge(*aa.at(f"kh{u}", i))
                k2 = kr[u][:].unsqueeze(2).to_broadcast([P, UB * NKV, 2, HD])
                for s in range(2):
                    last = dve.tensor_tensor(kst[u][:, :, s, 1, :, :], k2, kst[u][:, :, s, 0, :, :], ALU.subtract)
                last.then_inc(*D.done(f"kl{u}"))
            yield
            for u in range(UN):
                dve.wait_ge(*ta.at(f"qT{u}", i))
                dve.tensor_copy(qb[u][C:P, :, 1, :], bank(4 + 2 * u, FP16)[C:P, :].rearrange("p (g t) -> p g t", t=P)
                                ).then_inc(*D.done(f"qb{u}"))
            for u in range(UN):
                dve.tensor_copy(kd[u][:], bank(5 + 2 * u, FP16)).then_inc(*D.done(f"kd{u}"))
            yield
            for k in range(0, 2):
                for u in range(UN):
                    dve.wait_ge(*ta.at(f"s{k}{u}", i))
                    dve.tensor_reduce(mh[u][:, k * NH:(k + 1) * NH], grp(bank(4 + 2 * u + k % 2), P), AX.X,
                                      ALU.max).then_inc(*D.done(f"mx{k}{u}"))
            yield
            for k in range(2, 4):
                for u in range(UN):
                    dve.wait_ge(*ta.at(f"s{k}{u}", i))
                    dve.tensor_reduce(mh[u][:, k * NH:(k + 1) * NH], grp(bank(4 + 2 * u + k % 2), P), AX.X,
                                      ALU.max).then_inc(*D.done(f"mx{k}{u}"))
            yield
            for u in range(UN):
                dve.wait_ge(*D.at(f"mx3{u}", i))
                dve.tensor_scalar(mp[u][:, 0, :, 0], mh[u][:], -1.0, None, ALU.mult).then_inc(*D.done(f"mh{u}"))
            for u in range(UN):
                dve.wait_ge(*D.at(f"mh{u}", i))
                dve.scalar_tensor_tensor(mrem[u][:], mh[u][:], -1.0, mp[u][:, 0, :, 0], ALU.mult,
                                         ALU.subtract).then_inc(*D.done(f"mrem{u}"))
            for u in range(UN):
                dve.wait_ge(*D.at(f"mrem{u}", i))
                dve.tensor_copy(mp[u][:, 0, :, 1], mrem[u][:]).then_inc(*D.done(f"mm{u}"))
            for u in range(UN):
                dve.wait_ge(*D.at(f"mm{u}", i))
                dve.tensor_tensor(mp[u][:, 0, :, 2], mrem[u][:], mp[u][:, 0, :, 1], ALU.subtract).then_inc(*D.done(f"ml{u}"))
            yield
            yield
            yield
            for u in range(UN):
                dve.wait_ge(*ta.at(f"o{u}", i))
                dve.reciprocal(rc[u][:], heads(u)[:, :, HD]).then_inc(*D.done(f"rc{u}"))
            for u in range(UN):
                dve.wait_ge(*D.at(f"rc{u}", i))
                dve.tensor_tensor(grp(yt[u], HD), heads(u)[:, :, 0:HD], bc(rc[u][:], HD), ALU.mult).then_inc(*D.done(f"yt{u}"))
            yield
            for u in range(UN):
                dve.wait_ge(*ta.at(f"wo1{u}", i))
                dve.wait_ge(*qa.at(f"ex{u}", i))
                dve.tensor_tensor(dyn(x, i, u), bank(4 + 2 * u)[:, 256:512], dyn(x, i, u), ALU.add).then_inc(*D.done(f"xm{u}"))
            yield
            rms_dve(dve, D, aa, i, "g", norm_b, eps_rms)
            for u in range(UN):
                dve.wait_ge(*D.at("gr", i))
                dve.tensor_tensor(grp(tmp2[u]), grp(dyn(x, i, u)), bc(norm_b.r(u), C), ALU.mult).then_inc(*D.done(f"gf{u}"))
            yield
            for u in range(UN):
                dve.wait_ge(*aa.at(f"gh{u}", i))
                dve.tensor_tensor(xs2[u][:, :, 1, :], grp(tmp2[u]), xs2[u][:, :, 0, :], ALU.subtract).then_inc(*D.done(f"gl{u}"))
            yield
            for u in range(UN):
                dve.wait_ge(*ta.at(f"lg{u}", i))
                dve.tensor_scalar(l8[:, u * UB:(u + 1) * UB, :], grp(bank(4 + 2 * u)[:, 0:UB * E1], E1), 1.0 / WS, None,
                                  ALU.mult).then_inc(*D.done(f"lg{u}"))
            dve.wait_ge(*D.at("lg1", i))
            dve.tensor_reduce(sm[:, 5, :], l8, AX.X, ALU.max).then_inc(*D.done("sx"))
            dve.wait_ge(*D.at("sx", i))
            dve.tensor_tensor(l8, l8, bc(sm[:, 5, :], E1), ALU.subtract).then_inc(*D.done("ls"))
            dve.wait_ge(*aa.at("es", i))
            dve.tensor_reduce(sm[:, 6, :], w8, AX.X, ALU.add).then_inc(*D.done("se"))
            dve.wait_ge(*D.at("se", i))
            dve.reciprocal(sm[:, 7, :], sm[:, 6, :]).then_inc(*D.done("rse"))
            dve.wait_ge(*D.at("rse", i))
            dve.tensor_tensor(l8, w8, bc(sm[:, 7, :], E1), ALU.mult).then_inc(*D.done("pb"))
            dve.wait_ge(*D.at("pb", i))
            yield
            top2_dve(dve, D, i, l8, sm, k32["pri1"], E1)
            dve.tensor_tensor(sm[:, 8, :], sm[:, 0, :], sm[:, 3, :], ALU.add).then_inc(*D.done("d0"))
            dve.wait_ge(*D.at("d0", i))
            dve.tensor_scalar(sm[:, 9, :], sm[:, 8, :], 1e-9, None, ALU.add).then_inc(*D.done("d1"))
            dve.wait_ge(*D.at("d1", i))
            dve.reciprocal(sm[:, 10, :], sm[:, 9, :]).then_inc(*D.done("d2"))
            ff = f1[:, :, 0:E1]
            dve.tensor_tensor(ff, ff, f2[:, :, 0:E1], ALU.add).then_inc(*D.done("ff"))
            dve.wait_ge(*D.at("ff", i))
            dve.tensor_tensor(ff, ff, l8, ALU.mult).then_inc(*D.done("fp"))
            dve.wait_ge(*D.at("fp", i))
            dve.tensor_tensor(w8, ff, bc(sm[:, 10, :], E1), ALU.mult).then_inc(*D.done("wc"))
            dve.wait_ge(*D.at("wc", i))
            yield
            dve.wait_ge(*ta.at("wt", i, 1))
            parts_dve(dve, D, i, E1)

        def mixing_act(act, i):
            A = am

            norm_act(act, dm, A, i, "c", norm_a)
            yield
            yield
            norm_act(act, dm, A, i, "d", norm_a)
            yield
            for u in range(UN):
                act.wait_ge(*dm.at(f"dxn{u}", i))
                act.activation(xs[u][:, :, 0, :], grp(xr[u][:]), ACT.Copy).then_inc(*A.done(f"dh{u}"))
            yield
            for u in range(UN):
                act.wait_ge(*tm.at(f"dx{u}", i))
                act.activation(xp[u][:, :, 1:L + 1], grp(bank(2 * u + 1, FP16)[:, 0:512], P), ACT.Copy).then_inc(*A.done(f"xp{u}"))
            yield
            for u in range(UN):
                act.wait_ge(*dm.at(f"kc{u}", i))
                for q in range(2):
                    r = bank(2 * u + q)[:, 0:2 * KVR].rearrange("p (b n) -> p b n", b=2)[:, :, 2 * C:3 * C]
                    last = act.activation(grp(er[u][:, q * P:(q + 1) * P]), r, ACT.Exp, scale=-1.0 / WS)
                last.then_inc(*A.done(f"er{u}"))
            for u in range(UN):
                act.activation(ek[u][:], kc[u][:], ACT.Exp, scale=1.0 / WS).then_inc(*A.done(f"ek{u}"))
            yield
            yield
            yield
            for u in range(UN):
                act.wait_ge(*tm.at(f"rT{u}", i))
                act.activation(rT[u][:], bank(2 * u + 1)[:, 0:256], ACT.Copy).then_inc(*A.done(f"rT{u}"))
            yield

        def attention_act(act, i):
            A = aa

            norm_act(act, da, A, i, "e", norm_b)
            yield
            for u in range(UN):
                act.wait_ge(*da.at(f"hn{u}", i))
                act.activation(xs2[u][:, :, 0, :], grp(tmp2[u]), ACT.Copy).then_inc(*A.done(f"fh{u}"))
            yield
            for u in range(UN):
                act.wait_ge(*ta.at(f"fx{u}", i))
                act.wait_ge(*qa.at(f"xt{u}", i, 1))
                act.activation(xt16[u][:].rearrange("p b t -> p (b t)"), bank(4 + 2 * u, FP16)[:, 0:512],
                               ACT.Copy).then_inc(*A.done(f"xt{u}"))
            for u in range(UN):
                act.wait_ge(*ta.at(f"qkv{u}", i))
                v = bank(5 + 2 * u).rearrange("p (b n) -> p b n", b=UB)[:, :, 96:P].rearrange("p b (g d) -> p b g d", g=NKV)
                act.activation(va[u][:, :, :, 0:HD], v, ACT.Copy, scale=1.0 / WS).then_inc(*A.done(f"va{u}"))
            yield
            yield
            for u in range(UN):
                act.wait_ge(*da.at(f"qr{u}", i))
                q2 = qr[u][:].unsqueeze(2).to_broadcast([P, UB * NH, 2, HD])
                act.activation(qst[u][:, :, :, 0, :], q2, ACT.Copy).then_inc(*A.done(f"qh{u}"))
            for u in range(UN):
                act.wait_ge(*da.at(f"kr{u}", i))
                k2 = kr[u][:].unsqueeze(2).to_broadcast([P, UB * NKV, 2, HD])
                for s in range(2):
                    last = act.activation(kst[u][:, :, s, 0, :, :], k2, ACT.Copy)
                last.then_inc(*A.done(f"kh{u}"))
            yield
            yield
            for u in range(UN):
                act.wait_ge(*ta.at(f"qT{u}", i))
                act.activation(qb[u][0:C, :, 0, :], bank(4 + 2 * u, FP16)[0:C, :].rearrange("p (g t) -> p g t", t=P),
                               ACT.Copy).then_inc(*A.done(f"qb{u}"))
            yield
            yield
            yield
            for u in range(UN):
                act.wait_ge(*ta.at(f"mT{u}", i))
                act.activation(mT[u][:], bank(4 + 2 * u, BF16)[0:UB * NH * PARTS, 0:P], ACT.Copy).then_inc(*A.done(f"mT{u}"))
            yield
            for k in range(0, 2):
                for u in range(UN):
                    act.wait_ge(*ta.at(f"t{k}{u}", i))
                    act.activation(ex[u][:, k, :], bank(4 + 2 * u + k % 2), ACT.Exp).then_inc(*A.done(f"ex{k}{u}"))
            yield
            for k in range(2, 4):
                for u in range(UN):
                    act.wait_ge(*ta.at(f"t{k}{u}", i))
                    act.activation(ex[u][:, k, :], bank(4 + 2 * u + k % 2), ACT.Exp).then_inc(*A.done(f"ex{k}{u}"))
            for u in range(UN):
                act.wait_ge(*ta.at(f"oT{u}", i))
                act.activation(ot[u][:], bank(4 + 2 * u), ACT.Copy).then_inc(*A.done(f"ot{u}"))
            yield
            yield
            for u in range(UN):
                act.wait_ge(*ta.at(f"yT{u}", i))
                act.activation(rT2[u], bank(4 + 2 * u)[:, 0:256], ACT.Copy).then_inc(*A.done(f"yT{u}"))
            yield
            for u in range(UN):
                act.wait_ge(*da.at(f"xm{u}", i))
                act.activation(norm_b.sq[u], dyn(x, i, u), ACT.Square).then_inc(*A.done(f"gsq{u}"))
            yield
            for u in range(UN):
                act.wait_ge(*da.at(f"gf{u}", i))
                act.activation(xs2[u][:, :, 0, :], grp(tmp2[u]), ACT.Copy).then_inc(*A.done(f"gh{u}"))
            for u in range(UN):
                act.wait_ge(*ta.at(f"gx{u}", i))
                act.activation(xt16[u][:].rearrange("p b t -> p (b t)"), bank(5 + 2 * u, FP16)[:, 0:512],
                               ACT.Copy).then_inc(*A.done(f"xt3{u}"))
            yield
            act.wait_ge(*da.at("ls", i))
            act.activation(wr[:, :, 0:E1], lg[:, :, 0:E1], ACT.Exp).then_inc(*A.done("es"))
            yield
            yield
            act.wait_ge(*ta.at("wt", i))
            act.activation(wt[:, bass.ts(i, N)], bank(5, BF16)[0:2 * E0 * PARTS, 0:512], ACT.Copy).then_inc(*A.done("wt"))

        def pool3_zeros(pool):
            for u in range(UN):
                last = pool.memset(xp[u][:, :, 0:1], 0.0)
            last.then_inc(*p3.done("z0"))
            for u in range(UN):
                last = pool.memset(va[u][:], 0.0)
            last.then_inc(*p3.done("z1"))
            pool.wait_ge(*p3.at("z1"))
            for u in range(UN):
                last = pool.memset(va[u][:, :, :, HD:HD + 1], 1.0)
            last.then_inc(*p3.done("z2"))
            pool.wait_ge(*p3.at("z2"))
            for u in range(UN):
                last = pool.memset(qb[u][0:C, :, 1, :], 0.0)
            last.then_inc(*p3.done("z3"))
            pool.wait_ge(*p3.at("z3"))
            for u in range(UN):
                last = pool.memset(qb[u][C:P, :, 0, :], 0.0)
            last.then_inc(*p3.done("z4"))
            pool.wait_ge(*p3.at("z4"))
            for u in range(UN):
                last = pool.memset(mp[u][:], 0.0)
            last.then_inc(*p3.done("z5"))

        def mixing_pool(pool, i):
            S = qm

            for u in range(UN):
                pool.wait_ge(*tm.at(f"aT{u}", i, 1))
                if u == 0:
                    pool.wait_ge(*p2.at(f"acc{E0 - 1}", IT - 1))
                pool.tensor_copy(ar[u][:], acc[:, bass.ds(i * UN * 2 * P + u * 2 * P, 2 * P)]).then_inc(*S.done(f"ar{u}"))
            for u in range(UN):
                if u == 0:
                    pool.wait_ge(*d1a.at("h1", IT - 1))
                pool.tensor_tensor(grp(dyn(h, i, u)), grp(dyn(h, i, u)), mid(k32["beta"], UB), ALU.add).then_inc(*S.done(f"hb{u}"))
            for u in range(UN):
                pool.wait_ge(*dm.at(f"cxc{u}", i))
                pool.tensor_tensor(grp(tmp[u][:]), grp(xc[u][:]), mid(k32["gamma"], UB), ALU.mult).then_inc(*S.done(f"cg{u}"))
            yield
            yield
            yield
            yield
            yield
            yield
            yield
            yield
            yield

        def attention_pool(pool, i):
            S = qa

            yield
            for u in range(UN):
                pool.wait_ge(*da.at("er", i))
                pool.sem_inc(waited["pool"], 1)
                pool.tensor_tensor(grp(dyn(x, i, u)), grp(norm_b.xc[u]), bc(norm_b.r(u), C), ALU.mult).then_inc(*S.done(f"ex{u}"))
            yield
            yield
            yield
            yield
            yield
            yield
            yield
            yield
            yield
            yield
            yield
            yield
            yield
            yield
            for u in range(UN):
                pool.wait_ge(*aa.at(f"xt3{u}", i))
                for j in range(2):
                    last = pool.tensor_copy(xtgrp(j, i, u).rearrange("p (q t) -> p q t", q=2),
                                            xt16[u][:].rearrange("p (q j) t -> p j q t", j=2)[:, j])
                last.then_inc(*S.done(f"xt{u}"))
            yield
            yield
            yield

        def transposes(T, u, k, dt, src, ident, name, n=UB, w=P):
            for q in range(n):
                last = nc.tensor.transpose(bank(k, dt)[:, q * w:(q + 1) * w], src(q), ident)
            last.then_inc(*T.done(f"{name}{u}"))

        def mixing_pe(pe, i):
            T = tm

            def stack(u):
                return lambda q: xs[u][:, q].rearrange("p a c -> p (a c)")

            for u in range(UN):
                pe.wait_ge(*qm.at(f"ar{u}", i))
                transposes(T, u, 2 * u, F32, lambda q: ar[u][:, q * P:(q + 1) * P], k32["ident"], "aT", 2)
            yield
            yield
            yield
            yield
            for u in range(UN):
                pe.wait_ge(*dm.at(f"dl{u}", i))
                transposes(T, u, 2 * u + 1, FP16, stack(u), k16["ident16"], "dx")
            for u in range(UN):
                pe.wait_ge(*am.at(f"xp{u}", i))
                for k in range(UB):
                    dst = bank(2 * u + k // 2)[:, k % 2 * KVR:(k % 2 + 1) * KVR]
                    for n, (w, before_) in enumerate(((kvh, 0), (kvl, 0), (kvh, 1), (kvl, 1))):
                        last = pe.matmul(dst, xp[u][:, k, 1 - before_:L + 1 - before_], w[:, before_, :], start=n == 0,
                                         stop=n == 3)
                last.then_inc(*T.done(f"kvr{u}"))
            yield
            yield
            for u in range(UN):
                pe.wait_ge(*dm.at(f"kv{u}", i))
                pe.matmul(bank(2 * u)[:, 0:256], k32["tri"], ek[u][:], start=True, stop=True)
                pe.matmul(bank(2 * u)[:, 256:512], wtoep[:], kv[u][:], start=True, stop=True).then_inc(*T.done(f"sum{u}"))
            yield
            yield
            for u in range(UN):
                pe.wait_ge(*dm.at(f"rw{u}", i))
                transposes(T, u, 2 * u + 1, F32, lambda q: rw[u][:, q * P:(q + 1) * P], k32["ident"], "rT", 2)
            for u in range(UN):
                pe.wait_ge(*am.at(f"rT{u}", i))
                for q in range(2):
                    last = pe.matmul(bank(2 * u + 1)[:, 256 + q * P:256 + (q + 1) * P], rT[u][:, q * P:(q + 1) * P], k32["wo0"],
                                     start=True, stop=True)
                last.then_inc(*T.done(f"wo{u}"))
            yield

        def attention_pe(pe, i):
            T = ta

            def stack(u):
                return lambda q: xs2[u][:, q].rearrange("p a c -> p (a c)")

            def scores_ts(k):
                for u in range(UN):
                    if k == 0:
                        pe.wait_ge(*aa.at(f"qb{u}", i))
                        pe.wait_ge(*da.at(f"kd{u}", i))
                    if k > 1:
                        pe.wait_ge(*da.at(f"mx{k - 2}{u}", i))
                    dst = bank(4 + 2 * u + k % 2)
                    pe.matmul(dst, identb[:], mask_ts[:].rearrange("p h t -> p (h t)"), start=True, stop=False,
                              skip_group_check=True)
                    for n in range(NH):
                        last = pe.matmul(dst[:, n * P:(n + 1) * P], qb[u][:, NKV * k + n // 2, n % 2, :],
                                         kd[u][:, (NKV * k + n // 2) * P:(NKV * k + n // 2 + 1) * P], start=False,
                                         stop=n == NH - 1, skip_group_check=True)
                    last.then_inc(*T.done(f"s{k}{u}"))

            def scores_st(k):
                for u in range(UN):
                    if k == 0:
                        pe.wait_ge(*aa.at(f"mT{u}", i))
                    if k > 1:
                        pe.wait_ge(*aa.at(f"ex{k - 2}{u}", i))
                    dst = bank(4 + 2 * u + k % 2)
                    pe.matmul(dst, identb[:], mask_st[:].rearrange("p h t -> p (h t)"), start=True, stop=False,
                              skip_group_check=True)
                    for n in range(NH):
                        pe.matmul(dst[:, n * P:(n + 1) * P],
                                  k16["selm"][0:UB * NH * PARTS, (NH * k + n) * P:(NH * k + n + 1) * P], mT[u][:],
                                  start=False, stop=False, skip_group_check=True)
                    for g in range(NKV):
                        q = NKV * k + g
                        last = pe.matmul(dst[:, g * 256:(g + 1) * 256], kd[u][:, q * P:(q + 1) * P],
                                         qb[u][:, q].rearrange("p a t -> p (a t)"), start=False, stop=g == NKV - 1,
                                         skip_group_check=True)
                    last.then_inc(*T.done(f"t{k}{u}"))

            yield
            yield
            for u in range(UN):
                pe.wait_ge(*da.at(f"fl{u}", i))
                transposes(T, u, 4 + 2 * u, FP16, stack(u), k16["ident16"], "fx")
            for u in range(UN):
                pe.wait_ge(*aa.at(f"xt{u}", i))
                for k in range(UB):
                    for w in (qh_, ql_):
                        last = pe.matmul(bank(5 + 2 * u)[:, k * P:(k + 1) * P], xt16[u][:, k, :], w[:], start=w is qh_,
                                         stop=w is ql_)
                last.then_inc(*T.done(f"qkv{u}"))
            yield
            yield
            yield
            for u in range(UN):
                pe.wait_ge(*da.at(f"kl{u}", i))
                for g in range(UB * NKV):
                    pe.transpose(bank(4 + 2 * u, FP16)[:, g * P:(g + 1) * P],
                                 qst[u][:, 2 * g:2 * g + 2].rearrange("p g s two d -> p (g s two d)"), k16["ident16"])
                for g in range(UB * NKV):
                    last = pe.transpose(bank(5 + 2 * u, FP16)[:, g * P:(g + 1) * P],
                                        kst[u][:, g].rearrange("p a s two d -> p (a s two d)"), k16["ident16"])
                last.then_inc(*T.done(f"qT{u}"))
            yield
            scores_ts(0)
            scores_ts(1)
            yield
            scores_ts(2)
            scores_ts(3)
            yield
            yield
            for u in range(UN):
                pe.wait_ge(*da.at(f"ml{u}", i))
                pe.transpose(bank(4 + 2 * u, BF16)[0:2 * UB * NH * PARTS, 0:P], mp[u][:].rearrange("p z a b -> p (z a b)"),
                             identb[:]).then_inc(*T.done(f"mT{u}"))
            scores_st(0)
            scores_st(1)
            yield
            scores_st(2)
            scores_st(3)
            yield
            for u in range(UN):
                for k in range(UB):
                    pe.wait_ge(*aa.at(f"ex{max(k, 2)}{u}", i))
                    for n in range(NH):
                        last = pe.matmul(bank(4 + 2 * u)[32 * n:32 * n + 32, k * P:(k + 1) * P], va[u][:, k, n // 2, :],
                                         ex[u][:, k, n * P:(n + 1) * P], start=True, stop=True)
                last.then_inc(*T.done(f"oT{u}"))
            yield
            for u in range(UN):
                pe.wait_ge(*aa.at(f"ot{u}", i))
                transposes(T, u, 5 + 2 * u, F32, lambda q: ot[u][:, q * P:(q + 1) * P], k32["ident"], "o")
            yield
            for u in range(UN):
                pe.wait_ge(*da.at(f"yt{u}", i))
                transposes(T, u, 4 + 2 * u, F32, lambda q: yt[u][:, q * P:(q + 1) * P], k32["ident"], "yT", 2)
            for u in range(UN):
                pe.wait_ge(*aa.at(f"yT{u}", i))
                for q in range(2):
                    last = pe.matmul(bank(4 + 2 * u)[:, 256 + q * P:256 + (q + 1) * P], rT2[u][:, q * P:(q + 1) * P], k32["wo1"],
                                     start=True, stop=True)
                last.then_inc(*T.done(f"wo1{u}"))
            yield
            yield
            for u in range(UN):
                pe.wait_ge(*da.at(f"gl{u}", i))
                transposes(T, u, 5 + 2 * u, FP16, stack(u), k16["ident16"], "gx")
            for u in range(UN):
                pe.wait_ge(*aa.at(f"xt3{u}", i))
                for k in range(UB):
                    for w in (rh, rl):
                        last = pe.matmul(bank(4 + 2 * u)[:, k * E1:(k + 1) * E1], xt16[u][:, k, :], w[:], start=w is rh,
                                         stop=w is rl)
                last.then_inc(*T.done(f"lg{u}"))
            yield
            yield
            yield
            pe.wait_ge(*da.at("wpl", i))
            for q in range(GB // 2):
                w = 2 * E1 * PARTS
                last = pe.transpose(bank(5, BF16)[0:2 * w, q * P:(q + 1) * P], wpf[:, q * w:(q + 2) * w], identb[:])
            last.then_inc(*T.done("wt"))

        ORDER1 = "bfbbffbbbfbbfbbfffbbbbbbbfbbf"

        def layer1_dve(dve):
            dm.prime(dve)
            da.prime(dve)
            pipelined(dve, ORDER1, mixing_dve, attention_dve)

        def layer1_act(act):
            am.prime(act)
            aa.prime(act)
            act.wait_ge(*p1.at("xt1", IT - 1))
            pipelined(act, ORDER1, mixing_act, attention_act)

        def layer1_pool(pool):
            qm.prime(pool)
            qa.prime(pool)
            pipelined(pool, ORDER1, mixing_pool, attention_pool)

        def layer1_pe(pe):
            tm.prime(pe)
            ta.prime(pe)
            pe.wait_ge(*p3.at("z5"))
            pe.wait_ge(*ds.at("kvl"))
            pe.wait_ge(*ds.at("rl"))
            pe.wait_ge(*ds.at("mask_b"))
            pipelined(pe, ORDER1, mixing_pe, attention_pe)

        hm = hid
        ht = [[w1s[:, (2 * k + j) * N:(2 * k + j + 1) * N] for j in range(2)] for k in range(2)]
        sa = [a1s[:, k * N:(k + 1) * N] for k in range(2)]
        units = []
        for q in range(E1 // 2):
            for chunk, cols, buf in ((f"main{2 * q}", 2 * q * FM, hm[0]), (f"tail{q}", E1 * FM + q * P, ht[q % 2]),
                                     (f"main{2 * q + 1}", (2 * q + 1) * FM, hm[1])):
                units += [(chunk, cols, buf[j], j) for j in range(2)]
        plan = []
        for q in range(E1 // 2):
            n = 6 * q
            plan += [("wb", 2 * q), ("ab", n)] + ([("y", 2 * q - 1)] if q else []) + [("ab", n + 1), ("ab", n + 2), ("ab", n + 3),
                     ("wb", 2 * q + 1), ("ab", n + 4), ("y", 2 * q), ("ab", n + 5)]
        plan.append(("y", E1 - 1))
        t4 = Steps(sem("pe4"), [f"{a}{n}" for a, n in plan], loop=True)
        a4 = Steps(sem("act4"), [f"{'silu' if a == 'ab' else a}{n}" for a, n in plan if a != "y"], loop=True)
        d4 = Steps(sem("dve4"), [f"{'u' if a == 'ab' else 'yw'}{n}" for a, n in plan if a != "wb"], loop=True)
        p4 = Steps(sem("pool4"), [f"acc{e}" for e in range(E1)], loop=True)
        NU = len(units)

        def loop4_pe(pe):
            T = t4
            T.prime(pe)
            pe.wait_ge(*qa.at("xt1", IT - 1))
            pe.wait_ge(*aa.at("wt", IT - 1))
            pe.wait_ge(*ds.at("a3l"))
            pe.wait_ge(ld["w2m"], 16)
            pe.wait_ge(ld["w2t"], 16)
            with pe.Fori(0, IT) as i:
                for kind, n in plan:
                    if kind == "wb":
                        pe.wait_ge(*before(a4, "wb", n, 2, i, E1))
                        pe.matmul(bank(n % 2), k16["sel1"][0:2 * E0 * PARTS, n * P:(n + 1) * P], wt[:, bass.ts(i, N)], start=True, stop=True).then_inc(*T.done(f"wb{n}"))
                    elif kind == "ab":
                        _, cols, _, j = units[n]
                        pe.wait_ge(*before(d4, "u", n, 2, i, NU))
                        for m, (hi, lo) in enumerate(((a1h, a1l), (a3h, a3l))):
                            for w in (hi, lo):
                                last = pe.matmul(bank(2 + 2 * (n % 2) + m), w[:, cols:cols + P], xt[j][:, bass.ts(i, N)],
                                                 start=w is hi, stop=w is lo)
                        last.then_inc(*T.done(f"ab{n}"))
                    else:
                        pe.wait_ge(*d4.at(f"u{6 * (n // 2) + (5 if n % 2 else 3)}", i))
                        for w, buf in ((w2m, hm[n % 2]), (w2t, ht[n // 2 % 2])):
                            for j in range(2):
                                last = pe.matmul(bank(6 + n % 2)[C * j:C * j + C, :], w[:, n * C:(n + 1) * C], buf[j][:],
                                                 start=w is w2m, stop=w is w2t, skip_group_check=True)
                        last.then_inc(*T.done(f"y{n}"))

        def loop4_act(act):
            A = a4
            A.prime(act)
            with act.Fori(0, IT) as i:
                for kind, n in plan:
                    if kind == "wb":
                        act.wait_ge(*t4.at(f"wb{n}", i))
                        act.wait_ge(*before(d4, "yw", n, 2, i, E1))
                        act.activation(wbs[n % 2][:], bank(n % 2), ACT.Copy).then_inc(*A.done(f"wb{n}"))
                    elif kind == "ab":
                        act.wait_ge(*t4.at(f"ab{n}", i))
                        act.wait_ge(*before(d4, "u", n, 2, i, NU))
                        act.activation(sa[n % 2][:], bank(2 + 2 * (n % 2)), ACT.Silu, scale=1.0 / WS).then_inc(*A.done(f"silu{n}"))

        def loop4_dve(dve):
            D = d4
            D.prime(dve)
            with dve.Fori(0, IT) as i:
                for kind, n in plan:
                    if kind == "ab":
                        dve.wait_ge(*a4.at(f"silu{n}", i))
                        dve.tensor_tensor(units[n][2][:], sa[n % 2][:], bank(3 + 2 * (n % 2)), ALU.mult).then_inc(*D.done(f"u{n}"))
                    elif kind == "y":
                        dve.wait_ge(*t4.at(f"y{n}", i))
                        dve.wait_ge(*a4.at(f"wb{n}", i))
                        dve.wait_ge(*before(p4, "acc", n, 2, i, E1))
                        dve.tensor_tensor(yw[n % 2][:], bank(6 + n % 2), wbs[n % 2][:], ALU.mult).then_inc(*D.done(f"yw{n}"))

        GROUPS = IT * UN
        ob = [hidden[:, k * UB * C:(k + 1) * UB * C] for k in range(GROUPS)]
        te = Steps(sem("pe_end"), [f"aT{g}" for g in range(GROUPS)])
        de = Steps(sem("dve_end"), [f"{s}{g}" for g in range(GROUPS) for s in ("o", "out")])
        out_v = out.rearrange("b t c -> t b c")

        def end_pe(pe):
            pe.wait_ge(*p4.at(f"acc{E1 - 1}", IT - 1))
            for g in range(GROUPS):
                if g == 6:
                    pe.wait_ge(*d4.at(f"yw{E1 - 1}", IT - 1))
                for q in range(2):
                    last = pe.transpose(bank(g)[:, q * P:(q + 1) * P], acc[:, (2 * g + q) * P:(2 * g + q + 1) * P], k32["ident"])
                last.then_inc(*te.done(f"aT{g}"))

        def end_dve(dve):
            for g in range(GROUPS):
                cols = slice(g * UB * C, (g + 1) * UB * C)
                dve.wait_ge(*te.at(f"aT{g}"))
                dve.scalar_tensor_tensor(ob[g], bank(g)[:, 0:256], 1.0 / WS, x[:, cols], ALU.mult, ALU.add).then_inc(*de.done(f"o{g}"))
                dve.wait_ge(*de.at(f"o{g}"))
                dve.tensor_tensor(ob[g], ob[g], h[:, cols], ALU.add).then_inc(*de.done(f"out{g}"))

        def end_sync(sp):
            for g in range(GROUPS):
                sp.wait_ge(*de.at(f"out{g}"))
                sp.dma_start(out_v[:, g * UB:(g + 1) * UB, :], grp(ob[g])).then_inc(out_done, 16)
            sp.wait_ge(out_done, 16 * GROUPS)

        block = ctx.enter_context(nc.Block())

        @block.sync
        def _(sp):
            sp.dma_start(cs[:], c32).then_inc(ld["c32"], 16)
            for n, dst, src in (("w1", w1s, w1_0), ("c16", ch, c16), ("w2", w2s, w2_0), ("a1", a1s, w1_1),
                                ("a3", a3s, w3_1), ("w2m", w2m, w2m_1), ("w2t", w2t, w2t_1)):
                sp.dma_start(dst[:], src).then_inc(ld[n], 16)
            for g in range(B // UB):
                sp.wait_ge(rows_in[g], 16 * UB)
                sp.sem_inc(group_in, 1)
            end_sync(sp)

        @block.gpsimd
        def _(pool):
            pool3_zeros(pool)
            p1.prime(pool)
            pool.wait_ge(*ds.at("idx1"))
            AHEAD = 3
            edges_pool(pool, 0, GB + AHEAD)
            pool.wait_ge(*ds.at("spt"))
            for t in range(IT):
                index_pool(pool, t)
                rows_pool(pool, t)
                edges_pool(pool, min((t + 1) * GB + AHEAD, B), min((t + 2) * GB + AHEAD, B))
                if t == IT - 2:
                    tokens_pool(pool, 0)
            loop1_pool(pool)
            moe_pool(pool, p2, d2, E0)
            layer1_pool(pool)
            moe_pool(pool, p4, d4, E1)

        @block.scalar
        def _(act):
            act.dma_start(tok[:], tokens).then_inc(ld["tok"], 16)
            setup_act(act)
            loop1_act(act)
            loop2_act(act)
            layer1_act(act)
            loop4_act(act)

        @block.vector
        def _(dve):
            setup_dve(dve)
            loop1_dve(dve)
            loop2_dve(dve)
            layer1_dve(dve)
            loop4_dve(dve)
            end_dve(dve)

        @block.tensor
        def _(pe):
            setup_pe(pe)
            pe.wait_ge(ld["c16"], 16)
            loop1_pe(pe)
            loop2_pe(pe)
            layer1_pe(pe)
            loop4_pe(pe)
            end_pe(pe)


def packed(ins):
    f = np.float32
    t = np.arange(P)
    v = {"ident": np.eye(P, dtype=f), "tri": (t[:, None] <= t[None, :]).astype(f),
         "mask_ts": np.where(t[None, :] <= t[:, None], 0.0, NEG).astype(f),
         "mask_st": np.where(t[:, None] <= t[None, :], 0.0, NEG).astype(f)}
    inv = 1.0 / 10000.0 ** (np.arange(0, HD, 2, dtype=f) / HD)
    ang = np.outer(t.astype(f), inv).astype(f)
    cos, sin = np.cos(ang), np.sin(ang)
    scale = np.array([HD ** -0.5] * NH + [1.0] * NKV, f) / f(WS)
    v["cos"] = (scale[None, :, None] * np.concatenate([cos, cos], 1)[:, None, :]).reshape(P, 96)
    v["sin"] = (scale[None, :, None] * np.concatenate([-sin, sin], 1)[:, None, :]).reshape(P, 96)
    v["base"] = np.broadcast_to(np.minimum(np.arange(B), TAB_B - 1) * NODES * NODES, (P, B))
    v["pri0"] = np.broadcast_to(E0 - np.arange(E0), (P, E0))
    v["pri1"] = np.broadcast_to(E1 - np.arange(E1), (P, E1))
    v["eps_ln"], v["eps_rms"] = np.full((P, 1), 1e-5), np.full((P, 1), 1e-6)

    def twice(a):
        return np.concatenate([a, a], 0)

    def rows_(a):
        return np.broadcast_to(a[None, :], (P, a.shape[0]))

    def diag(a):
        d = np.zeros((P, P), f)
        d[:C, :C] = a
        d[C:, C:] = a
        return d

    g = ins
    v["wq0"], v["wk0"] = twice(g["L0_attn_Wq"]), twice(g["L0_attn_Wk"])
    v["gate_w"], v["gate_b"] = twice(g["L0_ffn_gate_w"]), rows_(g["L0_ffn_gate_b"])
    v["b1"], v["b2"] = g["L0_ffn_b1"].T, twice(g["L0_ffn_b2"].T)
    v["gamma"], v["beta"] = rows_(g["L0_ffn_gamma"]), rows_(g["L0_ffn_beta"])
    v["mix"] = twice(np.stack([g[f"L1_attn_time_mix_{m}"].reshape(C) for m in "kvr"], 1))
    v["wkvr"] = twice(np.concatenate([g[f"L1_attn_W{m}"] for m in "kvr"], 1))
    v["wo0"] = diag(g["L1_attn_Wo"])
    tw = g["L1_attn_time_w"]
    v["toep"] = tw[np.clip(tw.shape[0] - 1 - (t[None, :] - t[:, None]), 0, tw.shape[0] - 1)]
    v["ln1"], v["ln2"] = twice(g["L1_ffn_ln1_w"][:, None]), twice(g["L1_ffn_ln2_w"][:, None])
    v["wqkv"] = twice(np.concatenate([g["L1_ffn_wq"], g["L1_ffn_wk"], g["L1_ffn_wv"]], 0).T)
    v["wo1"] = diag(g["L1_ffn_wo"].T)
    v["router"] = twice(g["L1_ffn_router_w"].T)
    big = np.zeros((P, N32), f)
    for n, s in AT32.items():
        big[:, s] = v[n]
    return big


def selectors():
    out = np.zeros((P, N16), np.float16)
    out[:, AT16["ident16"]] = np.eye(P)
    for name, ne in (("sel0", E0), ("sel1", E1)):
        s = np.zeros((P, ne, P), np.float16)
        for j in range(2):
            for e in range(ne):
                r = (j * ne + e) * PARTS
                s[r:r + PARTS, e, j * C:(j + 1) * C] = 1
        out[:, AT16[name]] = s.reshape(P, -1)
    s = np.zeros((P, UB * NH, P), np.float16)
    for k in range(UB * NH):
        s[k * PARTS:(k + 1) * PARTS, k, :] = 1
    out[:, AT16["selm"]] = s.reshape(P, -1)
    return out


def laid_out(ins):
    def twice(a):
        return np.concatenate([a, a], 0)

    a = {"tokens": ins["x"], "t2e": ins["L0_tok_token_to_edge"],
         "rows": np.concatenate([ins["L0_tok_edge_emb"].reshape(ROWS, C), ins["L0_tok_special_emb"]], 0),
         "c32": packed(ins), "c16": selectors(),
         "w1_0": twice(ins["L0_ffn_w1"].transpose(1, 0, 2).reshape(C, E0 * F0)),
         "w2_0": ins["L0_ffn_w2"].transpose(1, 0, 2).reshape(F0, E0 * C)}
    for n, w in (("w1_1", ins["L1_ffn_w1"]), ("w3_1", ins["L1_ffn_w3"])):
        wt = w.transpose(2, 0, 1)
        tail = np.zeros((C, E1, FT), np.float32)
        tail[:, :, :F1 - FM] = wt[:, :, FM:]
        a[n] = twice(np.concatenate([wt[:, :, :FM].reshape(C, -1), tail.reshape(C, -1)], 1))
    wt = ins["L1_ffn_w2"].transpose(2, 0, 1)
    tail = np.zeros((2, FT, E1, C), np.float32)
    for e in range(E1):
        tail[e % 2, :F1 - FM, e] = wt[FM:, e]
    a["w2m_1"], a["w2t_1"] = wt[:FM].reshape(FM, -1), tail.reshape(P, -1)
    return {n: np.ascontiguousarray(v) for n, v in a.items()}


def kernel(**inputs):
    import concourse.bacc as _bacc
    from concourse.bass_utils import run_bass_kernel_spmd as _run

    nc = _bacc.Bacc("TRN2", target_bir_lowering=False, num_devices=1)
    arrays, args = {}, []
    for name, a in laid_out({n: np.asarray(v) for n, v in inputs.items()}).items():
        arrays[f"in_{name}"] = a
        args.append(nc.dram_tensor(f"in_{name}", a.shape, mybir.dt.from_np(a.dtype), kind="ExternalInput").ap())
    args.append(nc.dram_tensor("tower_out", (B, L, C), F32, kind="ExternalOutput").ap())
    lm_tower(nc, *args)
    r = _run(nc, [arrays], core_ids=[0])
    return r.results[0]["tower_out"]
```

```python
from contextlib import ExitStack

import concourse.bass as bass
import numpy as np
from concourse import mybir

B, L, C = 32, 128, 64
NODES, TAB_B, SPECIAL = 96, 8, 3
ROWS = TAB_B * NODES * NODES
E0, F0 = 16, 128
E1, F1 = 8, 170
FM, FT = 128, 64
NH, NKV, HD = 4, 2, 16
KVR = 3 * C
WS = 64.0
NEG = -1e30
P = 128
HALF = B // 2 * L
IT, UN, UB = 4, 2, 4
PARTS = 3

F32, BF16, FP16, I32 = mybir.dt.float32, mybir.dt.bfloat16, mybir.dt.float16, mybir.dt.int32
ALU, ACT, AX = mybir.AluOpType, mybir.ActivationFunctionType, mybir.AxisListType

COLS = [("ident", P), ("tri", P), ("mask_ts", P), ("mask_st", P), ("cos", 96), ("sin", 96), ("base", B),
        ("pri0", E0), ("pri1", E1),
        ("wq0", C), ("wk0", C), ("gate_w", E0), ("gate_b", E0), ("b1", E0), ("b2", E0), ("gamma", C), ("beta", C),
        ("mix", 3), ("wkvr", KVR), ("wo0", P), ("toep", P), ("ln1", 1), ("ln2", 1), ("wqkv", P), ("wo1", P),
        ("router", E1)]
COLS16 = [("ident16", P), ("sel0", E0 * P), ("sel1", E1 * P), ("selm", UB * NH * P)]


def offsets(cols):
    at, out = 0, {}
    for name, n in cols:
        out[name] = slice(at, at + n)
        at += n
    return out, at


AT32, N32 = offsets(COLS)
AT16, N16 = offsets(COLS16)


class Steps:

    def __init__(self, sem, names, loop=False):
        self.sem, self.names, self.loop, self.next = sem, names, loop, 0
        self.place = {n: k + 1 for k, n in enumerate(names)}
        assert len(self.place) == len(names)

    def done(self, name):
        assert self.names[self.next % len(self.names)] == name, (self.names[self.next % len(self.names)], name)
        self.next += 1
        return self.sem, 1

    def at(self, name, turn=0, back=0):
        assert self.loop or not back
        if not self.loop:
            return self.sem, self.place[name]
        return self.sem, (turn + 1 - back) * len(self.names) + self.place[name]

    def prime(self, eng):
        eng.sem_inc(self.sem, len(self.names))


def both(*stages):
    return [f"{s}{u}" for s in stages for u in range(UN)]


def lm_tower(nc, tokens, t2e, rows, c32, c16, w1_0, w2_0, w1_1, w3_1, w2m_1, w2t_1, out):
    with ExitStack() as ctx:
        def sb(name, shape, dt=F32):
            return ctx.enter_context(nc.sbuf_tensor(name, shape, dt))

        def sem(name):
            return ctx.enter_context(nc.semaphore(name))

        def grp(ap, n=C):
            return ap.rearrange("p (b f) -> p b f", f=n)

        def bc(ap, n):
            return ap.unsqueeze(len(ap.shape)).to_broadcast([*ap.shape, n])

        def mid(ap, n):
            return ap.unsqueeze(1).to_broadcast([ap.shape[0], n, ap.shape[1]])

        banks = ctx.enter_context(nc.psum_tensor("banks", [P, 8, 512], F32))

        def bank(k, dt=F32):
            return banks[:, k, :] if dt == F32 else banks[:, k, :].bitcast(dt)

        cs = sb("cs", [P, N32])
        ch = sb("ch", [P, N16], FP16)
        k32 = {n: cs[:, s] for n, s in AT32.items()}
        k16 = {n: ch[:, s] for n, s in AT16.items()}
        h = sb("h", [P, B * C])
        x = sb("x", [P, B * C])
        xt = [sb(f"xt{j}", [P, HALF], FP16) for j in range(2)]
        wt = sb("wt", [2 * E0 * PARTS, HALF], BF16)
        acc = sb("acc", [P, HALF])

        w1s, w1h, w1l = sb("w1s", [P, E0 * F0]), sb("w1h", [P, E0 * F0], FP16), sb("w1l", [P, E0 * F0], FP16)
        w2s = sb("w2s", [P, E0 * C])
        NA = E1 * (FM + FT)
        a1s, a1h, a1l = sb("a1s", [P, NA]), sb("a1h", [P, NA], FP16), sb("a1l", [P, NA], FP16)
        a3s, a3h, a3l = sb("a3s", [P, NA]), sb("a3h", [P, NA], FP16), sb("a3l", [P, NA], FP16)
        b1s, b2s = sb("b1s", [P, E0]), sb("b2s", [P, E0])
        w2m, w2t = sb("w2m", [P, E1 * C]), sb("w2t", [P, E1 * C])
        m2 = sb("m2", [P, P])
        gh, gl = sb("gh", [P, E0], FP16), sb("gl", [P, E0], FP16)
        mix1 = sb("mix1", [P, 3])
        kvs, kvh, kvl = sb("kvs", [P, 2, KVR]), sb("kvh", [P, 2, KVR], FP16), sb("kvl", [P, 2, KVR], FP16)
        wtoep = sb("wtoep", [P, P])
        qs, qh_, ql_ = sb("qs", [P, P]), sb("qh", [P, P], FP16), sb("ql", [P, P], FP16)
        rs_, rh, rl = sb("rs", [P, E1]), sb("rh", [P, E1], FP16), sb("rl", [P, E1], FP16)
        identb = sb("identb", [P, P], BF16)
        mask_ts, mask_st = sb("mask_ts", [P, NH, P], BF16), sb("mask_st", [P, NH, P], BF16)

        ld = {n: sem(f"ld_{n}") for n in ("tok", "c32", "c16", "w1", "w2", "a1", "a3", "w2m", "w2t")}
        edges_in = [sem(f"edges_in{t}") for t in range(IT)]
        rows_in = [sem(f"rows_in{g}") for g in range(B // UB)]
        group_in = sem("group_in")
        waited = {n: sem(f"waited_{n}") for n in ("pool", "dve")}
        out_done = sem("out_done")

        tok = sb("tok", [B, L], I32)
        tokf = sb("tokf", [B, L])
        tokt = sb("tokt", [P, B])
        idx1 = sb("idx1", [P, B], I32)
        edge = sb("edge", [P, B, 2], I32)
        edgef = sb("edgef", [P, B, 2])
        rowf, isp, sprow, spt = (sb(n, [P, B]) for n in ("rowf", "isp", "sprow", "spt"))
        idx2 = sb("idx2", [P, B], I32)

        ds = Steps(sem("dve_setup"), ["tokf", "tokt", "idx1", "spt", "m2z", "m2a", "m2b", "w1l", "gl", "mix1", "kvs",
                                      "kvl", "toep", "qs", "ql", "rs", "rl", "identb", "mask_a", "mask_b",
                                      "a1s", "a1l", "a3s", "a3l", "b1s", "b2s"])
        as_ = Steps(sem("act_setup"), ["w1h", "gh", "kvh", "qh", "rh", "a1h", "a3h"])
        ts_ = Steps(sem("pe_setup"), ["tokt", "m2"])

        px = Steps(sem("pool_index"), [f"{s}{t}" for t in range(IT) for s in
                                       ("edgef", "isp", "row0", "row1", "row2", "sprow", "spd", "row3", "idx2")])

        def edges_pool(pool, lo, hi):
            for b in range(lo, hi):
                pool.indirect_dma_start(edge[:, b, :], None, t2e, bass.IndirectOffsetOnAxis(ap=idx1[:, b:b + 1], axis=0)
                                        ).then_inc(edges_in[b // (UN * UB)], 16)

        def index_pool(pool, t):
            b = slice(t * UN * UB, (t + 1) * UN * UB)
            pool.wait_ge(edges_in[t], 16 * UN * UB)
            pool.tensor_scalar(edgef[:, b], edge[:, b], float(NODES - 1), 0.0, ALU.min,
                               ALU.max).then_inc(*px.done(f"edgef{t}"))
            pool.tensor_scalar(isp[:, b], tokt[:, b], float(SPECIAL), None, ALU.is_lt).then_inc(*px.done(f"isp{t}"))
            pool.wait_ge(*px.at(f"edgef{t}"))
            pool.tensor_scalar(rowf[:, b], edgef[:, b, 0], float(NODES), None, ALU.mult).then_inc(*px.done(f"row0{t}"))
            pool.wait_ge(*px.at(f"row0{t}"))
            pool.tensor_tensor(rowf[:, b], rowf[:, b], edgef[:, b, 1], ALU.add).then_inc(*px.done(f"row1{t}"))
            pool.wait_ge(*px.at(f"row1{t}"))
            pool.tensor_tensor(rowf[:, b], rowf[:, b], k32["base"][:, b], ALU.add).then_inc(*px.done(f"row2{t}"))
            pool.wait_ge(*px.at(f"row2{t}"))
            pool.tensor_tensor(sprow[:, b], spt[:, b], rowf[:, b], ALU.subtract).then_inc(*px.done(f"sprow{t}"))
            pool.wait_ge(*px.at(f"sprow{t}"))
            pool.tensor_tensor(sprow[:, b], sprow[:, b], isp[:, b], ALU.mult).then_inc(*px.done(f"spd{t}"))
            pool.wait_ge(*px.at(f"spd{t}"))
            pool.tensor_tensor(rowf[:, b], rowf[:, b], sprow[:, b], ALU.add).then_inc(*px.done(f"row3{t}"))
            pool.wait_ge(*px.at(f"row3{t}"))
            pool.tensor_copy(idx2[:, b], rowf[:, b]).then_inc(*px.done(f"idx2{t}"))

        def rows_pool(pool, t):
            pool.wait_ge(*px.at(f"idx2{t}"))
            for b in range(t * UN * UB, (t + 1) * UN * UB):
                pool.indirect_dma_start(h[:, b * C:(b + 1) * C], None, rows,
                                        bass.IndirectOffsetOnAxis(ap=idx2[:, b:b + 1], axis=0)
                                        ).then_inc(rows_in[b // UB], 16)

        def setup_dve(dve):
            dve.wait_ge(ld["tok"], 16)
            dve.tensor_copy(tokf[:], tok[:]).then_inc(*ds.done("tokf"))
            dve.wait_ge(*ts_.at("tokt"))
            dve.tensor_copy(tokt[:], bank(0)[:, 0:B]).then_inc(*ds.done("tokt"))
            dve.tensor_scalar(idx1[:], bank(0)[:, 0:B], float(SPECIAL + NODES * NODES - 1), 0.0, ALU.min,
                              ALU.max).then_inc(*ds.done("idx1"))
            dve.tensor_scalar(spt[:], bank(0)[:, 0:B], float(ROWS), None, ALU.add).then_inc(*ds.done("spt"))
            dve.memset(m2[:], 0.0).then_inc(*ds.done("m2z"))
            dve.wait_ge(*ts_.at("m2"))
            dve.wait_ge(*ds.at("m2z"))
            for j, n in enumerate(("m2a", "m2b")):
                q = slice(C * j, C * j + C)
                dve.tensor_scalar(m2[q, q], bank(1)[q, 0:C], C ** -0.5, None, ALU.mult).then_inc(*ds.done(n))

            def low(name, lo, src, hi, scale=1.0):
                dve.scalar_tensor_tensor(lo, src, scale, hi, ALU.mult, ALU.subtract).then_inc(*ds.done(name))

            dve.wait_ge(ld["w1"], 16)
            dve.wait_ge(*as_.at("w1h"))
            low("w1l", w1l[:], w1s[:], w1h[:], WS)
            dve.wait_ge(*as_.at("gh"))
            low("gl", gl[:], k32["gate_w"], gh[:], WS)
            dve.tensor_scalar(mix1[:], k32["mix"], -1.0, 1.0, ALU.mult, ALU.add).then_inc(*ds.done("mix1"))
            dve.wait_ge(*ds.at("mix1"))
            for m in range(3):
                q = slice(C * m, C * m + C)
                dve.tensor_scalar(kvs[:, 0, q], k32["wkvr"][:, q], k32["mix"][:, m:m + 1], WS, ALU.mult, ALU.mult)
                last = dve.tensor_scalar(kvs[:, 1, q], k32["wkvr"][:, q], mix1[:, m:m + 1], WS, ALU.mult, ALU.mult)
            last.then_inc(*ds.done("kvs"))
            dve.wait_ge(*as_.at("kvh"))
            low("kvl", kvl[:], kvs[:], kvh[:])
            dve.tensor_tensor(wtoep[:], k32["toep"], k32["tri"], ALU.mult).then_inc(*ds.done("toep"))
            dve.tensor_scalar(qs[:], k32["wqkv"], k32["ln1"], WS, ALU.mult, ALU.mult).then_inc(*ds.done("qs"))
            dve.wait_ge(*as_.at("qh"))
            low("ql", ql_[:], qs[:], qh_[:])
            dve.tensor_scalar(rs_[:], k32["router"], k32["ln2"], WS, ALU.mult, ALU.mult).then_inc(*ds.done("rs"))
            dve.wait_ge(*as_.at("rh"))
            low("rl", rl[:], rs_[:], rh[:])
            dve.tensor_copy(identb[:], k32["ident"]).then_inc(*ds.done("identb"))
            dve.tensor_copy(mask_ts[:], mid(k32["mask_ts"], NH)).then_inc(*ds.done("mask_a"))
            dve.tensor_copy(mask_st[:], mid(k32["mask_st"], NH)).then_inc(*ds.done("mask_b"))
            for n, s, hi, lo in (("a1", a1s, a1h, a1l), ("a3", a3s, a3h, a3l)):
                dve.wait_ge(ld[n], 16)
                dve.tensor_scalar(s[:], s[:], k32["ln2"], WS, ALU.mult, ALU.mult).then_inc(*ds.done(n + "s"))
                dve.wait_ge(*as_.at(n + "h"))
                low(n + "l", lo[:], s[:], hi[:])
            dve.tensor_scalar(b1s[:], k32["b1"], WS, None, ALU.mult).then_inc(*ds.done("b1s"))
            dve.tensor_scalar(b2s[:], k32["b2"], WS, None, ALU.mult).then_inc(*ds.done("b2s"))

        def setup_act(act):
            act.wait_ge(ld["w1"], 16)
            act.activation(w1h[:], w1s[:], ACT.Copy, scale=WS).then_inc(*as_.done("w1h"))
            act.wait_ge(ld["c32"], 16)
            act.activation(gh[:], k32["gate_w"], ACT.Copy, scale=WS).then_inc(*as_.done("gh"))
            for n, src, hi, dep in (("kvh", kvs, kvh, "kvs"), ("qh", qs, qh_, "qs"), ("rh", rs_, rh, "rs"),
                                    ("a1h", a1s, a1h, "a1s"), ("a3h", a3s, a3h, "a3s")):
                act.wait_ge(*ds.at(dep))
                act.activation(hi[:], src[:], ACT.Copy).then_inc(*as_.done(n))

        def setup_pe(pe):
            pe.wait_ge(ld["c32"], 16)
            pe.wait_ge(*ds.at("tokf"))
            pe.transpose(bank(0)[:, 0:B], tokf[:], k32["ident"][0:B, 0:B]).then_inc(*ts_.done("tokt"))
            for j in range(2):
                last = pe.matmul(bank(1)[C * j:C * j + C, 0:C], k32["wq0"][0:C, :], k32["wk0"][0:C, :],
                                 start=True, stop=True)
            last.then_inc(*ts_.done("m2"))

        eps_ln, eps_rms = 1e-5, 1e-6
        xc = [sb(f"xc{u}", [P, UB * C]) for u in range(UN)]
        sq = [sb(f"sq{u}", [P, UB * C]) for u in range(UN)]
        xr = [sb(f"xr{u}", [P, UB * C]) for u in range(UN)]
        tmp = [sb(f"tmp{u}", [P, UB * C]) for u in range(UN)]
        xs = [sb(f"xs{u}", [P, UB, 2, C], FP16) for u in range(UN)]
        fT = [sb(f"fT{u}", [P, 2 * P]) for u in range(UN)]
        qT = [sb(f"qT{u}", [P, 2 * P]) for u in range(UN)]
        at = [sb(f"at{u}", [P, UB, P]) for u in range(UN)]
        atT = [sb(f"atT{u}", [P, UB * P]) for u in range(UN)]
        xt16 = [sb(f"xt16{u}", [P, UB, P], FP16) for u in range(UN)]
        mx = [sb(f"mx{u}", [P, UB]) for u in range(UN)]
        smx = [sb(f"smx{u}", [P, UB]) for u in range(UN)]
        GB = UN * UB
        lg, eq, pr, wr = (sb(n, [P, GB, E0]) for n in ("lg", "eq", "pr", "wr"))
        f1, f2 = sb("f1", [P, GB, E0]), sb("f2", [P, GB, E0])
        sm = sb("sm", [P, 12, GB])
        wpf = sb("wp", [P, GB * E0 * PARTS], BF16)
        wp0 = wpf[:].rearrange("p (b e k) -> p b e k", b=GB, e=E0)
        wrem = sb("wrem", [P, GB, E0])

        SUM, SS, VAR, Y, A_, B_, R = range(7)
        RSQRT = ["guess", "a", "s", "t", "z", "b", "c", "r"]

        class Norm:

            def __init__(self, name, xc, sq):
                self.st, self.xc, self.sq = sb(name, [P, 7, 2, UN * UB]), xc, sq

            def row(self, k):
                return self.st[:, k, 0, :]

            def part(self, k, u, second=0):
                return self.st[:, k, second, u * UB:(u + 1) * UB]

            def r(self, u, second=0):
                return self.part(R, u, second)

        norm_a = Norm("st_a", [b[:] for b in xc], [b[:] for b in sq])
        mixed = sb("mixed", [P, 5 * UN * UB * C])
        parts_of_mixed = [mixed[:, k * UB * C:(k + 1) * UB * C] for k in range(5 * UN)]
        kc, ek, er, kv, rw = (parts_of_mixed[UN * k:UN * (k + 1)] for k in range(5))
        norm_r = Norm("st_r", [b[:] for b in kc], [b[:] for b in ek])

        def norm_names(p):
            var = ["var", "var2"] if p == "e" else ["var"]
            return both(p + "sum", p + "xc", p + "ss") + [p + s for s in var + RSQRT]

        def rms_names(p):
            return both(p + "ss") + [p + s for s in ["var"] + RSQRT]

        def norm_centre(dve, D, i, p, w, src, ready):
            for u in range(UN):
                ready(u)
                dve.sem_inc(waited["dve"], 1)
                dve.tensor_reduce(w.part(SUM, u), src(u), AX.X, ALU.add).then_inc(*D.done(f"{p}sum{u}"))
            for u in range(UN):
                dve.wait_ge(*D.at(f"{p}sum{u}", i))
                dve.scalar_tensor_tensor(grp(w.xc[u]), bc(w.part(SUM, u), C), 1.0 / C, src(u), ALU.mult,
                                         ALU.subtract).then_inc(*D.done(f"{p}xc{u}"))

        def rms_dve(dve, D, A, i, p, w, eps, sign=1.0, rms_too=False):
            for u in range(UN):
                dve.wait_ge(*A.at(f"{p}sq{u}", i))
                dve.tensor_reduce(w.part(SS, u), grp(w.sq[u]), AX.X, ALU.add).then_inc(*D.done(f"{p}ss{u}"))
            dve.wait_ge(*D.at(f"{p}ss{UN - 1}", i))
            dve.tensor_scalar(w.row(VAR), w.row(SS), 1.0 / C, eps, ALU.mult, ALU.add).then_inc(*D.done(p + "var"))
            if rms_too:
                dve.tensor_scalar(w.st[:, VAR, 1, :], w.row(SS), (1.0 + eps_rms) / C, eps_rms * eps, ALU.mult,
                                  ALU.add).then_inc(*D.done(p + "var2"))
            dve.wait_ge(*D.at(p + ("var2" if rms_too else "var"), i))
            var, y, a, b, r = (w.st[:, k, :, :].rearrange("p w b -> p (w b)") if rms_too else w.row(k)
                               for k in (VAR, Y, A_, B_, R))
            k = 3.0 / 8.0
            dve.tensor_scalar(y.bitcast(I32), var.bitcast(I32), -0.5, float(0x5f3759df), ALU.mult,
                              ALU.add).then_inc(*D.done(p + "guess"))
            yield p + "_cubic"
            dve.wait_ge(*D.at(p + "guess", i))
            dve.tensor_tensor(a, y, y, ALU.mult).then_inc(*D.done(p + "a"))
            dve.wait_ge(*D.at(p + "a", i))
            dve.tensor_tensor(a, a, var, ALU.mult).then_inc(*D.done(p + "s"))
            dve.wait_ge(*D.at(p + "s", i))
            dve.scalar_tensor_tensor(b, a, -10.0 / 3.0, a, ALU.add, ALU.mult).then_inc(*D.done(p + "t"))
            dve.wait_ge(*D.at(p + "t", i))
            dve.scalar_tensor_tensor(y, b, 5.0, y, ALU.add, ALU.mult).then_inc(*D.done(p + "z"))
            yield p + "_newton"
            dve.wait_ge(*D.at(p + "z", i))
            dve.tensor_tensor(a, y, y, ALU.mult).then_inc(*D.done(p + "b"))
            dve.wait_ge(*D.at(p + "b", i))
            dve.scalar_tensor_tensor(b, a, -0.5 * sign * k ** 3, var, ALU.mult, ALU.mult).then_inc(*D.done(p + "c"))
            dve.wait_ge(*D.at(p + "c", i))
            dve.scalar_tensor_tensor(r, b, 1.5 * sign * k, y, ALU.add, ALU.mult).then_inc(*D.done(p + "r"))

        def norm_act(act, D, A, i, p, w):
            for u in range(UN):
                act.wait_ge(*D.at(f"{p}xc{u}", i))
                act.activation(w.sq[u], w.xc[u], ACT.Square).then_inc(*A.done(f"{p}sq{u}"))

        def dyn(buf, i, u, n=UB * C):
            return buf[:, bass.ds(i * (UN * n) + u * n, n)]

        TOP = ["m1", "eq1", "pr1", "pm1", "f1", "l2", "m2", "eq2", "pr2", "pm2", "f2"]

        def top2_dve(dve, D, i, src, w, pri, n_e):
            def one(k, val, m, pm, f):
                dve.tensor_reduce(m, val, AX.X, ALU.max).then_inc(*D.done(f"m{k}"))
                dve.wait_ge(*D.at(f"m{k}", i))
                dve.tensor_tensor(eq[:, :, 0:n_e], val, bc(m, n_e), ALU.is_equal).then_inc(*D.done(f"eq{k}"))
                dve.wait_ge(*D.at(f"eq{k}", i))
                dve.tensor_tensor(pr[:, :, 0:n_e], eq[:, :, 0:n_e], mid(pri, GB), ALU.mult).then_inc(*D.done(f"pr{k}"))
                dve.wait_ge(*D.at(f"pr{k}", i))
                dve.tensor_reduce(pm, pr[:, :, 0:n_e], AX.X, ALU.max).then_inc(*D.done(f"pm{k}"))
                dve.wait_ge(*D.at(f"pm{k}", i))
                dve.tensor_tensor(f, pr[:, :, 0:n_e], bc(pm, n_e), ALU.is_equal).then_inc(*D.done(f"f{k}"))
                dve.wait_ge(*D.at(f"f{k}", i))

            one(1, src, w[:, 0, :], w[:, 1, :], f1[:, :, 0:n_e])
            dve.scalar_tensor_tensor(wr[:, :, 0:n_e], f1[:, :, 0:n_e], -3e38, src, ALU.mult,
                                     ALU.add).then_inc(*D.done("l2"))
            yield "second"
            dve.wait_ge(*D.at("l2", i))
            one(2, wr[:, :, 0:n_e], w[:, 3, :], w[:, 4, :], f2[:, :, 0:n_e])

        SPLIT = ["wph", "wprem", "wpm", "wpl"]

        def parts_dve(dve, D, i, n_e):
            ww, rem = wr[:, :, 0:n_e], wrem[:, :, 0:n_e]
            split = wpf[:, 0:GB * n_e * PARTS].rearrange("p (b e k) -> p b e k", b=GB, e=n_e)
            w = [split[:, :, :, k] for k in range(PARTS)]
            dve.tensor_copy(w[0], ww).then_inc(*D.done("wph"))
            dve.wait_ge(*D.at("wph", i))
            dve.tensor_tensor(rem, ww, w[0], ALU.subtract).then_inc(*D.done("wprem"))
            yield "parts"
            dve.wait_ge(*D.at("wprem", i))
            dve.tensor_copy(w[1], rem).then_inc(*D.done("wpm"))
            dve.wait_ge(*D.at("wpm", i))
            dve.tensor_tensor(w[2], rem, w[1], ALU.subtract).then_inc(*D.done("wpl"))

        d1a = Steps(sem("dve_attention0"),
                    norm_names("a") + both("axn", "qT", "mxa", "mxb", "nmx", "atT", "rs", "yn", "h"),
                    loop=True)
        d1r = Steps(sem("dve_routing0"), norm_names("b") + both("bxn", "xl", "lg") + TOP
                    + ["dd", "den", "rec", "g2", "wa", "wb", "wc"] + SPLIT, loop=True)
        a1a = Steps(sem("act_attention0"), both("asq", "fT", "exp"), loop=True)
        a1r = Steps(sem("act_routing0"), both("bsq", "xh", "xt") + ["ed", "wt"], loop=True)
        t1a = Steps(sem("pe_attention0"), both("fT", "qT", "sim", "atT", "av"), loop=True)
        t1r = Steps(sem("pe_routing0"), both("xt", "lg") + ["wt"], loop=True)
        p1 = Steps(sem("pool1"), both("xt"), loop=True)

        def xtgrp(j, i, u):
            return xt[j][:, bass.ds(i * (UN * 2 * P) + u * 2 * P, 2 * P)]

        ATTENTION0 = ("centre project a_cubic a_newton scores softmax values residual").split()
        ROUTING0 = ("centre norm b_cubic b_newton logits top2 second gates weights split_weights parts").split()
        MIXING = ("experts_in layer_end c_cubic c_newton centre norm d_cubic d_newton project exp sums divide "
                  "reciprocal out_project residual").split()
        ATTENTION = ("centre norm e_cubic e_newton qkv rotate rotate_sin add_halves split head_operands maxima01 "
                     "maxima23 minus_max exp01 exp23 heads out_project rms g_cubic g_newton tokens logits shares top2 "
                     "second kept split_weights parts").split()
        ORDER0 = "bffffbbbfbfbbbfbbbf"
        ORDER1 = "bfbbbbffffbbbbfffbbfbbffffbbbbbbbbbbfbbbbbf"
        ORDER_RE = "ffbbfbbbfbbbbfbfbbfbbffbffbbbb"
        ORDER_ME = "fbbfbfbbbfffbbfbfbbfbfbfbfbbfbfbfb"
        ORDER_AE = "bffbfbbfffbfbfbfbffbfbfbffbfbfbfbffbfbbffffbbffbbfbbbbbbbbbbbbbbbbbbb"

        class Part:

            def __init__(self, names, program):
                self.left, self.program, self.at = list(names), program, names[0]

            def segment(self):
                name = self.left.pop(0)
                while self.at == name:
                    self.at = next(self.program, None)
                assert self.at is None or self.at in self.left, self.at

            def all(self):
                while self.left:
                    self.segment()

        def side_by_side(order, f, b):
            assert (order.count("f"), order.count("b")) == (len(f.left), len(b.left))
            for k in order:
                (f if k == "f" else b).segment()

        def pipelined(eng, order, front, back, front_names, back_names):
            with eng.Fori(0, IT - 1) as i:
                side_by_side(order, Part(front_names, front(eng, i + 1)), Part(back_names, back(eng, i)))

        def attention0_dve(dve, i):
            D = d1a

            def rows(u):
                return grp(dyn(h, i, u))

            def rows_ready(u):
                dve.wait_ge(group_in, i * UN + u + 1)
                dve.wait_ge(*D.at("h1", i, 1))

            norm_centre(dve, D, i, "a", norm_a, rows, rows_ready)
            yield "project"
            yield from rms_dve(dve, D, a1a, i, "a", norm_a, eps_ln, -1.0)
            for u in range(UN):
                dve.wait_ge(*D.at("ar", i))
                dve.wait_ge(*t1a.at(f"av{u}", i, 1))
                dve.tensor_tensor(grp(xr[u][:]), grp(xc[u][:]), bc(norm_a.r(u), C),
                                  ALU.mult).then_inc(*D.done(f"axn{u}"))
            yield "scores"
            for u in range(UN):
                dve.wait_ge(*t1a.at(f"qT{u}", i))
                dve.tensor_copy(qT[u][:], bank(2 * u)[:, 256:512]).then_inc(*D.done(f"qT{u}"))
            yield "softmax"
            for j, n in enumerate(("mxa", "mxb")):
                for u in range(UN):
                    dve.wait_ge(*t1a.at(f"sim{u}", i))
                    dve.tensor_reduce(mx[u][:].rearrange("p (q j) -> p j q", j=2)[:, j, :],
                                      bank(2 * u + j)[:, 0:256].rearrange("p (q s) -> p q s", q=2), AX.X,
                                      ALU.max).then_inc(*D.done(f"{n}{u}"))
            for u in range(UN):
                dve.wait_ge(*D.at(f"mxb{u}", i))
                dve.tensor_scalar(mx[u][:], mx[u][:], -1.0, None, ALU.mult).then_inc(*D.done(f"nmx{u}"))
            yield "values"
            for u in range(UN):
                dve.wait_ge(*t1a.at(f"atT{u}", i))
                dve.tensor_copy(atT[u][:], bank(2 * u)).then_inc(*D.done(f"atT{u}"))
            yield "residual"
            for u in range(UN):
                dve.wait_ge(*a1a.at(f"exp{u}", i))
                dve.reciprocal(smx[u][:], smx[u][:]).then_inc(*D.done(f"rs{u}"))
            for u in range(UN):
                dve.wait_ge(*t1a.at(f"av{u}", i))
                dve.wait_ge(*D.at(f"rs{u}", i))
                dve.tensor_tensor(grp(tmp[u][:]), grp(bank(2 * u + 1)[:, 0:256]), bc(smx[u][:], C),
                                  ALU.mult).then_inc(*D.done(f"yn{u}"))
            for u in range(UN):
                dve.wait_ge(*D.at(f"yn{u}", i))
                dve.tensor_tensor(dyn(h, i, u), dyn(h, i, u), tmp[u][:], ALU.add).then_inc(*D.done(f"h{u}"))

        def routing0_dve(dve, i):
            D = d1r

            def rows(u):
                return grp(dyn(h, i, u))

            norm_centre(dve, D, i, "b", norm_r, rows, lambda u: dve.wait_ge(*d1a.at(f"h{u}", i)))
            yield "norm"
            yield from rms_dve(dve, D, a1r, i, "b", norm_r, eps_ln, -1.0)
            for u in range(UN):
                dve.wait_ge(*D.at("br", i))
                dve.tensor_tensor(grp(dyn(x, i, u)), grp(norm_r.xc[u]), bc(norm_r.r(u), C),
                                  ALU.mult).then_inc(*D.done(f"bxn{u}"))
            yield "logits"
            for u in range(UN):
                dve.wait_ge(*a1r.at(f"xh{u}", i))
                dve.tensor_tensor(xs[u][:, :, 1, :], grp(dyn(x, i, u)), xs[u][:, :, 0, :],
                                  ALU.subtract).then_inc(*D.done(f"xl{u}"))
            yield "top2"
            for u in range(UN):
                dve.wait_ge(*t1r.at(f"lg{u}", i))
                dve.scalar_tensor_tensor(lg[:, u * UB:(u + 1) * UB, :], grp(bank(6 + u)[:, 0:UB * E0], E0), 1.0 / WS,
                                         mid(k32["gate_b"], UB), ALU.mult, ALU.add).then_inc(*D.done(f"lg{u}"))
            dve.wait_ge(*D.at("lg1", i))
            yield from top2_dve(dve, D, i, lg[:], sm, k32["pri0"], E0)
            yield "gates"
            dve.tensor_tensor(sm[:, 5, :], sm[:, 3, :], sm[:, 0, :], ALU.subtract).then_inc(*D.done("dd"))
            yield "weights"
            dve.wait_ge(*a1r.at("ed", i))
            dve.tensor_scalar(sm[:, 7, :], sm[:, 6, :], 1.0, None, ALU.add).then_inc(*D.done("den"))
            dve.wait_ge(*D.at("den", i))
            dve.reciprocal(sm[:, 8, :], sm[:, 7, :]).then_inc(*D.done("rec"))
            dve.wait_ge(*D.at("rec", i))
            dve.tensor_tensor(sm[:, 9, :], sm[:, 8, :], sm[:, 6, :], ALU.mult).then_inc(*D.done("g2"))
            dve.wait_ge(*D.at("g2", i))
            dve.tensor_tensor(f1[:], f1[:], bc(sm[:, 8, :], E0), ALU.mult).then_inc(*D.done("wa"))
            dve.tensor_tensor(f2[:], f2[:], bc(sm[:, 9, :], E0), ALU.mult).then_inc(*D.done("wb"))
            dve.wait_ge(*D.at("wb", i))
            dve.tensor_tensor(wr[:], f1[:], f2[:], ALU.add).then_inc(*D.done("wc"))
            dve.wait_ge(*D.at("wc", i))
            yield "split_weights"
            dve.wait_ge(*t1r.at("wt", i, 1))
            yield from parts_dve(dve, D, i, E0)

        def attention0_act(act, i):
            A = a1a

            norm_act(act, d1a, A, i, "a", norm_a)
            yield "a_newton"
            for u in range(UN):
                act.wait_ge(*t1a.at(f"fT{u}", i))
                act.activation(fT[u][:], bank(2 * u)[:, 0:256], ACT.Copy).then_inc(*A.done(f"fT{u}"))
            yield "softmax"
            for u in range(UN):
                act.wait_ge(*d1a.at(f"nmx{u}", i))
                for k in range(UB):
                    last = act.activation(at[u][:, k, :], bank(2 * u + k % 2)[:, k // 2 * P:k // 2 * P + P],
                                          ACT.Exp, bias=mx[u][:, k:k + 1], accum_out=smx[u][:, k:k + 1])
                last.then_inc(*A.done(f"exp{u}"))

        def routing0_act(act, i):
            A = a1r

            norm_act(act, d1r, A, i, "b", norm_r)
            yield "b_newton"
            for u in range(UN):
                act.wait_ge(*d1r.at(f"bxn{u}", i))
                act.activation(xs[u][:, :, 0, :], grp(dyn(x, i, u)), ACT.Copy).then_inc(*A.done(f"xh{u}"))
            yield "logits"
            for u in range(UN):
                act.wait_ge(*t1r.at(f"xt{u}", i))
                act.wait_ge(*p1.at(f"xt{u}", i, 1))
                act.activation(xt16[u][:].rearrange("p b t -> p (b t)"), bank(4 + u, FP16)[:, 0:512],
                               ACT.Copy).then_inc(*A.done(f"xt{u}"))
            yield "gates"
            act.wait_ge(*d1r.at("dd", i))
            act.activation(sm[:, 6, :], sm[:, 5, :], ACT.Exp).then_inc(*A.done("ed"))
            yield "parts"
            act.wait_ge(*t1r.at("wt", i))
            act.activation(wt[:, bass.ds(i * 512, 512)], bank(4, BF16)[0:2 * E0 * PARTS, 0:512],
                           ACT.Copy).then_inc(*A.done("wt"))

        def tokens_pool(pool, i):
            for u in range(UN):
                pool.wait_ge(*a1r.at(f"xt{u}", i))
                for j in range(2):
                    last = pool.tensor_copy(xtgrp(j, i, u).rearrange("p (q t) -> p q t", q=2),
                                            xt16[u][:].rearrange("p (q j) t -> p j q t", j=2)[:, j])
                last.then_inc(*p1.done(f"xt{u}"))

        def routing0_pool(pool, i):
            yield "logits"
            tokens_pool(pool, i)

        def attention0_pe(pe, i):
            T = t1a

            yield "a_newton"
            for u in range(UN):
                pe.wait_ge(*d1a.at(f"axn{u}", i))
                for q in range(2):
                    last = pe.transpose(bank(2 * u)[:, q * P:q * P + P], xr[u][:, q * P:q * P + P], k32["ident"])
                last.then_inc(*T.done(f"fT{u}"))
            for u in range(UN):
                pe.wait_ge(*a1a.at(f"fT{u}", i))
                pe.matmul(bank(2 * u)[:, 256:512], m2[:], fT[u][:], start=True, stop=True).then_inc(*T.done(f"qT{u}"))
            yield "scores"
            for u in range(UN):
                pe.wait_ge(*d1a.at(f"qT{u}", i))
                for q in range(2):
                    for j in range(2):
                        r, c = slice(C * j, C * j + C), slice(q * P, q * P + P)
                        last = pe.matmul(bank(2 * u + j)[:, c], qT[u][r, c], fT[u][r, c], start=True, stop=True)
                last.then_inc(*T.done(f"sim{u}"))
            yield "values"
            for u in range(UN):
                pe.wait_ge(*a1a.at(f"exp{u}", i))
                for k in range(UB):
                    last = pe.transpose(bank(2 * u)[:, k * P:k * P + P], at[u][:, k, :], k32["ident"])
                last.then_inc(*T.done(f"atT{u}"))
            for u in range(UN):
                pe.wait_ge(*d1a.at(f"atT{u}", i))
                for k in range(UB):
                    last = pe.matmul(bank(2 * u + 1)[:, k * C:k * C + C], atT[u][:, k * P:k * P + P],
                                     xr[u][:, k * C:k * C + C],
                                     start=True, stop=True)
                last.then_inc(*T.done(f"av{u}"))

        def routing0_pe(pe, i):
            T = t1r

            yield "logits"
            for u in range(UN):
                pe.wait_ge(*d1r.at(f"xl{u}", i))
                for k in range(UB):
                    last = pe.transpose(bank(4 + u, FP16)[:, k * P:k * P + P],
                                        xs[u][:, k].rearrange("p a c -> p (a c)"),
                                        k16["ident16"])
                last.then_inc(*T.done(f"xt{u}"))
            for u in range(UN):
                pe.wait_ge(*a1r.at(f"xt{u}", i))
                for k in range(UB):
                    for w in (gh, gl):
                        last = pe.matmul(bank(6 + u)[:, k * E0:k * E0 + E0], xt16[u][:, k, :], w[:], start=w is gh,
                                         stop=w is gl)
                last.then_inc(*T.done(f"lg{u}"))
            yield "parts"
            pe.wait_ge(*d1r.at("wpl", i))
            for q in range(GB // 2):
                last = pe.transpose(bank(4, BF16)[0:2 * E0 * PARTS, q * P:q * P + P],
                                    wp0[:, 2 * q:2 * q + 2].rearrange("p b e k -> p (b e k)"), identb[:])
            last.then_inc(*T.done("wt"))

        N = 512
        hidden = sb("hidden", [P, 4 * N])
        HB = 4
        hid = [[b[:, (2 * k + j) * N:(2 * k + j + 1) * N] for j in range(2)] for b in (hidden, w1s) for k in range(2)]
        wbs = [sb(f"wbs{k}", [P, N]) for k in range(2)]
        yw = [sb(f"yw{k}", [P, N]) for k in range(2)]
        accs = sb("accs", [P, N])

        def before(S, name, e, back, i, n):
            return S.at(f"{name}{e - back}", i) if e >= back else S.at(f"{name}{e - back + n}", i, 1)

        SLOTS = [f"slot{s}" for s in range(E0 + 3)]

        def slot(k, n):
            return [k] if 0 <= k < n else []

        def slots(stages, n, names):
            return [f"{name}{e}" for s in range(n) for name, lag in stages for e in slot(s - lag, names)]

        t2 = Steps(sem("pe2"), slots([("z0_", 0), ("z1_", 0), ("wb", 2), ("y", 2)], E0 + 3, E0), loop=True)
        a2 = Steps(sem("act2"), slots([("hid", 1), ("wb", 3)], E0 + 3, E0), loop=True)
        d2 = Steps(sem("dve2"), slots([("hid", 1), ("yw", 3)], E0 + 3, E0), loop=True)
        p2 = Steps(sem("pool2"), [f"acc{e}" for e in range(E0)], loop=True)

        class Banks:

            def __init__(self, first, ring):
                self.first, self.ring = first, ring

            def z(self, e, j):
                return bank(self.first + 4 * (e % self.ring) + j)

            def wb(self, e):
                return bank(self.first + 4 * (e % self.ring) + 2)

            def y(self, e):
                return bank(self.first + 4 * (e % self.ring) + 3)

        def experts0_pe(pe, i, banks):
            T, r = t2, banks.ring
            for s, name in enumerate(SLOTS):
                yield name
                for e in slot(s, E0):
                    for j in range(2):
                        pe.wait_ge(*before(d2 if j else a2, "hid", e, r, i, E0))
                        if e == j == 0:
                            pe.wait_ge(*p1.at("xt1", i))
                        for w in (w1h, w1l):
                            last = pe.matmul(banks.z(e, j), w[:, e * F0:(e + 1) * F0], xt[j][:, bass.ts(i, N)],
                                             start=w is w1h, stop=w is w1l)
                        last.then_inc(*T.done(f"z{j}_{e}"))
                for f in slot(s - 2, E0):
                    pe.wait_ge(*before(a2, "wb", f, r, i, E0))
                    if f == 0:
                        pe.wait_ge(*a1r.at("wt", i))
                    pe.matmul(banks.wb(f), k16["sel0"][0:2 * E0 * PARTS, f * P:(f + 1) * P], wt[:, bass.ts(i, N)],
                              start=True, stop=True).then_inc(*T.done(f"wb{f}"))
                    pe.wait_ge(*a2.at(f"hid{f}", i))
                    pe.wait_ge(*d2.at(f"yw{f - r}" if f >= r else f"hid{f}", i))
                    for j in range(2):
                        last = pe.matmul(banks.y(f)[C * j:C * j + C, :], w2s[:, f * C:(f + 1) * C], hid[f % HB][j],
                                         start=True, stop=True)
                    last.then_inc(*T.done(f"y{f}"))

        def experts0_act(act, i, banks):
            A = a2
            for s, name in enumerate(SLOTS):
                yield name
                for e in slot(s - 1, E0):
                    act.wait_ge(*t2.at(f"z0_{e}", i))
                    act.activation(hid[e % HB][0], banks.z(e, 0), ACT.Relu,
                                   bias=b1s[:, e:e + 1]).then_inc(*A.done(f"hid{e}"))
                for f in slot(s - 3, E0):
                    act.wait_ge(*t2.at(f"wb{f}", i))
                    act.wait_ge(*before(d2, "yw", f, 2, i, E0))
                    act.activation(wbs[f % 2][:], banks.wb(f), ACT.Copy).then_inc(*A.done(f"wb{f}"))

        def experts0_dve(dve, i, banks):
            D = d2
            for s, name in enumerate(SLOTS):
                yield name
                for e in slot(s - 1, E0):
                    dve.wait_ge(*t2.at(f"z1_{e}", i))
                    dve.tensor_scalar(hid[e % HB][1], banks.z(e, 1), b1s[:, e:e + 1], 0.0, ALU.add,
                                      ALU.max).then_inc(*D.done(f"hid{e}"))
                for f in slot(s - 3, E0):
                    dve.wait_ge(*t2.at(f"y{f}", i))
                    dve.wait_ge(*a2.at(f"wb{f}", i))
                    dve.wait_ge(*before(p2, "acc", f, 2, i, E0))
                    dve.scalar_tensor_tensor(yw[f % 2][:], banks.y(f), b2s[:, f:f + 1], wbs[f % 2][:], ALU.add,
                                             ALU.mult).then_inc(*D.done(f"yw{f}"))

        def sum_expert(pool, S, D, ne, e, i):
            pool.wait_ge(*D.at(f"yw{e}", i))
            pool.wait_ge(*before(S, "acc", e, 1, i, ne))
            if e == 0:
                pool.sem_inc(waited["pool"], 1)
                pool.tensor_copy(accs[:], yw[0][:]).then_inc(*S.done("acc0"))
            elif e < ne - 1:
                pool.tensor_tensor(accs[:], accs[:], yw[e % 2][:], ALU.add).then_inc(*S.done(f"acc{e}"))
            else:
                pool.sem_inc(waited["pool"], 1)
                pool.tensor_tensor(acc[:, bass.ts(i, N)], accs[:], yw[e % 2][:], ALU.add).then_inc(*S.done(f"acc{e}"))

        def experts0_pool(pool, i, banks):
            for s, name in enumerate(SLOTS):
                yield name
                for e in slot(s - 3, E0):
                    sum_expert(pool, p2, d2, E0, e, i)

        ar = qT
        xp = [sb(f"xp{u}", [P, UB, L + 1], FP16) for u in range(UN)]
        rT = [sb(f"rT{u}", [P, 2 * P]) for u in range(UN)]
        ra, rb = ([sb(f"{n}{u}", [P, UB, 96]) for u in range(UN)] for n in ("ra", "rb"))
        qr = [sb(f"qr{u}", [P, UB * NH, HD]) for u in range(UN)]
        kr = [sb(f"kr{u}", [P, UB * NKV, HD]) for u in range(UN)]
        qst = [sb(f"qst{u}", [P, UB * NH, 2, 2, HD], FP16) for u in range(UN)]
        kst = [sb(f"kst{u}", [P, UB * NKV, 2, 2, 2, HD], FP16) for u in range(UN)]
        va = [sb(f"va{u}", [P, UB, NKV, 32]) for u in range(UN)]
        qb = [sb(f"qb{u}", [P, UB * NKV, 2, P], FP16) for u in range(UN)]
        kd = [sb(f"kd{u}", [P, UB * NKV * P], FP16) for u in range(UN)]
        mh = [sb(f"mh{u}", [P, UB * NH]) for u in range(UN)]
        mrem = [sb(f"mrem{u}", [P, UB * NH]) for u in range(UN)]
        mp = [sb(f"mp{u}", [P, 2, UB * NH, PARTS], BF16) for u in range(UN)]
        mT = [sb(f"mT{u}", [UB * NH * PARTS, P], BF16) for u in range(UN)]
        ex = [grp(w1s[:], NH * P), grp(hidden[:], NH * P)]
        ot = atT
        quarters = [b[:].bitcast(F32)[:, k * UB * C:(k + 1) * UB * C] for b in (w1h, w1l) for k in range(4)]
        tmp2, xc2, sq2, rT2 = (quarters[2 * k:2 * k + 2] for k in range(4))
        norm_b = Norm("st_b", xc2, sq2)
        xs2 = [fT[u][:].bitcast(FP16).rearrange("p (b a c) -> p b a c", b=UB, a=2) for u in range(UN)]
        yt = [at[u][:].rearrange("p b t -> p (b t)")[:, 0:UB * C] for u in range(UN)]
        rc = [sb(f"rc{u}", [P, UB * NH]) for u in range(UN)]

        dm = Steps(sem("dve_mixing"), both("y") + norm_names("c") + both("cx", "h") + norm_names("d")
                   + both("dxn", "dl", "kc", "kv", "den", "rden", "rw", "ho"), loop=True)
        am = Steps(sem("act_mixing"), both("csq", "dsq", "dh", "xp", "er", "ek", "rT"), loop=True)
        tm = Steps(sem("pe_mixing"), both("aT", "dx", "kvr", "sum", "rT", "wo"), loop=True)
        qm = Steps(sem("pool_mixing"), both("ar", "hb", "cg"), loop=True)
        da = Steps(sem("dve_attention"), norm_names("e")
                   + both("hn", "fl", "ra", "rb", "qr", "kr", "ql", "kl", "qb", "kd", "mx0", "mx1", "mx2", "mx3", "mh",
                          "mrem", "mm", "ml", "rc", "yt", "xm") + rms_names("g") + both("gf", "gl", "lg")
                   + ["sx", "ls", "se", "rse", "pb"] + TOP + ["d0", "d1", "d2", "ff", "fp", "wc"] + SPLIT, loop=True)
        aa = Steps(sem("act_attention"),
                   both("esq", "fh", "xt", "va", "qh", "kh", "qb", "mT", "ex0", "ex1", "ex2", "ex3", "ot",
                                              "yT", "gsq", "gh", "xt3") + ["es", "wt"], loop=True)
        ta = Steps(sem("pe_attention"),
                   both("fx", "qkv", "qT", "s0", "s1", "s2", "s3", "mT", "t0", "t1", "t2", "t3", "oT", "o",
                                             "yT", "wo1", "gx", "lg") + ["wt"], loop=True)
        qa = Steps(sem("pool_attention"), both("ex", "xt"), loop=True)
        p3 = Steps(sem("pool3"), ["z0", "z1", "z2", "z3", "z4", "z5"], loop=False)

        def mixing_dve(dve, i):
            D = dm

            def state(u):
                return grp(dyn(h, i, u))

            def kvr(u, q, m):
                return bank(2 * u + q)[:, 0:2 * KVR].rearrange("p (b n) -> p b n", b=2)[:, :, m * C:(m + 1) * C]

            for u in range(UN):
                dve.wait_ge(*tm.at(f"aT{u}", i))
                dve.wait_ge(*D.at("ho1", i, 1))
                dve.scalar_tensor_tensor(tmp[u][:], bank(2 * u)[:, 0:256], 1.0 / WS, dyn(x, i, u), ALU.mult,
                                         ALU.add).then_inc(*D.done(f"y{u}"))
            norm_centre(dve, D, i, "c", norm_a, lambda u: grp(tmp[u][:]), lambda u: dve.wait_ge(*D.at(f"y{u}", i)))
            yield "layer_end"
            yield from rms_dve(dve, D, am, i, "c", norm_a, eps_ln, -1.0)
            for u in range(UN):
                dve.wait_ge(*D.at("cr", i))
                dve.wait_ge(*qm.at(f"cg{u}", i))
                dve.tensor_tensor(grp(tmp[u][:]), grp(tmp[u][:]), bc(norm_a.r(u), C),
                                  ALU.mult).then_inc(*D.done(f"cx{u}"))
            for u in range(UN):
                dve.wait_ge(*D.at(f"cx{u}", i))
                dve.tensor_tensor(dyn(h, i, u), dyn(h, i, u), tmp[u][:], ALU.add).then_inc(*D.done(f"h{u}"))
            yield "centre"
            norm_centre(dve, D, i, "d", norm_a, state, lambda u: dve.wait_ge(*D.at(f"h{u}", i)))
            yield "norm"
            yield from rms_dve(dve, D, am, i, "d", norm_a, eps_ln, -1.0)
            for u in range(UN):
                dve.wait_ge(*D.at("dr", i))
                dve.tensor_tensor(grp(xr[u][:]), grp(xc[u][:]), bc(norm_a.r(u), C),
                                  ALU.mult).then_inc(*D.done(f"dxn{u}"))
            yield "project"
            for u in range(UN):
                dve.wait_ge(*am.at(f"dh{u}", i))
                dve.tensor_tensor(xs[u][:, :, 1, :], grp(xr[u][:]), xs[u][:, :, 0, :],
                                  ALU.subtract).then_inc(*D.done(f"dl{u}"))
            yield "exp"
            for u in range(UN):
                dve.wait_ge(*tm.at(f"kvr{u}", i))
                for q in range(2):
                    last = dve.tensor_scalar(grp(kc[u][:, q * P:(q + 1) * P]), kvr(u, q, 0), 30.0 * WS, -60.0 * WS,
                                             ALU.min,
                                             ALU.max)
                last.then_inc(*D.done(f"kc{u}"))
            yield "sums"
            for u in range(UN):
                dve.wait_ge(*am.at(f"ek{u}", i))
                for q in range(2):
                    last = dve.tensor_tensor(grp(kv[u][:, q * P:(q + 1) * P]), kvr(u, q, 1),
                                             grp(ek[u][:, q * P:(q + 1) * P]),
                                             ALU.mult)
                last.then_inc(*D.done(f"kv{u}"))
            yield "divide"
            for u in range(UN):
                dve.wait_ge(*tm.at(f"sum{u}", i))
                dve.scalar_tensor_tensor(er[u][:], er[u][:], 1.0, bank(2 * u)[:, 0:256], ALU.add,
                                         ALU.mult).then_inc(*D.done(f"den{u}"))
            yield "reciprocal"
            for u in range(UN):
                dve.wait_ge(*D.at(f"den{u}", i))
                dve.reciprocal(er[u][:], er[u][:]).then_inc(*D.done(f"rden{u}"))
            yield "out_project"
            for u in range(UN):
                dve.wait_ge(*D.at(f"rden{u}", i))
                dve.tensor_tensor(rw[u][:], bank(2 * u)[:, 256:512], er[u][:], ALU.mult).then_inc(*D.done(f"rw{u}"))
            yield "residual"
            for u in range(UN):
                dve.wait_ge(*tm.at(f"wo{u}", i))
                dve.scalar_tensor_tensor(dyn(h, i, u), bank(2 * u + 1)[:, 256:512], 1.0 / WS, dyn(h, i, u), ALU.mult,
                                         ALU.add).then_inc(*D.done(f"ho{u}"))

        def attention_dve(dve, i):
            D = da

            def state(u):
                return grp(dyn(h, i, u))

            def qkv(u):
                return bank(5 + 2 * u).rearrange("p (b n) -> p b n", b=UB)

            def halves(ap):
                return ap.rearrange("p b (g s d) -> p b g s d", g=NH + NKV, s=2)

            def table(name, s):
                return k32[name].rearrange("p (g s d) -> p g s d", g=NH + NKV, s=2)[:, :, s, :].unsqueeze(1) \
                    .to_broadcast([P, UB, NH + NKV, HD // 2])

            def heads(u):
                return bank(5 + 2 * u).rearrange("p (g n) -> p g n", n=32)

            l8, w8 = lg[:, :, 0:E1], wr[:, :, 0:E1]

            norm_centre(dve, D, i, "e", norm_b, state, lambda u: dve.wait_ge(*dm.at(f"ho{u}", i)))
            yield "norm"
            yield from rms_dve(dve, D, aa, i, "e", norm_b, eps_ln, -1.0, rms_too=True)
            for u in range(UN):
                dve.wait_ge(*D.at("er", i))
                dve.tensor_tensor(grp(tmp2[u]), grp(norm_b.xc[u]), bc(norm_b.r(u, 1), C),
                                  ALU.mult).then_inc(*D.done(f"hn{u}"))
            yield "qkv"
            for u in range(UN):
                dve.wait_ge(*aa.at(f"fh{u}", i))
                dve.tensor_tensor(xs2[u][:, :, 1, :], grp(tmp2[u]), xs2[u][:, :, 0, :],
                                  ALU.subtract).then_inc(*D.done(f"fl{u}"))
            yield "rotate"
            for u in range(UN):
                dve.wait_ge(*aa.at(f"va{u}", i))
                dve.tensor_tensor(ra[u][:], qkv(u)[:, :, 0:96], mid(k32["cos"], UB),
                                  ALU.mult).then_inc(*D.done(f"ra{u}"))
            yield "rotate_sin"
            for u in range(UN):
                for s in range(2):
                    last = dve.tensor_tensor(halves(rb[u][:])[:, :, :, s, :],
                                             halves(qkv(u)[:, :, 0:96])[:, :, :, 1 - s, :],
                                             table("sin", s), ALU.mult)
                last.then_inc(*D.done(f"rb{u}"))
            yield "add_halves"
            for u in range(UN):
                dve.wait_ge(*D.at(f"rb{u}", i))
                dve.tensor_tensor(qr[u][:].rearrange("p (b g) d -> p b (g d)", b=UB), ra[u][:, :, 0:C],
                                  rb[u][:, :, 0:C],
                                  ALU.add).then_inc(*D.done(f"qr{u}"))
            for u in range(UN):
                dve.tensor_tensor(kr[u][:].rearrange("p (b g) d -> p b (g d)", b=UB), ra[u][:, :, C:96],
                                  rb[u][:, :, C:96],
                                  ALU.add).then_inc(*D.done(f"kr{u}"))
            yield "split"
            for u in range(UN):
                dve.wait_ge(*aa.at(f"qh{u}", i))
                q2 = qr[u][:].unsqueeze(2).to_broadcast([P, UB * NH, 2, HD])
                dve.tensor_tensor(qst[u][:, :, :, 1, :], q2, qst[u][:, :, :, 0, :],
                                  ALU.subtract).then_inc(*D.done(f"ql{u}"))
            for u in range(UN):
                dve.wait_ge(*aa.at(f"kh{u}", i))
                k2 = kr[u][:].unsqueeze(2).to_broadcast([P, UB * NKV, 2, HD])
                for s in range(2):
                    last = dve.tensor_tensor(kst[u][:, :, s, 1, :, :], k2, kst[u][:, :, s, 0, :, :], ALU.subtract)
                last.then_inc(*D.done(f"kl{u}"))
            yield "head_operands"
            for u in range(UN):
                dve.wait_ge(*ta.at(f"qT{u}", i))
                dve.tensor_copy(qb[u][C:P, :, 1, :], bank(4 + 2 * u, FP16)[C:P, :].rearrange("p (g t) -> p g t", t=P)
                                ).then_inc(*D.done(f"qb{u}"))
            for u in range(UN):
                dve.tensor_copy(kd[u][:], bank(5 + 2 * u, FP16)).then_inc(*D.done(f"kd{u}"))
            yield "maxima01"
            for k in range(0, 2):
                for u in range(UN):
                    dve.wait_ge(*ta.at(f"s{k}{u}", i))
                    dve.tensor_reduce(mh[u][:, k * NH:(k + 1) * NH], grp(bank(4 + 2 * u + k % 2), P), AX.X,
                                      ALU.max).then_inc(*D.done(f"mx{k}{u}"))
            yield "maxima23"
            for k in range(2, 4):
                for u in range(UN):
                    dve.wait_ge(*ta.at(f"s{k}{u}", i))
                    dve.tensor_reduce(mh[u][:, k * NH:(k + 1) * NH], grp(bank(4 + 2 * u + k % 2), P), AX.X,
                                      ALU.max).then_inc(*D.done(f"mx{k}{u}"))
            yield "minus_max"
            for u in range(UN):
                dve.wait_ge(*D.at(f"mx3{u}", i))
                dve.tensor_scalar(mp[u][:, 0, :, 0], mh[u][:], -1.0, None, ALU.mult).then_inc(*D.done(f"mh{u}"))
            for u in range(UN):
                dve.wait_ge(*D.at(f"mh{u}", i))
                dve.scalar_tensor_tensor(mrem[u][:], mh[u][:], -1.0, mp[u][:, 0, :, 0], ALU.mult,
                                         ALU.subtract).then_inc(*D.done(f"mrem{u}"))
            for u in range(UN):
                dve.wait_ge(*D.at(f"mrem{u}", i))
                dve.tensor_copy(mp[u][:, 0, :, 1], mrem[u][:]).then_inc(*D.done(f"mm{u}"))
            for u in range(UN):
                dve.wait_ge(*D.at(f"mm{u}", i))
                dve.tensor_tensor(mp[u][:, 0, :, 2], mrem[u][:], mp[u][:, 0, :, 1],
                                  ALU.subtract).then_inc(*D.done(f"ml{u}"))
            yield "heads"
            for u in range(UN):
                dve.wait_ge(*ta.at(f"o{u}", i))
                dve.reciprocal(rc[u][:], heads(u)[:, :, HD]).then_inc(*D.done(f"rc{u}"))
            for u in range(UN):
                dve.wait_ge(*D.at(f"rc{u}", i))
                dve.tensor_tensor(grp(yt[u], HD), heads(u)[:, :, 0:HD], bc(rc[u][:], HD),
                                  ALU.mult).then_inc(*D.done(f"yt{u}"))
            yield "out_project"
            for u in range(UN):
                dve.wait_ge(*ta.at(f"wo1{u}", i))
                dve.wait_ge(*qa.at(f"ex{u}", i))
                dve.tensor_tensor(dyn(x, i, u), bank(4 + 2 * u)[:, 256:512], dyn(x, i, u),
                                  ALU.add).then_inc(*D.done(f"xm{u}"))
            yield "rms"
            yield from rms_dve(dve, D, aa, i, "g", norm_b, eps_rms)
            for u in range(UN):
                dve.wait_ge(*D.at("gr", i))
                dve.tensor_tensor(grp(tmp2[u]), grp(dyn(x, i, u)), bc(norm_b.r(u), C),
                                  ALU.mult).then_inc(*D.done(f"gf{u}"))
            yield "tokens"
            for u in range(UN):
                dve.wait_ge(*aa.at(f"gh{u}", i))
                dve.tensor_tensor(xs2[u][:, :, 1, :], grp(tmp2[u]), xs2[u][:, :, 0, :],
                                  ALU.subtract).then_inc(*D.done(f"gl{u}"))
            yield "logits"
            for u in range(UN):
                dve.wait_ge(*ta.at(f"lg{u}", i))
                dve.tensor_scalar(l8[:, u * UB:(u + 1) * UB, :], grp(bank(4 + 2 * u)[:, 0:UB * E1], E1), 1.0 / WS, None,
                                  ALU.mult).then_inc(*D.done(f"lg{u}"))
            dve.wait_ge(*D.at("lg1", i))
            dve.tensor_reduce(sm[:, 5, :], l8, AX.X, ALU.max).then_inc(*D.done("sx"))
            dve.wait_ge(*D.at("sx", i))
            dve.tensor_tensor(l8, l8, bc(sm[:, 5, :], E1), ALU.subtract).then_inc(*D.done("ls"))
            yield "shares"
            dve.wait_ge(*aa.at("es", i))
            dve.tensor_reduce(sm[:, 6, :], w8, AX.X, ALU.add).then_inc(*D.done("se"))
            dve.wait_ge(*D.at("se", i))
            dve.reciprocal(sm[:, 7, :], sm[:, 6, :]).then_inc(*D.done("rse"))
            dve.wait_ge(*D.at("rse", i))
            dve.tensor_tensor(l8, w8, bc(sm[:, 7, :], E1), ALU.mult).then_inc(*D.done("pb"))
            dve.wait_ge(*D.at("pb", i))
            yield "top2"
            yield from top2_dve(dve, D, i, l8, sm, k32["pri1"], E1)
            yield "kept"
            dve.tensor_tensor(sm[:, 8, :], sm[:, 0, :], sm[:, 3, :], ALU.add).then_inc(*D.done("d0"))
            dve.wait_ge(*D.at("d0", i))
            dve.tensor_scalar(sm[:, 9, :], sm[:, 8, :], 1e-9, None, ALU.add).then_inc(*D.done("d1"))
            dve.wait_ge(*D.at("d1", i))
            dve.reciprocal(sm[:, 10, :], sm[:, 9, :]).then_inc(*D.done("d2"))
            ff = f1[:, :, 0:E1]
            dve.tensor_tensor(ff, ff, f2[:, :, 0:E1], ALU.add).then_inc(*D.done("ff"))
            dve.wait_ge(*D.at("ff", i))
            dve.tensor_tensor(ff, ff, l8, ALU.mult).then_inc(*D.done("fp"))
            dve.wait_ge(*D.at("fp", i))
            dve.tensor_tensor(w8, ff, bc(sm[:, 10, :], E1), ALU.mult).then_inc(*D.done("wc"))
            dve.wait_ge(*D.at("wc", i))
            yield "split_weights"
            dve.wait_ge(*ta.at("wt", i, 1))
            yield from parts_dve(dve, D, i, E1)

        def mixing_act(act, i):
            A = am

            norm_act(act, dm, A, i, "c", norm_a)
            yield "centre"
            norm_act(act, dm, A, i, "d", norm_a)
            yield "d_newton"
            for u in range(UN):
                act.wait_ge(*dm.at(f"dxn{u}", i))
                act.activation(xs[u][:, :, 0, :], grp(xr[u][:]), ACT.Copy).then_inc(*A.done(f"dh{u}"))
            yield "project"
            for u in range(UN):
                act.wait_ge(*tm.at(f"dx{u}", i))
                act.activation(xp[u][:, :, 1:L + 1], grp(bank(2 * u + 1, FP16)[:, 0:512], P),
                               ACT.Copy).then_inc(*A.done(f"xp{u}"))
            yield "exp"
            for u in range(UN):
                act.wait_ge(*dm.at(f"kc{u}", i))
                for q in range(2):
                    r = bank(2 * u + q)[:, 0:2 * KVR].rearrange("p (b n) -> p b n", b=2)[:, :, 2 * C:3 * C]
                    last = act.activation(grp(er[u][:, q * P:(q + 1) * P]), r, ACT.Exp, scale=-1.0 / WS)
                last.then_inc(*A.done(f"er{u}"))
            for u in range(UN):
                act.activation(ek[u][:], kc[u][:], ACT.Exp, scale=1.0 / WS).then_inc(*A.done(f"ek{u}"))
            yield "out_project"
            for u in range(UN):
                act.wait_ge(*tm.at(f"rT{u}", i))
                act.activation(rT[u][:], bank(2 * u + 1)[:, 0:256], ACT.Copy).then_inc(*A.done(f"rT{u}"))

        def attention_act(act, i):
            A = aa

            norm_act(act, da, A, i, "e", norm_b)
            yield "e_newton"
            for u in range(UN):
                act.wait_ge(*da.at(f"hn{u}", i))
                act.activation(xs2[u][:, :, 0, :], grp(tmp2[u]), ACT.Copy).then_inc(*A.done(f"fh{u}"))
            yield "qkv"
            for u in range(UN):
                act.wait_ge(*ta.at(f"fx{u}", i))
                act.wait_ge(*qa.at(f"xt{u}", i, 1))
                act.activation(xt16[u][:].rearrange("p b t -> p (b t)"), bank(4 + 2 * u, FP16)[:, 0:512],
                               ACT.Copy).then_inc(*A.done(f"xt{u}"))
            for u in range(UN):
                act.wait_ge(*ta.at(f"qkv{u}", i))
                v = bank(5 + 2 * u).rearrange("p (b n) -> p b n", b=UB)[:, :, 96:P]
                v = v.rearrange("p b (g d) -> p b g d", g=NKV)
                act.activation(va[u][:, :, :, 0:HD], v, ACT.Copy, scale=1.0 / WS).then_inc(*A.done(f"va{u}"))
            yield "add_halves"
            for u in range(UN):
                act.wait_ge(*da.at(f"qr{u}", i))
                q2 = qr[u][:].unsqueeze(2).to_broadcast([P, UB * NH, 2, HD])
                act.activation(qst[u][:, :, :, 0, :], q2, ACT.Copy).then_inc(*A.done(f"qh{u}"))
            for u in range(UN):
                act.wait_ge(*da.at(f"kr{u}", i))
                k2 = kr[u][:].unsqueeze(2).to_broadcast([P, UB * NKV, 2, HD])
                for s in range(2):
                    last = act.activation(kst[u][:, :, s, 0, :, :], k2, ACT.Copy)
                last.then_inc(*A.done(f"kh{u}"))
            yield "head_operands"
            for u in range(UN):
                act.wait_ge(*ta.at(f"qT{u}", i))
                act.activation(qb[u][0:C, :, 0, :], bank(4 + 2 * u, FP16)[0:C, :].rearrange("p (g t) -> p g t", t=P),
                               ACT.Copy).then_inc(*A.done(f"qb{u}"))
            yield "minus_max"
            for u in range(UN):
                act.wait_ge(*ta.at(f"mT{u}", i))
                act.activation(mT[u][:], bank(4 + 2 * u, BF16)[0:UB * NH * PARTS, 0:P],
                               ACT.Copy).then_inc(*A.done(f"mT{u}"))
            yield "exp01"
            for k in range(0, 2):
                for u in range(UN):
                    act.wait_ge(*ta.at(f"t{k}{u}", i))
                    act.activation(ex[u][:, k, :], bank(4 + 2 * u + k % 2), ACT.Exp).then_inc(*A.done(f"ex{k}{u}"))
            yield "exp23"
            for k in range(2, 4):
                for u in range(UN):
                    act.wait_ge(*ta.at(f"t{k}{u}", i))
                    act.activation(ex[u][:, k, :], bank(4 + 2 * u + k % 2), ACT.Exp).then_inc(*A.done(f"ex{k}{u}"))
            for u in range(UN):
                act.wait_ge(*ta.at(f"oT{u}", i))
                act.activation(ot[u][:], bank(4 + 2 * u), ACT.Copy).then_inc(*A.done(f"ot{u}"))
            yield "out_project"
            for u in range(UN):
                act.wait_ge(*ta.at(f"yT{u}", i))
                act.activation(rT2[u], bank(4 + 2 * u)[:, 0:256], ACT.Copy).then_inc(*A.done(f"yT{u}"))
            yield "rms"
            for u in range(UN):
                act.wait_ge(*da.at(f"xm{u}", i))
                act.activation(norm_b.sq[u], dyn(x, i, u), ACT.Square).then_inc(*A.done(f"gsq{u}"))
            yield "tokens"
            for u in range(UN):
                act.wait_ge(*da.at(f"gf{u}", i))
                act.activation(xs2[u][:, :, 0, :], grp(tmp2[u]), ACT.Copy).then_inc(*A.done(f"gh{u}"))
            for u in range(UN):
                act.wait_ge(*ta.at(f"gx{u}", i))
                act.activation(xt16[u][:].rearrange("p b t -> p (b t)"), bank(5 + 2 * u, FP16)[:, 0:512],
                               ACT.Copy).then_inc(*A.done(f"xt3{u}"))
            yield "logits"
            act.wait_ge(*da.at("ls", i))
            act.activation(wr[:, :, 0:E1], lg[:, :, 0:E1], ACT.Exp).then_inc(*A.done("es"))
            yield "parts"
            act.wait_ge(*ta.at("wt", i))
            act.activation(wt[:, bass.ts(i, N)], bank(5, BF16)[0:2 * E0 * PARTS, 0:512],
                           ACT.Copy).then_inc(*A.done("wt"))

        def pool3_zeros(pool):
            for u in range(UN):
                last = pool.memset(xp[u][:, :, 0:1], 0.0)
            last.then_inc(*p3.done("z0"))
            for u in range(UN):
                last = pool.memset(va[u][:], 0.0)
            last.then_inc(*p3.done("z1"))
            pool.wait_ge(*p3.at("z1"))
            for u in range(UN):
                last = pool.memset(va[u][:, :, :, HD:HD + 1], 1.0)
            last.then_inc(*p3.done("z2"))
            pool.wait_ge(*p3.at("z2"))
            for u in range(UN):
                last = pool.memset(qb[u][0:C, :, 1, :], 0.0)
            last.then_inc(*p3.done("z3"))
            pool.wait_ge(*p3.at("z3"))
            for u in range(UN):
                last = pool.memset(qb[u][C:P, :, 0, :], 0.0)
            last.then_inc(*p3.done("z4"))
            pool.wait_ge(*p3.at("z4"))
            for u in range(UN):
                last = pool.memset(mp[u][:], 0.0)
            last.then_inc(*p3.done("z5"))

        def mixing_pool(pool, i):
            S = qm

            for u in range(UN):
                pool.wait_ge(*tm.at(f"aT{u}", i, 1))
                if u == 0:
                    pool.wait_ge(*p2.at(f"acc{E0 - 1}", i))
                pool.tensor_copy(ar[u][:],
                                 acc[:, bass.ds(i * UN * 2 * P + u * 2 * P, 2 * P)]).then_inc(*S.done(f"ar{u}"))
            yield "c_newton"
            for u in range(UN):
                if u == 0:
                    pool.wait_ge(*d1a.at("h1", IT - 1))
                pool.tensor_tensor(grp(dyn(h, i, u)), grp(dyn(h, i, u)), mid(k32["beta"], UB),
                                   ALU.add).then_inc(*S.done(f"hb{u}"))
            for u in range(UN):
                pool.wait_ge(*dm.at(f"cxc{u}", i))
                pool.tensor_tensor(grp(tmp[u][:]), grp(xc[u][:]), mid(k32["gamma"], UB),
                                   ALU.mult).then_inc(*S.done(f"cg{u}"))

        def attention_pool(pool, i):
            S = qa

            yield "e_newton"
            for u in range(UN):
                pool.wait_ge(*da.at("er", i))
                pool.sem_inc(waited["pool"], 1)
                pool.tensor_tensor(grp(dyn(x, i, u)), grp(norm_b.xc[u]), bc(norm_b.r(u), C),
                                   ALU.mult).then_inc(*S.done(f"ex{u}"))
            yield "tokens"
            for u in range(UN):
                pool.wait_ge(*aa.at(f"xt3{u}", i))
                for j in range(2):
                    last = pool.tensor_copy(xtgrp(j, i, u).rearrange("p (q t) -> p q t", q=2),
                                            xt16[u][:].rearrange("p (q j) t -> p j q t", j=2)[:, j])
                last.then_inc(*S.done(f"xt{u}"))

        def transposes(T, u, k, dt, src, ident, name, n=UB, w=P):
            for q in range(n):
                last = nc.tensor.transpose(bank(k, dt)[:, q * w:(q + 1) * w], src(q), ident)
            last.then_inc(*T.done(f"{name}{u}"))

        def mixing_pe(pe, i):
            T = tm

            def stack(u):
                return lambda q: xs[u][:, q].rearrange("p a c -> p (a c)")

            for u in range(UN):
                pe.wait_ge(*qm.at(f"ar{u}", i))
                transposes(T, u, 2 * u, F32, lambda q: ar[u][:, q * P:(q + 1) * P], k32["ident"], "aT", 2)
            yield "project"
            for u in range(UN):
                pe.wait_ge(*dm.at(f"dl{u}", i))
                transposes(T, u, 2 * u + 1, FP16, stack(u), k16["ident16"], "dx")
            for u in range(UN):
                pe.wait_ge(*am.at(f"xp{u}", i))
                for k in range(UB):
                    dst = bank(2 * u + k // 2)[:, k % 2 * KVR:(k % 2 + 1) * KVR]
                    for n, (w, before_) in enumerate(((kvh, 0), (kvl, 0), (kvh, 1), (kvl, 1))):
                        last = pe.matmul(dst, xp[u][:, k, 1 - before_:L + 1 - before_], w[:, before_, :], start=n == 0,
                                         stop=n == 3)
                last.then_inc(*T.done(f"kvr{u}"))
            yield "sums"
            for u in range(UN):
                pe.wait_ge(*dm.at(f"kv{u}", i))
                pe.matmul(bank(2 * u)[:, 0:256], k32["tri"], ek[u][:], start=True, stop=True)
                pe.matmul(bank(2 * u)[:, 256:512], wtoep[:], kv[u][:], start=True,
                          stop=True).then_inc(*T.done(f"sum{u}"))
            yield "out_project"
            for u in range(UN):
                pe.wait_ge(*dm.at(f"rw{u}", i))
                transposes(T, u, 2 * u + 1, F32, lambda q: rw[u][:, q * P:(q + 1) * P], k32["ident"], "rT", 2)
            for u in range(UN):
                pe.wait_ge(*am.at(f"rT{u}", i))
                for q in range(2):
                    last = pe.matmul(bank(2 * u + 1)[:, 256 + q * P:256 + (q + 1) * P], rT[u][:, q * P:(q + 1) * P],
                                     k32["wo0"],
                                     start=True, stop=True)
                last.then_inc(*T.done(f"wo{u}"))

        def attention_pe(pe, i):
            T = ta

            def stack(u):
                return lambda q: xs2[u][:, q].rearrange("p a c -> p (a c)")

            def scores_ts(k):
                for u in range(UN):
                    if k == 0:
                        pe.wait_ge(*aa.at(f"qb{u}", i))
                        pe.wait_ge(*da.at(f"kd{u}", i))
                    if k > 1:
                        pe.wait_ge(*da.at(f"mx{k - 2}{u}", i))
                    dst = bank(4 + 2 * u + k % 2)
                    pe.matmul(dst, identb[:], mask_ts[:].rearrange("p h t -> p (h t)"), start=True, stop=False,
                              skip_group_check=True)
                    for n in range(NH):
                        last = pe.matmul(dst[:, n * P:(n + 1) * P], qb[u][:, NKV * k + n // 2, n % 2, :],
                                         kd[u][:, (NKV * k + n // 2) * P:(NKV * k + n // 2 + 1) * P], start=False,
                                         stop=n == NH - 1, skip_group_check=True)
                    last.then_inc(*T.done(f"s{k}{u}"))

            def scores_st(k):
                for u in range(UN):
                    if k == 0:
                        pe.wait_ge(*aa.at(f"mT{u}", i))
                    if k > 1:
                        pe.wait_ge(*aa.at(f"ex{k - 2}{u}", i))
                    dst = bank(4 + 2 * u + k % 2)
                    pe.matmul(dst, identb[:], mask_st[:].rearrange("p h t -> p (h t)"), start=True, stop=False,
                              skip_group_check=True)
                    for n in range(NH):
                        pe.matmul(dst[:, n * P:(n + 1) * P],
                                  k16["selm"][0:UB * NH * PARTS, (NH * k + n) * P:(NH * k + n + 1) * P], mT[u][:],
                                  start=False, stop=False, skip_group_check=True)
                    for g in range(NKV):
                        q = NKV * k + g
                        last = pe.matmul(dst[:, g * 256:(g + 1) * 256], kd[u][:, q * P:(q + 1) * P],
                                         qb[u][:, q].rearrange("p a t -> p (a t)"), start=False, stop=g == NKV - 1,
                                         skip_group_check=True)
                    last.then_inc(*T.done(f"t{k}{u}"))

            yield "qkv"
            for u in range(UN):
                pe.wait_ge(*da.at(f"fl{u}", i))
                transposes(T, u, 4 + 2 * u, FP16, stack(u), k16["ident16"], "fx")
            for u in range(UN):
                pe.wait_ge(*aa.at(f"xt{u}", i))
                for k in range(UB):
                    for w in (qh_, ql_):
                        last = pe.matmul(bank(5 + 2 * u)[:, k * P:(k + 1) * P], xt16[u][:, k, :], w[:], start=w is qh_,
                                         stop=w is ql_)
                last.then_inc(*T.done(f"qkv{u}"))
            yield "split"
            for u in range(UN):
                pe.wait_ge(*da.at(f"kl{u}", i))
                for g in range(UB * NKV):
                    pe.transpose(bank(4 + 2 * u, FP16)[:, g * P:(g + 1) * P],
                                 qst[u][:, 2 * g:2 * g + 2].rearrange("p g s two d -> p (g s two d)"), k16["ident16"])
                for g in range(UB * NKV):
                    last = pe.transpose(bank(5 + 2 * u, FP16)[:, g * P:(g + 1) * P],
                                        kst[u][:, g].rearrange("p a s two d -> p (a s two d)"), k16["ident16"])
                last.then_inc(*T.done(f"qT{u}"))
            yield "head_operands"
            scores_ts(0)
            scores_ts(1)
            yield "maxima01"
            scores_ts(2)
            scores_ts(3)
            yield "minus_max"
            for u in range(UN):
                pe.wait_ge(*da.at(f"ml{u}", i))
                pe.transpose(bank(4 + 2 * u, BF16)[0:2 * UB * NH * PARTS, 0:P],
                             mp[u][:].rearrange("p z a b -> p (z a b)"),
                             identb[:]).then_inc(*T.done(f"mT{u}"))
            scores_st(0)
            scores_st(1)
            yield "exp01"
            scores_st(2)
            scores_st(3)
            yield "exp23"
            for u in range(UN):
                for k in range(UB):
                    pe.wait_ge(*aa.at(f"ex{max(k, 2)}{u}", i))
                    for n in range(NH):
                        last = pe.matmul(bank(4 + 2 * u)[32 * n:32 * n + 32, k * P:(k + 1) * P], va[u][:, k, n // 2, :],
                                         ex[u][:, k, n * P:(n + 1) * P], start=True, stop=True)
                last.then_inc(*T.done(f"oT{u}"))
            yield "heads"
            for u in range(UN):
                pe.wait_ge(*aa.at(f"ot{u}", i))
                transposes(T, u, 5 + 2 * u, F32, lambda q: ot[u][:, q * P:(q + 1) * P], k32["ident"], "o")
            yield "out_project"
            for u in range(UN):
                pe.wait_ge(*da.at(f"yt{u}", i))
                transposes(T, u, 4 + 2 * u, F32, lambda q: yt[u][:, q * P:(q + 1) * P], k32["ident"], "yT", 2)
            for u in range(UN):
                pe.wait_ge(*aa.at(f"yT{u}", i))
                for q in range(2):
                    last = pe.matmul(bank(4 + 2 * u)[:, 256 + q * P:256 + (q + 1) * P], rT2[u][:, q * P:(q + 1) * P],
                                     k32["wo1"],
                                     start=True, stop=True)
                last.then_inc(*T.done(f"wo1{u}"))
            yield "tokens"
            for u in range(UN):
                pe.wait_ge(*da.at(f"gl{u}", i))
                transposes(T, u, 5 + 2 * u, FP16, stack(u), k16["ident16"], "gx")
            for u in range(UN):
                pe.wait_ge(*aa.at(f"xt3{u}", i))
                for k in range(UB):
                    for w in (rh, rl):
                        last = pe.matmul(bank(4 + 2 * u)[:, k * E1:(k + 1) * E1], xt16[u][:, k, :], w[:], start=w is rh,
                                         stop=w is rl)
                last.then_inc(*T.done(f"lg{u}"))
            yield "parts"
            pe.wait_ge(*da.at("wpl", i))
            for q in range(GB // 2):
                w = 2 * E1 * PARTS
                last = pe.transpose(bank(5, BF16)[0:2 * w, q * P:(q + 1) * P], wpf[:, q * w:(q + 2) * w], identb[:])
            last.then_inc(*T.done("wt"))

        WIDE = 13
        RING = 3
        hid1 = [b[:, k * N:(k + 1) * N] for b, n in ((mixed, 5), (a3s, 3)) for k in range(n)]
        hm = [hid1[0:2], hid1[2:4]]
        ht = [hid1[4:6], hid1[6:8]]
        sa = [a1s[:, k * N:(k + 1) * N] for k in range(RING)]
        silu_table = sb("silu_table", [P, 1])
        units = []
        for q in range(E1 // 2):
            for cols, buf in ((2 * q * FM, hm[0]), (E1 * FM + q * P, ht[q % 2]), ((2 * q + 1) * FM, hm[1])):
                units += [(cols, buf[j], j) for j in range(2)]
        NU = len(units)
        plan = []
        for q in range(E1 // 2):
            n = 6 * q
            plan += [("ab", n), ("wb", 2 * q)] + ([("y", 2 * q - 1)] if q else [])
            plan += [("ab", n + 1), ("ab", n + 2), ("ab", n + 3), ("wb", 2 * q + 1), ("ab", n + 4), ("ab", n + 5)]
            plan += [("y", 2 * q)]
        plan.append(("y", E1 - 1))
        SLOTS1 = [f"slot{k}" for k in range(len(plan) + 1)]
        t4 = Steps(sem("pe4"), [f"{a}{n}" for a, n in plan], loop=True)
        a4 = Steps(sem("act4"), [f"{'silu' if a == 'ab' else a}{n}" for a, n in plan if a != "y"], loop=True)
        d4 = Steps(sem("dve4"), [f"{'u' if a == 'ab' else 'yw'}{n}" for a, n in plan if a != "wb"], loop=True)
        p4 = Steps(sem("pool4"), [f"acc{e}" for e in range(E1)], loop=True)

        def y_bank(n):
            return bank(0 if n == E1 - 1 else 1)

        def ab_bank(n, wide, m):
            return bank(2 + 2 * (n % RING if n >= wide else 0) + m)

        def experts1_pe(pe, i, wide):
            T = t4
            for k, (kind, n) in enumerate(plan):
                yield f"slot{k}"
                if kind == "wb":
                    pe.wait_ge(*before(a4, "wb", n, 1, i, E1))
                    if n == 0:
                        pe.wait_ge(*before(d4, "yw", n, 1, i, E1))
                    pe.matmul(bank(0), k16["sel1"][0:2 * E0 * PARTS, n * P:(n + 1) * P], wt[:, bass.ts(i, N)],
                              start=True, stop=True).then_inc(*T.done(f"wb{n}"))
                elif kind == "ab":
                    cols, _, j = units[n]
                    if n < wide:
                        pe.wait_ge(*before(d4, "u", n, 1, i, NU))
                    elif wide == 0 or n - RING >= wide:
                        pe.wait_ge(*before(d4, "u", n, RING, i, NU))
                    elif n % RING == 0:
                        pe.wait_ge(*d4.at(f"u{wide - 1}", i))
                    if n == wide > 0:
                        pe.wait_ge(*aa.at("wt", IT - 1))
                    for m, (hi, lo) in enumerate(((a1h, a1l), (a3h, a3l))):
                        for w in (hi, lo):
                            last = pe.matmul(ab_bank(n, wide, m), w[:, cols:cols + P], xt[j][:, bass.ts(i, N)],
                                             start=w is hi, stop=w is lo)
                    last.then_inc(*T.done(f"ab{n}"))
                else:
                    if n == E1 - 1:
                        pe.wait_ge(*a4.at(f"wb{n}", i))
                    else:
                        pe.wait_ge(*before(d4, "yw", n, 1, i, E1))
                    pe.wait_ge(*d4.at(f"u{6 * (n // 2) + (5 if n % 2 else 3)}", i))
                    for w, buf in ((w2m, hm[n % 2]), (w2t, ht[n // 2 % 2])):
                        for j in range(2):
                            last = pe.matmul(y_bank(n)[C * j:C * j + C, :], w[:, n * C:(n + 1) * C], buf[j],
                                             start=w is w2m, stop=w is w2t, skip_group_check=True)
                    last.then_inc(*T.done(f"y{n}"))

        def experts1_act(act, i, wide):
            A = a4
            for k, (kind, n) in enumerate(plan):
                yield f"slot{k + 1}"
                if kind == "wb":
                    act.wait_ge(*t4.at(f"wb{n}", i))
                    act.wait_ge(*before(d4, "yw", n, 2, i, E1))
                    act.activation(wbs[n % 2][:], bank(0), ACT.Copy).then_inc(*A.done(f"wb{n}"))
                elif kind == "ab":
                    act.wait_ge(*t4.at(f"ab{n}", i))
                    act.wait_ge(*before(d4, "u", n, RING, i, NU))
                    act.activation(sa[n % RING], ab_bank(n, wide, 0), ACT.Silu,
                                   scale=1.0 / WS).then_inc(*A.done(f"silu{n}"))

        def experts1_dve(dve, i, wide):
            D = d4
            for k, (kind, n) in enumerate(plan):
                yield f"slot{k + 1}"
                if kind == "ab":
                    dve.wait_ge(*a4.at(f"silu{n}", i))
                    dve.tensor_tensor(units[n][1], sa[n % RING], ab_bank(n, wide, 1),
                                      ALU.mult).then_inc(*D.done(f"u{n}"))
                elif kind == "y":
                    dve.wait_ge(*t4.at(f"y{n}", i))
                    dve.wait_ge(*a4.at(f"wb{n}", i))
                    dve.wait_ge(*before(p4, "acc", n, 2, i, E1))
                    dve.tensor_tensor(yw[n % 2][:], y_bank(n), wbs[n % 2][:], ALU.mult).then_inc(*D.done(f"yw{n}"))

        def experts1_pool(pool, i, wide):
            for k, (kind, n) in enumerate(plan):
                yield f"slot{k + 1}"
                if kind == "y":
                    sum_expert(pool, p4, d4, E1, n, i)

        def layers_dve(dve):
            d1a.prime(dve)
            d1r.prime(dve)
            d2.prime(dve)
            dm.prime(dve)
            da.prime(dve)
            Part(ATTENTION0, attention0_dve(dve, 0)).all()
            pipelined(dve, ORDER0, attention0_dve, routing0_dve, ATTENTION0, ROUTING0)
            side_by_side(ORDER_RE, Part(ROUTING0, routing0_dve(dve, IT - 1)),
                         Part(SLOTS, experts0_dve(dve, 0, Banks(0, 1))))
            with dve.Fori(1, IT - 1) as i:
                Part(SLOTS, experts0_dve(dve, i, Banks(0, 2))).all()
            side_by_side(ORDER_ME, Part(MIXING, mixing_dve(dve, 0)),
                         Part(SLOTS, experts0_dve(dve, IT - 1, Banks(4, 1))))
            pipelined(dve, ORDER1, mixing_dve, attention_dve, MIXING, ATTENTION)
            d4.prime(dve)
            side_by_side(ORDER_AE, Part(ATTENTION, attention_dve(dve, IT - 1)),
                         Part(SLOTS1, experts1_dve(dve, 0, WIDE)))
            with dve.Fori(1, IT) as i:
                Part(SLOTS1, experts1_dve(dve, i, 0)).all()

        def layers_act(act):
            a1a.prime(act)
            a1r.prime(act)
            a2.prime(act)
            am.prime(act)
            aa.prime(act)
            Part(ATTENTION0, attention0_act(act, 0)).all()
            pipelined(act, ORDER0, attention0_act, routing0_act, ATTENTION0, ROUTING0)
            act.wait_ge(*ds.at("b2s"))
            side_by_side(ORDER_RE, Part(ROUTING0, routing0_act(act, IT - 1)),
                         Part(SLOTS, experts0_act(act, 0, Banks(0, 1))))
            with act.Fori(1, IT - 1) as i:
                Part(SLOTS, experts0_act(act, i, Banks(0, 2))).all()
            side_by_side(ORDER_ME, Part(MIXING, mixing_act(act, 0)),
                         Part(SLOTS, experts0_act(act, IT - 1, Banks(4, 1))))
            pipelined(act, ORDER1, mixing_act, attention_act, MIXING, ATTENTION)
            a4.prime(act)
            side_by_side(ORDER_AE, Part(ATTENTION, attention_act(act, IT - 1)),
                         Part(SLOTS1, experts1_act(act, 0, WIDE)))
            with act.Fori(1, IT) as i:
                act.activation(silu_table[:], k32["tri"][:, 0:1], ACT.Silu)
                Part(SLOTS1, experts1_act(act, i, 0)).all()

        def layers_pool(pool):
            p2.prime(pool)
            qm.prime(pool)
            qa.prime(pool)
            with pool.Fori(0, IT - 2) as i:
                tokens_pool(pool, i + 1)
            side_by_side(ORDER_RE, Part(ROUTING0, routing0_pool(pool, IT - 1)),
                         Part(SLOTS, experts0_pool(pool, 0, Banks(0, 1))))
            with pool.Fori(1, IT - 1) as i:
                Part(SLOTS, experts0_pool(pool, i, Banks(0, 2))).all()
            side_by_side(ORDER_ME, Part(MIXING, mixing_pool(pool, 0)),
                         Part(SLOTS, experts0_pool(pool, IT - 1, Banks(4, 1))))
            pipelined(pool, ORDER1, mixing_pool, attention_pool, MIXING, ATTENTION)
            p4.prime(pool)
            side_by_side(ORDER_AE, Part(ATTENTION, attention_pool(pool, IT - 1)),
                         Part(SLOTS1, experts1_pool(pool, 0, WIDE)))
            with pool.Fori(1, IT) as i:
                Part(SLOTS1, experts1_pool(pool, i, 0)).all()

        def layers_pe(pe):
            t1a.prime(pe)
            t1r.prime(pe)
            t2.prime(pe)
            tm.prime(pe)
            ta.prime(pe)
            Part(ATTENTION0, attention0_pe(pe, 0)).all()
            pipelined(pe, ORDER0, attention0_pe, routing0_pe, ATTENTION0, ROUTING0)
            pe.wait_ge(ld["w2"], 16)
            pe.wait_ge(*d1a.at("h1", IT - 1))
            side_by_side(ORDER_RE, Part(ROUTING0, routing0_pe(pe, IT - 1)),
                         Part(SLOTS, experts0_pe(pe, 0, Banks(0, 1))))
            pe.wait_ge(*a2.at(f"wb{E0 - 1}", 0))
            pe.wait_ge(*d2.at(f"yw{E0 - 1}", 0))
            pe.wait_ge(*a1r.at("wt", IT - 1))
            with pe.Fori(1, IT - 1) as i:
                Part(SLOTS, experts0_pe(pe, i, Banks(0, 2))).all()
            pe.wait_ge(*a2.at(f"wb{E0 - 1}", IT - 2))
            pe.wait_ge(*d2.at(f"yw{E0 - 1}", IT - 2))
            pe.wait_ge(*p3.at("z5"))
            pe.wait_ge(*ds.at("kvl"))
            pe.wait_ge(*ds.at("rl"))
            pe.wait_ge(*ds.at("mask_b"))
            side_by_side(ORDER_ME, Part(MIXING, mixing_pe(pe, 0)),
                         Part(SLOTS, experts0_pe(pe, IT - 1, Banks(4, 1))))
            pipelined(pe, ORDER1, mixing_pe, attention_pe, MIXING, ATTENTION)
            t4.prime(pe)
            pe.wait_ge(*dm.at("ho1", IT - 1))
            pe.wait_ge(*qa.at("xt1", 0))
            pe.wait_ge(*aa.at("wt", 0))
            pe.wait_ge(*ds.at("a3l"))
            pe.wait_ge(ld["w2m"], 16)
            pe.wait_ge(ld["w2t"], 16)
            side_by_side(ORDER_AE, Part(ATTENTION, attention_pe(pe, IT - 1)),
                         Part(SLOTS1, experts1_pe(pe, 0, WIDE)))
            pe.wait_ge(*qa.at("xt1", IT - 1))
            pe.wait_ge(*aa.at("wt", IT - 1))
            with pe.Fori(1, IT) as i:
                Part(SLOTS1, experts1_pe(pe, i, 0)).all()

        GROUPS = IT * UN
        ob = [hidden[:, k * UB * C:(k + 1) * UB * C] for k in range(GROUPS)]
        te = Steps(sem("pe_end"), [f"aT{g}" for g in range(GROUPS)])
        de = Steps(sem("dve_end"), [f"{s}{g}" for g in range(GROUPS) for s in ("o", "out")])
        out_v = out.rearrange("b t c -> t b c")

        def end_pe(pe):
            pe.wait_ge(*p4.at(f"acc{E1 - 1}", IT - 1))
            for g in range(GROUPS):
                for q in range(2):
                    last = pe.transpose(bank(g)[:, q * P:(q + 1) * P], acc[:, (2 * g + q) * P:(2 * g + q + 1) * P],
                                        k32["ident"])
                last.then_inc(*te.done(f"aT{g}"))

        def end_dve(dve):
            for g in range(GROUPS):
                cols = slice(g * UB * C, (g + 1) * UB * C)
                dve.wait_ge(*te.at(f"aT{g}"))
                dve.scalar_tensor_tensor(ob[g], bank(g)[:, 0:256], 1.0 / WS, x[:, cols], ALU.mult,
                                         ALU.add).then_inc(*de.done(f"o{g}"))
                dve.wait_ge(*de.at(f"o{g}"))
                dve.tensor_tensor(ob[g], ob[g], h[:, cols], ALU.add).then_inc(*de.done(f"out{g}"))

        def end_sync(sp):
            for g in range(GROUPS):
                sp.wait_ge(*de.at(f"out{g}"))
                sp.dma_start(out_v[:, g * UB:(g + 1) * UB, :], grp(ob[g])).then_inc(out_done, 16)
            sp.wait_ge(out_done, 16 * GROUPS)

        block = ctx.enter_context(nc.Block())

        @block.sync
        def _(sp):
            sp.dma_start(cs[:], c32).then_inc(ld["c32"], 16)
            for n, dst, src in (("w1", w1s, w1_0), ("c16", ch, c16), ("w2", w2s, w2_0), ("a1", a1s, w1_1),
                                ("a3", a3s, w3_1), ("w2m", w2m, w2m_1), ("w2t", w2t, w2t_1)):
                sp.dma_start(dst[:], src).then_inc(ld[n], 16)
            for g in range(B // UB):
                sp.wait_ge(rows_in[g], 16 * UB)
                sp.sem_inc(group_in, 1)
            end_sync(sp)

        @block.gpsimd
        def _(pool):
            pool3_zeros(pool)
            p1.prime(pool)
            pool.wait_ge(*ds.at("idx1"))
            AHEAD = 3
            edges_pool(pool, 0, GB + AHEAD)
            pool.wait_ge(*ds.at("spt"))
            for t in range(IT):
                index_pool(pool, t)
                rows_pool(pool, t)
                edges_pool(pool, min((t + 1) * GB + AHEAD, B), min((t + 2) * GB + AHEAD, B))
                if t == IT - 2:
                    tokens_pool(pool, 0)
            layers_pool(pool)

        @block.scalar
        def _(act):
            act.dma_start(tok[:], tokens).then_inc(ld["tok"], 16)
            setup_act(act)
            layers_act(act)

        @block.vector
        def _(dve):
            setup_dve(dve)
            layers_dve(dve)
            end_dve(dve)

        @block.tensor
        def _(pe):
            setup_pe(pe)
            pe.wait_ge(ld["c16"], 16)
            layers_pe(pe)
            end_pe(pe)


def packed(ins):
    f = np.float32
    t = np.arange(P)
    v = {"ident": np.eye(P, dtype=f), "tri": (t[:, None] <= t[None, :]).astype(f),
         "mask_ts": np.where(t[None, :] <= t[:, None], 0.0, NEG).astype(f),
         "mask_st": np.where(t[:, None] <= t[None, :], 0.0, NEG).astype(f)}
    inv = 1.0 / 10000.0 ** (np.arange(0, HD, 2, dtype=f) / HD)
    ang = np.outer(t.astype(f), inv).astype(f)
    cos, sin = np.cos(ang), np.sin(ang)
    scale = np.array([HD ** -0.5] * NH + [1.0] * NKV, f) / f(WS)
    v["cos"] = (scale[None, :, None] * np.concatenate([cos, cos], 1)[:, None, :]).reshape(P, 96)
    v["sin"] = (scale[None, :, None] * np.concatenate([-sin, sin], 1)[:, None, :]).reshape(P, 96)
    v["base"] = np.broadcast_to(np.minimum(np.arange(B), TAB_B - 1) * NODES * NODES, (P, B))
    v["pri0"] = np.broadcast_to(E0 - np.arange(E0), (P, E0))
    v["pri1"] = np.broadcast_to(E1 - np.arange(E1), (P, E1))

    def twice(a):
        return np.concatenate([a, a], 0)

    def rows_(a):
        return np.broadcast_to(a[None, :], (P, a.shape[0]))

    def diag(a):
        d = np.zeros((P, P), f)
        d[:C, :C] = a
        d[C:, C:] = a
        return d

    g = ins
    v["wq0"], v["wk0"] = twice(g["L0_attn_Wq"]), twice(g["L0_attn_Wk"])
    v["gate_w"], v["gate_b"] = twice(g["L0_ffn_gate_w"]), rows_(g["L0_ffn_gate_b"])
    v["b1"], v["b2"] = g["L0_ffn_b1"].T, twice(g["L0_ffn_b2"].T)
    v["gamma"], v["beta"] = rows_(g["L0_ffn_gamma"]), rows_(g["L0_ffn_beta"])
    v["mix"] = twice(np.stack([g[f"L1_attn_time_mix_{m}"].reshape(C) for m in "kvr"], 1))
    v["wkvr"] = twice(np.concatenate([g[f"L1_attn_W{m}"] for m in "kvr"], 1))
    v["wo0"] = diag(g["L1_attn_Wo"])
    tw = g["L1_attn_time_w"]
    v["toep"] = tw[np.clip(tw.shape[0] - 1 - (t[None, :] - t[:, None]), 0, tw.shape[0] - 1)]
    v["ln1"], v["ln2"] = twice(g["L1_ffn_ln1_w"][:, None]), twice(g["L1_ffn_ln2_w"][:, None])
    v["wqkv"] = twice(np.concatenate([g["L1_ffn_wq"], g["L1_ffn_wk"], g["L1_ffn_wv"]], 0).T)
    v["wo1"] = diag(g["L1_ffn_wo"].T)
    v["router"] = twice(g["L1_ffn_router_w"].T)
    big = np.zeros((P, N32), f)
    for n, s in AT32.items():
        big[:, s] = v[n]
    return big


def selectors():
    out = np.zeros((P, N16), np.float16)
    out[:, AT16["ident16"]] = np.eye(P)
    for name, ne in (("sel0", E0), ("sel1", E1)):
        s = np.zeros((P, ne, P), np.float16)
        for j in range(2):
            for e in range(ne):
                r = (j * ne + e) * PARTS
                s[r:r + PARTS, e, j * C:(j + 1) * C] = 1
        out[:, AT16[name]] = s.reshape(P, -1)
    s = np.zeros((P, UB * NH, P), np.float16)
    for k in range(UB * NH):
        s[k * PARTS:(k + 1) * PARTS, k, :] = 1
    out[:, AT16["selm"]] = s.reshape(P, -1)
    return out


def laid_out(ins):
    def twice(a):
        return np.concatenate([a, a], 0)

    a = {"tokens": ins["x"], "t2e": ins["L0_tok_token_to_edge"],
         "rows": np.concatenate([ins["L0_tok_edge_emb"].reshape(ROWS, C), ins["L0_tok_special_emb"]], 0),
         "c32": packed(ins), "c16": selectors(),
         "w1_0": twice(ins["L0_ffn_w1"].transpose(1, 0, 2).reshape(C, E0 * F0)),
         "w2_0": ins["L0_ffn_w2"].transpose(1, 0, 2).reshape(F0, E0 * C)}
    for n, w in (("w1_1", ins["L1_ffn_w1"]), ("w3_1", ins["L1_ffn_w3"])):
        wt = w.transpose(2, 0, 1)
        tail = np.zeros((C, E1, FT), np.float32)
        tail[:, :, :F1 - FM] = wt[:, :, FM:]
        a[n] = twice(np.concatenate([wt[:, :, :FM].reshape(C, -1), tail.reshape(C, -1)], 1))
    wt = ins["L1_ffn_w2"].transpose(2, 0, 1)
    tail = np.zeros((2, FT, E1, C), np.float32)
    for e in range(E1):
        tail[e % 2, :F1 - FM, e] = wt[FM:, e]
    a["w2m_1"], a["w2t_1"] = wt[:FM].reshape(FM, -1), tail.reshape(P, -1)
    return {n: np.ascontiguousarray(v) for n, v in a.items()}


def kernel(**inputs):
    import concourse.bacc as _bacc
    from concourse.bass_utils import run_bass_kernel_spmd as _run

    nc = _bacc.Bacc("TRN2", target_bir_lowering=False, num_devices=1)
    arrays, args = {}, []
    for name, a in laid_out({n: np.asarray(v) for n, v in inputs.items()}).items():
        arrays[f"in_{name}"] = a
        args.append(nc.dram_tensor(f"in_{name}", a.shape, mybir.dt.from_np(a.dtype), kind="ExternalInput").ap())
    args.append(nc.dram_tensor("tower_out", (B, L, C), F32, kind="ExternalOutput").ap())
    lm_tower(nc, *args)
    r = _run(nc, [arrays], core_ids=[0])
    return r.results[0]["tower_out"]
```
